# Optimizing a Trainium2 kernel written in Bass

```python
import numpy as np
import jax
import jax.numpy as jnp

def _softmax(x, axis=-1):
    return jax.nn.softmax(x, axis=axis)

def _gelu(x):
    return jax.nn.gelu(x, approximate=True)

def _silu(x):
    return jax.nn.silu(x)

def _sigmoid(x):
    return jax.nn.sigmoid(x)

def _layernorm(x, axis=-1, eps=1e-05):
    m = jnp.mean(x, axis=axis, keepdims=True)
    v = jnp.var(x, axis=axis, keepdims=True)
    return (x - m) / jnp.sqrt(v + eps)

def _scatter_add(tgt, idx, src, axis=0):
    return tgt.at[idx].add(src)

def _segment_sum(src, seg, n):
    return jax.ops.segment_sum(src, seg, n)
kernel_name = 'mk_gnn_preln_d2_gnn_r8_c8ffa0'

def setup_inputs(seed: int=0):
    np.random.seed(seed)
    _w = jnp.asarray

    def _rec_inputs():
        import jax
        import jax.numpy as jnp
        _gk = jax.random.key(seed)
        x = -0.0003713 + 1 * jax.random.normal(jax.random.fold_in(_gk, 1), (12500, 256), jnp.float32)
        src = jax.random.randint(jax.random.fold_in(_gk, 2), (200000,), 0, 12500, jnp.int32)
        dst = jnp.minimum((12500 * jax.random.uniform(jax.random.fold_in(_gk, 3), (200000,)) ** 2.0).astype(jnp.int32), 99999)
        _o = jnp.argsort(dst, stable=True)
        src = src[_o]
        dst = dst[_o]
        edge_attr_64 = jax.random.uniform(jax.random.fold_in(_gk, 12), (200000, 64), jnp.float32, 0.0, 1)
        return (x, src, dst, edge_attr_64)
    x, src, dst, edge_attr_64 = _rec_inputs()

    def _L0_gnn_setup():
        import jax, jax.numpy as jnp
        import numpy as np
        NEG_SLOPE = 0.2
        N_NODES = 6250
        N_EDGES = 100000

        def gat_conv(h, src, dst, W, al, ar, residual):
            N = h.shape[0]
            H, D = al.shape
            feat = (h @ W).reshape(N, H, D)
            el = jnp.sum(feat * al, axis=-1)
            er = jnp.sum(feat * ar, axis=-1)
            e = jax.nn.leaky_relu(el[src] + er[dst], NEG_SLOPE)
            emax = jax.ops.segment_max(e, dst, num_segments=N)
            ex = jnp.exp(e - emax[dst])
            denom = jax.ops.segment_sum(ex, dst, num_segments=N)
            a = ex / denom[dst]
            msg = feat[src] * a[:, :, None]
            rst = jax.ops.segment_sum(msg, dst, num_segments=N)
            if residual:
                rst = rst + h.reshape(N, H, D)
            return jax.nn.elu(rst).reshape(N, H * D)
        key = jax.random.key(seed)
        ks = jax.random.split(key, 9)
        features = jax.random.normal(ks[0], (N_NODES, 256), dtype=jnp.float32)
        src = jax.random.randint(ks[1], (N_EDGES,), 0, N_NODES, dtype=jnp.int32)
        dst = jax.random.randint(ks[2], (N_EDGES,), 0, N_NODES, dtype=jnp.int32)
        s1 = 1.0 / np.sqrt(256.0)
        W1 = jax.random.normal(ks[3], (256, 256), dtype=jnp.float32) * s1
        al1 = jax.random.normal(ks[4], (4, 64), dtype=jnp.float32) * 0.1
        ar1 = jax.random.normal(ks[5], (4, 64), dtype=jnp.float32) * 0.1
        W2 = jax.random.normal(ks[6], (256, 256), dtype=jnp.float32) * s1
        al2 = jax.random.normal(ks[7], (4, 64), dtype=jnp.float32) * 0.1
        ar2 = jax.random.normal(ks[8], (4, 64), dtype=jnp.float32) * 0.1
        return {'features': features, 'src': src, 'dst': dst, 'W1': W1, 'al1': al1, 'ar1': ar1, 'W2': W2, 'al2': al2, 'ar2': ar2}
    _L0_gnn_all = _L0_gnn_setup()
    _L0_gnn_in = {k: v for k, v in _L0_gnn_all.items() if k in ('W1', 'al1', 'ar1', 'W2', 'al2', 'ar2')}
    del _L0_gnn_all

    def _L1_gnn_setup():
        import jax, jax.numpy as jnp
        import numpy as np
        N, E, HID, NRBF = (1250, 40000, 256, 64)
        key = jax.random.key(seed)
        ks = jax.random.split(key, 12)

        def lin(k, fin, fout):
            bound = 1.0 / np.sqrt(fin)
            kw, kb = jax.random.split(k)
            W = jax.random.uniform(kw, (fin, fout), jnp.float32, -bound, bound)
            b = jax.random.uniform(kb, (fout,), jnp.float32, -bound, bound)
            return (W, b)
        W1, b1 = lin(ks[0], NRBF, HID)
        W2, b2 = lin(ks[1], HID, HID)
        U1, c1 = lin(ks[2], 2 * HID, HID)
        U2, c2 = lin(ks[3], HID, HID)
        h = jax.random.normal(ks[4], (N, HID), jnp.float32)
        edge_index = jax.random.randint(ks[5], (2, E), 0, N, jnp.int64)
        rbf = jax.random.uniform(ks[6], (E, NRBF), jnp.float32)
        return {'h': h, 'edge_index': edge_index, 'rbf': rbf, 'W1': W1, 'b1': b1, 'W2': W2, 'b2': b2, 'U1': U1, 'c1': c1, 'U2': U2, 'c2': c2}
    _L1_gnn_all = _L1_gnn_setup()
    _L1_gnn_in = {k: v for k, v in _L1_gnn_all.items() if k in ('W1', 'b1', 'W2', 'b2', 'U1', 'c1', 'U2', 'c2')}
    del _L1_gnn_all
    return {'x': x, 'src': src, 'dst': dst, 'edge_attr_64': edge_attr_64, 'L0_gnn_W1': _L0_gnn_in['W1'], 'L0_gnn_al1': _L0_gnn_in['al1'], 'L0_gnn_ar1': _L0_gnn_in['ar1'], 'L0_gnn_W2': _L0_gnn_in['W2'], 'L0_gnn_al2': _L0_gnn_in['al2'], 'L0_gnn_ar2': _L0_gnn_in['ar2'], 'L1_gnn_W1': _L1_gnn_in['W1'], 'L1_gnn_b1': _L1_gnn_in['b1'], 'L1_gnn_W2': _L1_gnn_in['W2'], 'L1_gnn_b2': _L1_gnn_in['b2'], 'L1_gnn_U1': _L1_gnn_in['U1'], 'L1_gnn_c1': _L1_gnn_in['c1'], 'L1_gnn_U2': _L1_gnn_in['U2'], 'L1_gnn_c2': _L1_gnn_in['c2']}

def reference(x, src, dst, edge_attr_64, L0_gnn_W1, L0_gnn_al1, L0_gnn_ar1, L0_gnn_W2, L0_gnn_al2, L0_gnn_ar2, L1_gnn_W1, L1_gnn_b1, L1_gnn_W2, L1_gnn_b2, L1_gnn_U1, L1_gnn_c1, L1_gnn_U2, L1_gnn_c2):
    import jax
    import jax.numpy as jnp

    def _L0_gnn_ref(features, src, dst, W1, al1, ar1, W2, al2, ar2):
        import jax, jax.numpy as jnp
        import numpy as np
        NEG_SLOPE = 0.2
        N_NODES = 6250
        N_EDGES = 100000

        def gat_conv(h, src, dst, W, al, ar, residual):
            N = h.shape[0]
            H, D = al.shape
            feat = (h @ W).reshape(N, H, D)
            el = jnp.sum(feat * al, axis=-1)
            er = jnp.sum(feat * ar, axis=-1)
            e = jax.nn.leaky_relu(el[src] + er[dst], NEG_SLOPE)
            emax = jax.ops.segment_max(e, dst, num_segments=N)
            ex = jnp.exp(e - emax[dst])
            denom = jax.ops.segment_sum(ex, dst, num_segments=N)
            a = ex / denom[dst]
            msg = feat[src] * a[:, :, None]
            rst = jax.ops.segment_sum(msg, dst, num_segments=N)
            if residual:
                rst = rst + h.reshape(N, H, D)
            return jax.nn.elu(rst).reshape(N, H * D)
        h = gat_conv(features, src, dst, W1, al1, ar1, residual=False)
        h = gat_conv(h, src, dst, W2, al2, ar2, residual=True)
        return h

    def _L1_gnn_ref(h, edge_index, rbf, W1, b1, W2, b2, U1, c1, U2, c2):
        import jax, jax.numpy as jnp
        import numpy as np
        N, E, HID, NRBF = (1250, 40000, 256, 64)
        src, dst = (edge_index[0], edge_index[1])
        gate = jax.nn.sigmoid(jax.nn.silu(rbf @ W1 + b1) @ W2 + b2)
        msg = gate * h[src]
        aggr = jax.ops.segment_sum(msg, dst, num_segments=h.shape[0])
        upd = jax.nn.silu(jnp.concatenate([h, aggr], axis=-1) @ U1 + c1) @ U2 + c2
        return h + upd
    edge_index = jnp.stack([src, dst])
    h = jnp.maximum(_layernorm(x, axis=-1), 0.0)
    x = x + _L0_gnn_ref(h, src, dst, L0_gnn_W1, L0_gnn_al1, L0_gnn_ar1, L0_gnn_W2, L0_gnn_al2, L0_gnn_ar2)
    h = jnp.maximum(_layernorm(x, axis=-1), 0.0)
    x = x + _L1_gnn_ref(h, edge_index, edge_attr_64, L1_gnn_W1, L1_gnn_b1, L1_gnn_W2, L1_gnn_b2, L1_gnn_U1, L1_gnn_c1, L1_gnn_U2, L1_gnn_c2)
    return x

_drawn_inputs = setup_inputs


def setup_inputs(seed=0):
    import zlib

    import numpy as np

    out = dict(_drawn_inputs(seed))
    spreads = {}
    factors = {'edge_attr_64': 8.0,
     'L0_gnn_ar1': 29.263,
     'L0_gnn_al2': 21.366,
     'L0_gnn_ar2': 169.42,
     'L1_gnn_b1': 7.389,
     'L1_gnn_b2': 5.446,
     'L1_gnn_c1': 8.0,
     'L1_gnn_c2': 3.128}
    for name, (base, spread) in spreads.items():
        noise = np.random.default_rng([zlib.crc32(name.encode()), seed]).standard_normal(out[name].shape)
        drawn = base * np.exp(spread * noise) if base else spread * noise
        out[name] = jnp.asarray(drawn.astype(out[name].dtype))
    for name, factor in factors.items():
        out[name] = (out[name] * factor).astype(out[name].dtype)
    return out
```

```python
from contextlib import ExitStack

import concourse.bass as bass
from concourse import mybir

P = 128
F = 256
H = 4
D = F // H
HW = D + 1
ROW = H * HW
NR = 64
U = 16
R = H * U
G4 = 4
BIG = 1.0e30
SLOPE = 0.2
EPS = 1.0e-5
BANKS = 4

F32 = mybir.dt.float32
I32 = mybir.dt.int32
BF16 = mybir.dt.bfloat16
ALU = mybir.AluOpType
ACT = mybir.ActivationFunctionType
AX = mybir.AxisListType


class Linked:

    def __init__(self, eng, sem):
        self.eng, self.sem, self.n = eng, sem, 0

    def run(self, ins):
        self.n += 1
        ins.then_inc(self.sem, 1)
        self.eng.wait_ge(self.sem, self.n)


class LoopLinked:

    def __init__(self, eng, sem, turn, per):
        self.eng, self.sem, self.turn, self.per, self.n = eng, sem, turn, per, 0

    def run(self, ins):
        self.n += 1
        assert self.n <= self.per
        ins.then_inc(self.sem, 1)
        self.eng.wait_ge(self.sem, self.turn * self.per + self.n)


class Sizes:
    def __init__(self, n, e):
        self.N, self.E = n, e
        self.NT = -(-n // P)
        self.EB = -(-e // P)
        self.LAST = n - (self.NT - 1) * P
        assert self.LAST < P and self.NT % (2 * G4) == 2
        most = self.EB + self.NT - 1
        self.NI = 2 * -(-most // (2 * U))
        self.NC = -(-(self.NI + 2) * U // P)
        self.V = self.NC * P


outer = [None]


def allocators(nc, ctx, phase):
    def sb(name, shape, dt=F32):
        return ctx.enter_context(nc.sbuf_tensor(f"{phase}_{name}", shape, dt))

    def ps(name, shape):
        return ctx.enter_context(nc.psum_tensor(f"{phase}_{name}", shape, F32))

    def sem(name):
        made.append(ctx.enter_context(nc.semaphore(f"{phase}_{name}")))
        return made[-1]

    def lasting(name):
        return outer[0].enter_context(nc.semaphore(f"{phase}_{name}"))

    made = []
    sem.made, sem.lasting = made, lasting
    return sb, ps, sem


def phase_block(nc, ctx, sem):
    def clear():
        with nc.Block() as after:
            @after.gpsimd
            def _(pool):
                for s in sem.made:
                    pool.sem_clear(s)

    ctx.callback(clear)
    return ctx.enter_context(nc.Block())


def constants(nc, K):
    with ExitStack() as ctx:
        sb, ps, sem = allocators(nc, ctx, "constants")
        col_i, row_i, head_i, fill = (sb(n, s, I32) for n, s in
                                ((("col_i", [P, P])), ("row_i", [P, 1]), ("head_i", [H, R]), ("fill", [R, 2])))
        iotas, linked = sem("iotas"), sem("dve_linked")
        block = phase_block(nc, ctx, sem)

        @block.gpsimd
        def _(pool):
            pool.iota(col_i[:, :], [[1, P]], base=0, channel_multiplier=0).then_inc(iotas, 1)
            pool.iota(row_i[:, :], [[0, 1]], base=0, channel_multiplier=1).then_inc(iotas, 1)
            pool.iota(head_i[:, :], [[1, H], [0, U]], base=0, channel_multiplier=0).then_inc(iotas, 1)

        @block.vector
        def _(dve):
            link = Linked(dve, linked)
            dve.wait_ge(iotas, 3)
            link.run(dve.tensor_copy(K.col[:, :], col_i[:, :]))
            link.run(dve.tensor_copy(K.row[:, :], row_i[:, :]))
            link.run(dve.tensor_scalar(K.ident[:, :], K.col[:, :], K.row[:, 0:1], None, ALU.is_equal))
            link.run(dve.tensor_scalar(fill[:, 0:1], row_i[0:R, :], U.bit_length() - 1, None,
                                       ALU.logical_shift_right))
            link.run(dve.tensor_scalar(fill[:, 1:2], row_i[0:R, :], U - 1, None, ALU.bitwise_and))
            link.run(dve.tensor_copy(K.hu[:, :], fill[:, :]))
            link.run(dve.tensor_scalar(K.head_of[:, :], K.col[0:R, 0:H], K.hu[:, 0:1], None, ALU.is_equal))
            link.run(dve.tensor_scalar(K.visit_of[:, :], K.col[0:R, 0:U], K.hu[:, 1:2], None, ALU.is_equal))
            link.run(dve.tensor_copy(K.rows_of[:, :], head_i[:, :]))
            link.run(dve.tensor_scalar(K.rows_of[:, :], K.rows_of[:, :], K.row[0:H, 0:1], None, ALU.is_equal))
            link.run(dve.memset(K.ones[:, :], 1.0))
            link.run(dve.memset(K.ones3[:, :], 1.0))
            link.run(dve.tensor_copy(K.col3[:, :], K.ident[0:3, 0:3]))
            link.run(dve.memset(K.eps[:, :], EPS))


def visit_tables(nc, S, K, M, src, dst):
    EB, V, NC, NT, E = S.EB, S.V, S.NC, S.NT, S.E
    W = EB + 1
    tail = EB * P - E
    CH = 512
    with ExitStack() as ctx:
        sb, ps, sem = allocators(nc, ctx, "visits")
        pad = sb("pad", [1, 2, P], I32)
        ends = sb("ends", [1, 2, EB], I32)
        tiles = sb("tiles", [1, 2, EB])
        until = sb("until", [1, W])
        skip = sb("skip", [1, W])
        one = sb("one", [1, W])
        until_b = sb("until_b", [P, W])
        skip_b = sb("skip_b", [P, W])
        ones_b = sb("ones_b", [P, W])
        junk = sb("junk", [P, W])
        number = sb("number", [P, NC])
        count = sb("count", [P, NC])
        tile_v = sb("tile_v", [P, NC])
        tile_c = sb("tile_c", [P, NC])
        tile_m = sb("tile_m", [P, NC])
        tile_i = sb("tile_i", [P, NC], I32)
        block_f = sb("block_f", [P, NC])
        block_i = sb("block_i", [P, NC], I32)
        rows_d = sb("rows_d", [P, NC, P], I32)
        rows_s = sb("rows_s", [P, NC, P], I32)
        dst_f = sb("dst_f", [P, NC, P])
        src_f = sb("src_f", [P, NC, P])
        prev_f = sb("prev_f", [P, NC, P])
        local = sb("local", [P, NC, P])
        local_h = sb("local_h", [P, NC, P], BF16)
        same = sb("same", [P, NC, P])
        same0 = sb("same0", [P, NC])
        whole = sb("whole", [P, NC])
        alike = sb("alike", [P, NC])
        local_t = sb("local_t", [P, V])
        src_t = sb("src_t", [P, V], I32)
        bcast = ps("bcast", [P, 2, CH])
        turned = ps("turned", [P, 2, 512])
        got = sem.lasting("rows_got")
        (pads, padded, loaded, linked, rows_up, broad, lists, local_up, turned_up, kept, prevs,
         stored, cols, edges_in) = (sem(n) for n in (
             "pads", "padded", "ends_loaded", "dve_linked", "rows_up", "broad", "lists", "local_up",
             "turned_up", "turned_kept", "prevs", "stored", "tables_up", "broad_up"))
        chunks = [(a, min(CH, W - a)) for a in range(0, W, CH)]
        turns = [(which, c, min(4, NC - c)) for which in range(2) for c in range(0, NC, 4)]
        block = phase_block(nc, ctx, sem)

        @block.sync
        def _(sp):
            sp.dma_start(M.dst_e[0:E].rearrange("(a b) -> a b", a=16), dst.rearrange("(a b) -> a b", a=16)).then_inc(padded, 16)
            sp.dma_start(M.src_e[0:E].rearrange("(a b) -> a b", a=16), src.rearrange("(a b) -> a b", a=16)).then_inc(padded, 16)
            sp.wait_ge(pads, 2)
            sp.dma_start(M.dst_e[E:E + tail].rearrange("(a b) -> a b", a=1), pad[:, 0, 0:tail]).then_inc(padded, 16)
            sp.dma_start(M.src_e[E:E + tail].rearrange("(a b) -> a b", a=1), pad[:, 1, 0:tail]).then_inc(padded, 16)
            sp.wait_ge(padded, 64)
            blocks = M.dst_e.rearrange("(o b e) -> o b e", e=P, o=1)
            sp.dma_start(ends[:, 0, :].unsqueeze(2), blocks[:, :, 0:1], allow_slow_non_contiguous=True).then_inc(loaded, 16)
            sp.dma_start(ends[:, 1, :].unsqueeze(2), blocks[:, :, P - 1:P], allow_slow_non_contiguous=True).then_inc(loaded, 16)
            sp.wait_ge(local_up, 1)
            sp.dma_start(M.dst_v[1:1 + V * P].rearrange("(c p e) -> p c e", p=P, e=P), dst_f[:, :, :]).then_inc(stored, 16)
            sp.wait_ge(lists, 1)
            sp.dma_start(M.dst_v[0:1].rearrange("(a b) -> a b", a=1), until[0:1, 0:1]).then_inc(stored, 16)
            sp.wait_ge(stored, 32)
            sp.dma_start(prev_f[:, :, :], M.dst_v[0:V * P].rearrange("(c p e) -> p c e", p=P, e=P)).then_inc(prevs, 16)
            by_visit = lambda t: t.rearrange("(c p o) -> p c o", p=P, o=1)
            sp.wait_ge(lists, 3)
            sp.dma_start(by_visit(M.tile), tile_i[:, :].unsqueeze(2), allow_slow_non_contiguous=True).then_inc(stored, 16)
            sp.dma_start(by_visit(M.block), block_i[:, :].unsqueeze(2), allow_slow_non_contiguous=True).then_inc(stored, 16)
            sp.wait_ge(local_up, 3)
            sp.dma_start(M.local_row.rearrange("(c p e) -> p c e", p=P, e=P), local_h[:, :, :]).then_inc(stored, 16)
            sp.wait_ge(kept, len(turns))
            sp.dma_start(M.local_col, local_t[:, :]).then_inc(stored, 16)
            sp.dma_start(M.src_col, src_t[:, :]).then_inc(stored, 16)
            sp.wait_ge(cols, 1)
            sp.dma_start(M.apart.rearrange("(c p e) -> p c e", p=P, e=P), same[:, :, :]).then_inc(stored, 16)
            sp.dma_start(by_visit(M.alike), alike[:, :].unsqueeze(2), allow_slow_non_contiguous=True).then_inc(stored, 16)
            sp.dma_start(by_visit(M.whole), whole[:, :].unsqueeze(2), allow_slow_non_contiguous=True).then_inc(stored, 16)
            sp.dma_start(by_visit(M.goes_on), same0[:, :].unsqueeze(2), allow_slow_non_contiguous=True).then_inc(stored, 16)
            sp.wait_ge(stored, 32 + 9 * 16)

        @block.tensor
        def _(pe):
            pe.wait_ge(rows_up, 1)
            for n, (a, w) in enumerate(chunks * 2):
                row = until if n < len(chunks) else skip
                if n >= 2:
                    pe.wait_ge(broad, n - 1)
                pe.matmul(bcast[:, n % 2, 0:w], K.ones[0:1, :], row[0:1, a:a + w], start=True, stop=True).then_inc(edges_in, 1)
            pe.wait_ge(local_up, 3)
            for n, (which, c, w) in enumerate(turns):
                if n >= 2:
                    pe.wait_ge(kept, n - 1)
                for k in range(w):
                    mm = pe.transpose(turned[:, n % 2, k * P:k * P + P], (src_f if which else local)[:, c + k, :], K.ident[:, :])
                mm.then_inc(turned_up, 1)

        @block.gpsimd
        def _(pool):
            pool.memset(pad[:, 0, :], NT * P - 1).then_inc(pads, 1)
            pool.memset(pad[:, 1, :], 0).then_inc(pads, 1)
            pool.iota(rows_d[:, 0, 0:NC], [[P, NC]], base=0, channel_multiplier=1).then_inc(pads, 1)
            pool.wait_ge(lists, 3)
            pool.wait_ge(padded, 64)
            for table, rows in ((M.dst_e, rows_d), (M.src_e, rows_s)):
                for c in range(NC):
                    pool.indirect_dma_start(rows[:, c, :], None, table.rearrange("(b e) -> b e", e=P),
                                            bass.IndirectOffsetOnAxis(block_i[:, c:c + 1], 0)).then_inc(got, 16)

        @block.scalar
        def _(act):
            for n, (which, c, w) in enumerate(turns):
                act.wait_ge(turned_up, n + 1)
                out = (src_t if which else local_t)[:, c * P:(c + w) * P]
                act.activation(out, turned[:, n % 2, 0:w * P], ACT.Copy).then_inc(kept, 1)

        @block.vector
        def _(dve):
            link = Linked(dve, linked)
            dve.wait_ge(pads, 3)
            link.run(dve.tensor_copy(number[:, :], rows_d[:, 0, 0:NC]))
            link.run(dve.memset(ones_b[:, :], 1.0))
            link.run(dve.memset(one[:, :], 1.0))
            dve.wait_ge(loaded, 32)
            link.run(dve.tensor_scalar(ends[:, :, :], ends[:, :, :], P.bit_length() - 1, None, ALU.logical_shift_right))
            link.run(dve.tensor_copy(tiles[:, :, :], ends[:, :, :]))
            link.run(dve.memset(until[:, :], -1.0))
            link.run(dve.memset(skip[:, :], 0.0))
            link.run(dve.scalar_tensor_tensor(junk[0:1, 0:EB], tiles[:, 1, :], 1.0, tiles[:, 0, :], ALU.add, ALU.subtract))
            link.run(dve.tensor_tensor_scan(until[:, 1:W], one[:, 1:W], junk[0:1, 0:EB], 0.0, ALU.mult, ALU.add))
            link.run(dve.tensor_copy(skip[:, 0:1], tiles[:, 0, 0:1]))
            if EB > 1:
                link.run(dve.scalar_tensor_tensor(skip[:, 1:EB], tiles[:, 0, 1:EB], -1.0, tiles[:, 1, 0:EB - 1],
                                                  ALU.add, ALU.subtract))
            dve.sem_inc(rows_up, 1)
            for n, (a, w) in enumerate(chunks * 2):
                dve.wait_ge(edges_in, n + 1)
                out = until_b if n < len(chunks) else skip_b
                dve.tensor_copy(out[:, a:a + w], bcast[:, n % 2, 0:w]).then_inc(broad, 1)
            dve.wait_ge(broad, 2 * len(chunks))
            dve.sem_inc(lists, 1)
            for c in range(NC):
                link.run(dve.scalar_tensor_tensor(junk[:, :], until_b[:, :], number[:, c:c + 1], ones_b[:, :],
                                                  ALU.is_le, ALU.mult, accum_out=count[:, c:c + 1]))
                link.run(dve.scalar_tensor_tensor(junk[:, :], until_b[:, :], number[:, c:c + 1], skip_b[:, :],
                                                  ALU.is_le, ALU.mult, accum_out=tile_v[:, c:c + 1]))
            link.run(dve.tensor_scalar(block_f[:, :], count[:, :], -1.0, EB - 1.0, ALU.add, ALU.min))
            dve.tensor_copy(block_i[:, :], block_f[:, :]).then_inc(lists, 1)
            link.run(dve.tensor_tensor(tile_v[:, :], tile_v[:, :], number[:, :], ALU.add))
            link.run(dve.tensor_scalar(tile_c[:, :], tile_v[:, :], NT - 1.0, None, ALU.min))
            link.run(dve.tensor_scalar(tile_m[:, :], tile_v[:, :], -float(P), None, ALU.mult))
            dve.tensor_copy(tile_i[:, :], tile_c[:, :]).then_inc(lists, 1)
            dve.wait_ge(got, 2 * NC * 16)
            dve.tensor_copy(dst_f[:, :, :], rows_d[:, :, :]).then_inc(local_up, 1)
            link.run(dve.tensor_copy(src_f[:, :, :], rows_s[:, :, :]))
            dve.wait_ge(local_up, 1)
            link.run(dve.tensor_tensor(local[:, :, :], dst_f[:, :, :], tile_m[:, :].unsqueeze(2).broadcast_to([P, NC, P]), ALU.add))
            dve.tensor_copy(local_h[:, :, :], local[:, :, :]).then_inc(local_up, 2)
            dve.wait_ge(prevs, 16)
            link.run(dve.tensor_tensor(same[:, :, :], dst_f[:, :, :], prev_f[:, :, :], ALU.is_equal))
            link.run(dve.tensor_copy(same0[:, :], same[:, :, 0]))
            link.run(dve.tensor_scalar(same[:, :, :], same[:, :, :], -1.0, BIG, ALU.add, ALU.mult))
            dve.tensor_reduce(alike[:, :], same[:, :, 1:P], AX.X, ALU.min)
            dve.tensor_reduce(whole[:, :], same[:, :, :], AX.X, ALU.min).then_inc(cols, 1)


def attention_weights(nc, K, M, W_dram, al, ar, Waug, layer):
    with ExitStack() as ctx:
        sb, ps, sem = allocators(nc, ctx, f"weights{layer}")
        w = sb("w", [P, 2, F])
        a = sb("a", [P, 2, F])
        prod = sb("prod", [P, 2, 2, F])
        loaded, linked = sem("w_loaded"), sem("dve_linked")
        block = phase_block(nc, ctx, sem)

        @block.sync
        def _(sp):
            sp.dma_start(w[:, :, :], W_dram.rearrange("(k p) f -> p k f", p=P)).then_inc(loaded, 16)
            for n, v in enumerate((al, ar)):
                row = v.rearrange("(o h) d -> o (h d)", o=1)
                sp.dma_start(a[:, n, :], row.broadcast_to([P, F])).then_inc(loaded, 16)

        @block.vector
        def _(dve):
            link = Linked(dve, linked)
            dve.wait_ge(loaded, 48)
            for k in range(2):
                row = Waug[:, k, 0:ROW].rearrange("p (h d) -> p h d", d=HW)
                dve.tensor_copy(row[:, :, 0:D], w[:, k, :].rearrange("p (h d) -> p h d", d=D))
                for n in range(2):
                    link.run(dve.tensor_tensor(prod[:, k, n, :], w[:, k, :], a[:, n, :], ALU.mult))
                    out = row[:, :, D] if n == 0 else Waug[:, k, ROW:ROW + H]
                    link.run(dve.tensor_reduce(out, prod[:, k, n, :].rearrange("p (h d) -> p h d", d=D), AX.X, ALU.add))


class Nodes:

    def __init__(self, S):
        self.S, self.turns = S, (S.NT - 2) // (2 * G4)

    def run(self, eng, group):
        with eng.Fori(0, self.turns) as j:
            for p in range(2):
                group(j * (2 * G4) + p * G4, j * 2 + p, p, G4, P)
        group(self.S.NT - 2, 2 * self.turns, 0, 2, self.S.LAST)


def hold(eng, sem, value, passed):
    eng.wait_ge(sem, value)
    eng.sem_inc(passed, 1)


def half(g, p):
    return g // 2 if isinstance(g, int) else (g - p) // 2


def tiles_of(table, tile, n):
    return table[bass.ds(tile * P, n * P), :].rearrange("(k p) f -> p k f", p=P)


def load_tiles(eng, buf, p, table, tile, n, rows, done):
    eng.dma_start(buf[:, p, 0:n - 1, :], tiles_of(table, tile, n - 1)).then_inc(done, 16)
    eng.dma_start(buf[0:rows, p, n - 1, :], table[bass.ds((tile + n - 1) * P, rows), :]).then_inc(done, 16)


def project_nodes(nc, S, K, M, first, x, Waug, er3, acc):
    NT = S.NT
    nodes = Nodes(S)
    with ExitStack() as ctx:
        sb, ps, sem = allocators(nc, ctx, "project1" if first else "project2")
        xin = sb("xin", [P, 2, G4, F]) if first else None
        stats = sb("stats", [P, 2, G4, nc.vector.BN_STATS_DIM])
        mv = sb("mv", [P, 2, G4, 2])
        den = sb("den", [P, 2, G4, H])
        dev = sb("dev", [P, 2, G4])
        scale = sb("scale", [P, 2, G4])
        shift = sb("shift", [P, 2, G4])
        low = sb("low", [P, 2, G4, F])
        h = sb("h", [P, 2, G4, F])
        hT = sb("hT", [P, 2, G4, F])
        row = sb("row", [P, 2, G4, ROW])
        er = sb("er", [P, NT, H])
        rest = sb("rest", [P, NT, H])
        psT = ps("psT", [P, 2, 512])
        psF = ps("psF", [P, G4, 512])
        (used, moments, devs, scales, h_up, low_up, exp_up, turned, hT_up, products, kept, out_free,
         linked, cleared) = (sem(n) for n in (
             "x_used", "moments", "devs", "scales", "h_up", "low_up", "exp_up", "turned", "hT_up",
             "products", "rows_kept", "out_free", "dve_linked", "cleared"))
        split, passed = sem("split"), sem("passed")
        loaded = [sem("loaded0"), sem("loaded1")]
        stored = [sem.lasting("stored0"), sem.lasting("stored1")]
        block = phase_block(nc, ctx, sem)

        @block.sync
        def _(sp):
            def group(tile, g, p, n, rows):
                sp.wait_ge(used, g + 1)
                if rows != P:
                    sp.wait_ge(cleared, 1)
                load_tiles(sp, xin, p, x, tile, n, rows, loaded[p])
            if first:
                nodes.run(sp, group)

        @block.gpsimd
        def _(pool):
            def group(tile, g, p, n, rows):
                pool.wait_ge(kept, tile + n + G4)
                pool.dma_start(tiles_of(M.table, tile, n), row[:, p, 0:n, :]).then_inc(stored[p], 16)
                if not first:
                    pool.dma_start(tiles_of(M.h2, tile, n), h[:, p, 0:n, :]).then_inc(stored[p], 16)
                each = 16 if first else 32
                pool.wait_ge(stored[p], half(g, p) * each + each)
                pool.sem_inc(out_free, 1)
            nodes.run(pool, group)

        @block.tensor
        def _(pe):
            def product(T, p, k):
                pe.wait_ge(hT_up, T + 3)
                pe.wait_ge(kept, T + 1)
                for c in range(2):
                    mm = pe.matmul(psF[:, k, 0:ROW + H], hT[:, p, k, c * P:c * P + P], Waug[:, c, :],
                                   start=(c == 0), stop=(c == 1))
                mm.then_inc(products, 1)

            def group(tile, g, p, n, rows):
                for k in range(n):
                    T = tile + k
                    pe.wait_ge(h_up, T + 1)
                    pe.wait_ge(hT_up, T + 1)
                    for c in range(2):
                        mm = pe.transpose(psT[:, k % 2, c * P:c * P + P], h[:, p, k, c * P:c * P + P], K.ident[:, :])
                    mm.then_inc(turned, 1)
                    if k:
                        product(T - 1, p, k - 1)
                product(tile + n - 1, p, n - 1)
            nodes.run(pe, group)

        @block.scalar
        def _(act):
            act.sem_inc(hT_up, 2)
            if first:
                act.sem_inc(used, 2)

            def group(tile, g, p, n, rows):
                if first:
                    act.wait_ge(moments, g + 1)
                    act.activation(dev[:, p, 0:n], mv[:, p, 0:n, 1], ACT.Sqrt, bias=K.eps[:, 0:1]).then_inc(devs, 1)
                    act.wait_ge(scales, g + 1)
                    act.wait_ge(out_free, g + 1)
                    for k in range(n):
                        act.activation(h[:, p, k, :], xin[:, p, k, :], ACT.Relu, bias=shift[:, p, k:k + 1],
                                       scale=scale[:, p, k:k + 1]).then_inc(h_up, 1)
                    act.wait_ge(h_up, tile + n)
                    act.sem_inc(used, 1)
                else:
                    for k in range(n):
                        act.wait_ge(low_up, tile + k + 1)
                        act.activation(low[:, p, k, :], low[:, p, k, :], ACT.Exp).then_inc(exp_up, 1)
                for k in range(n):
                    act.wait_ge(turned, tile + k + 1)
                    act.activation(hT[:, p, k, :], psT[:, k % 2, 0:F], ACT.Copy).then_inc(hT_up, 1)
            nodes.run(act, group)

        @block.vector
        def _(dve):
            dve.sem_inc(kept, G4)
            dve.sem_inc(out_free, 2)
            per = 2 if first else 4 * G4

            def group(tile, g, p, n, rows):
                link = LoopLinked(dve, linked, g, per)
                if first:
                    if rows != P:
                        dve.wait_ge(used, g + 1)
                        dve.memset(xin[:, p, n - 1, :], 0.0).then_inc(cleared, 1)
                    dve.wait_ge(loaded[p], half(g, p) * 32 + 32)
                    for k in range(n):
                        ins = dve.bn_stats(stats[:, p, k, :], xin[:, p, k, :])
                    link.run(ins)
                    dve.sem_inc(passed, 1)
                    for k in range(n):
                        ins = dve.bn_aggr(mv[:, p, k, :], stats[:, p, k, :])
                    ins.then_inc(moments, 1)
                    dve.wait_ge(devs, g + 1)
                    dve.wait_ge(moments, g + 1)
                    link.run(dve.reciprocal(scale[:, p, 0:n], dev[:, p, 0:n]))
                    dve.scalar_tensor_tensor(shift[:, p, 0:n], mv[:, p, 0:n, 0], -1.0, scale[:, p, 0:n], ALU.mult, ALU.mult)\
                        .then_inc(scales, 1)
                else:
                    dve.wait_ge(out_free, g + 1)
                    for k in range(n):
                        a = acc[:, bass.ds((tile + k) * ROW, ROW)].rearrange("p (h d) -> p h d", d=HW)
                        hk = h[:, p, k, :].rearrange("p (h d) -> p h d", d=D)
                        link.run(dve.tensor_scalar(den[:, p, k, :], a[:, :, D], 1e-30, None, ALU.max))
                        link.run(dve.reciprocal(den[:, p, k, :], den[:, p, k, :]))
                        link.run(dve.tensor_tensor(hk, a[:, :, 0:D], den[:, p, k, :].unsqueeze(2).broadcast_to([P, H, D]), ALU.mult))
                        dve.tensor_scalar(low[:, p, k, :], h[:, p, k, :], 0.0, None, ALU.min).then_inc(low_up, 1)
                        link.run(dve.tensor_scalar(h[:, p, k, :], h[:, p, k, :], 0.0, None, ALU.max))
                    for k in range(n):
                        dve.wait_ge(exp_up, tile + k + 1)
                        dve.scalar_tensor_tensor(h[:, p, k, :], low[:, p, k, :], -1.0, h[:, p, k, :], ALU.add, ALU.add)\
                            .then_inc(h_up, 1)
                if first:
                    dve.wait_ge(out_free, g + 1)
                for k in range(n):
                    dve.wait_ge(products, tile + k + 1)
                    dve.tensor_copy(er[:, bass.ds(tile + k, 1), :], psF[:, k, ROW:ROW + H].unsqueeze(1))
                    dve.tensor_copy(row[:, p, k, :], psF[:, k, 0:ROW]).then_inc(kept, 1)
            nodes.run(dve, group)
            dve.wait_ge(kept, NT + G4)
            link = Linked(dve, split)
            link.run(dve.tensor_copy(er3[:, :, 0, :], er[:, :, :]))
            link.run(dve.tensor_tensor(rest[:, :, :], er[:, :, :], er3[:, :, 0, :], ALU.subtract))
            link.run(dve.tensor_copy(er3[:, :, 1, :], rest[:, :, :]))
            link.run(dve.tensor_tensor(er3[:, :, 2, :], rest[:, :, :], er3[:, :, 1, :], ALU.subtract))


def attend(nc, S, K, M, er3, acc, layer):
    NI = S.NI
    TABLES = 9
    with ExitStack() as ctx:
        sb, ps, sem = allocators(nc, ctx, f"attend{layer}")
        G = sb("G", [P, 2, U, ROW])
        hot = sb("hot", [P, 2, U, P])
        hotT = sb("hotT", [P, U, P], BF16)
        index = sb("index", [P, 2, U], I32)
        local_b = sb("local_b", [P, 2, U * P], BF16)
        local_c = sb("local_c", [P, 2, U])
        apart = sb("apart", [R, 2, P + 1])
        whole = sb("whole", [H, 2, U])
        alike = sb("alike", [H, 2, U])
        goes_on = sb("goes_on", [H, 2, U + 1])
        tile_r = sb("tile_r", [1, S.V], I32)
        el = sb("el", [P, R])
        er = sb("er", [P, R])
        run = sb("run", [R, P])
        top = sb("top", [R, P])
        ends = sb("ends", [R, 2, U])
        last = sb("last", [H, 1])
        carry = sb("carry", [H, U + 1])
        back = sb("back", [H, U + 1])
        around = sb("around", [H, 2, U])
        through = sb("through", [H, 2, U])
        spread = sb("spread", [R, 2, U])
        start = sb("start", [R, 2])
        low = sb("low", [P, R])
        high = sb("high", [P, R])
        low2 = sb("low2", [P, R])
        high2 = sb("high2", [P, R])
        diff = sb("diff", [P, R])
        old = sb("old", [1, 3, H])
        shrink = sb("shrink", [1, 2 * H])
        first_n = sb("first_n", [P, 1])
        other = sb("other", [P, H])
        same = sb("same", [P, H])
        keep = sb("keep", [P, 2, H])
        psP = ps("psP", [P, BANKS, 512])
        psA = ps("psA", [P, 512])
        psE = ps("psE", [P, 512])
        psR = ps("psR", [P, 512])
        psS = ps("psS", [P, 512])
        elT, ends_p, start_p = psA[0:R, 0:P], psA[0:H, P:P + 2 * U], psA[0:R, 2 * P:2 * P + 2 * U]
        er_p = psE[:, 0:3 * R].rearrange("p (u k h) -> p k h u", k=3, h=H)
        top_p, old_p, keep_p = psR[:, 0:R], psR[0:1, P:P + R], psS[:, 0:2 * H]
        index_up, tables_up = ([sem(f"{n}{p}") for p in range(2)] for n in ("index_up", "tables_up"))
        gathered = [sem.lasting(f"gathered{p}") for p in range(2)]
        (tiles_up, el_up, hotT_up, hot_up, el_turned, er_up, ends_up, ends_in, around_up, start_in, top_up, top_turned,
         diff_up, weights_up, shrink_up, shrunk_up, keep_in, keep_up, weighed, summed, added, linked) = (sem(n) for n in (
             "tiles_up", "el_up", "hotT_up", "hot_up", "el_turned", "er_up", "ends_up", "ends_in", "around_up", "start_in",
             "top_up", "top_turned", "diff_up", "weights_up", "shrink_up", "shrunk_up", "keep_in", "keep_up", "weighed",
             "summed", "added", "dve_linked"))
        ready = sem("ready")
        passed_pe, passed_pool = sem("passed_pe"), sem("passed_pool")
        CREDIT = BANKS
        block = phase_block(nc, ctx, sem)

        def el_of(p):
            return G[:, p, :, :].rearrange("p u (h d) -> p h u d", d=HW)[:, :, :, D]

        @block.sync
        def _(sp):
            def tables(i, p):
                v = i * U
                sp.dma_start(index[:, p, :], M.src_col[:, bass.ds(v, U)]).then_inc(index_up[p], 16)
                row = M.local_row[bass.ds(v * P, U * P)].rearrange("(o n) -> o n", o=1)
                sp.dma_start(local_b[:, p, :], row.broadcast_to([P, U * P])).then_inc(tables_up[p], 16)
                sp.dma_start(local_c[:, p, :], M.local_col[:, bass.ds(v, U)]).then_inc(tables_up[p], 16)
                rows = M.apart[bass.ds(v * P, U * P)].rearrange("(u e) -> u e", e=P)
                for h in range(H):
                    sp.dma_start(apart[h * U:h * U + U, p, 0:P], rows).then_inc(tables_up[p], 16)
                for out, table, w in ((whole, M.whole, U), (alike, M.alike, U), (goes_on, M.goes_on, U + 1)):
                    line = table[bass.ds(v, w)].rearrange("(o n) -> o n", o=1)
                    sp.dma_start(out[:, p, :], line.broadcast_to([H, w])).then_inc(tables_up[p], 16)

            sp.dma_start(tile_r[:, :], M.tile.rearrange("(o n) -> o n", o=1)).then_inc(tiles_up, 16)
            tables(0, 0)
            tables(1, 1)
            with sp.Fori(0, NI // 2) as j:
                for p in range(2):
                    i = j * 2 + p
                    sp.wait_ge(gathered[p], j * (16 * U) + 16 * U)
                    sp.wait_ge(shrunk_up, i + 1)
                    sp.wait_ge(hot_up, 2 * i + 2)
                    tables(i + 2, p)
            sp.wait_ge(tiles_up, 16)
            for p in range(2):
                sp.wait_ge(tables_up[p], (NI // 2 + 1) * 16 * TABLES)
                sp.wait_ge(index_up[p], (NI // 2 + 1) * 16)

        @block.gpsimd
        def _(pool):
            def gather(j, p, before=None):
                hold(pool, index_up[p], j * 16 + 16, passed_pool)
                for u in range(U):
                    if before is not None and u % 2 == 0:
                        hold(pool, summed, before * U + u + 2, passed_pool)
                    pool.indirect_dma_start(G[:, p, u, :], None, M.table, bass.IndirectOffsetOnAxis(index[:, p, u:u + 1], 0))\
                        .then_inc(gathered[p], 16)
            gather(0, 0)
            gather(0, 1)
            with pool.Fori(0, NI // 2) as j:
                for p in range(2):
                    gather(j + 1, p, j * 2 + p)
            for p in range(2):
                pool.wait_ge(gathered[p], (NI // 2 + 1) * 16 * U)

        @block.tensor
        def _(pe):
            regs = [pe.alloc_register(f"pe{layer}_tile{u}") for u in range(U)]
            parts = er3.rearrange("p t k h -> p (t k h)")

            def prepare(i, p):
                pe.load(regs, tile_r[0:1, bass.ds(i * U, U)])
                hold(pe, el_up, i + 1, passed_pe)
                pe.transpose(elT, el[:, :], K.ident[:, :]).then_inc(el_turned, 1)
                yield
                pe.wait_ge(hotT_up, i + 1)
                for u in range(U):
                    t = pe.snap(regs[u], min_val=0, max_val=S.NT - 1)
                    mm = pe.matmul(psE[:, u * 3 * H:u * 3 * H + 3 * H], hotT[:, u, :], parts[:, bass.ds(t * (3 * H), 3 * H)],
                                   start=True, stop=True)
                mm.then_inc(er_up, 1)
                yield
                hold(pe, ends_up, i + 1, passed_pe)
                pe.matmul(ends_p, K.head_of[:, :], ends[:, :, :], start=True, stop=True).then_inc(ends_in, 1)
                yield
                hold(pe, around_up, i + 1, passed_pe)
                pe.matmul(start_p, K.rows_of[:, :], around[:, :, :], start=True, stop=True).then_inc(start_in, 1)
                yield
                hold(pe, top_up, i + 1, passed_pe)
                pe.transpose(top_p, top[:, :], K.ident[0:R, 0:R])
                pe.transpose(old_p, start[:, 0:1], K.ident[0:R, 0:R]).then_inc(top_turned, 1)
                yield
                hold(pe, shrunk_up, i + 1, passed_pe)
                pe.matmul(keep_p, K.ones[:, :], shrink[:, :], start=True, stop=True).then_inc(keep_in, 1)
                yield

            def sums(i, p, u):
                pe.wait_ge(weighed, i * U + u + 1)
                pe.wait_ge(added, i * U + u + 1)
                pe.matmul(psP[:, u % BANKS, 0:ROW], hot[:, p, u, :], G[:, p, u, :], start=True, stop=True).then_inc(summed, 1)

            pe.wait_ge(tiles_up, 16)
            pe.wait_ge(ready, 1)
            for _ in prepare(0, 0):
                pass
            after = {5, 6, 7, 8, 9, 15}
            with pe.Fori(0, NI // 2) as j:
                for p in range(2):
                    i = j * 2 + p
                    steps = prepare(i + 1, 1 - p)
                    pe.wait_ge(hot_up, 2 * i + 2)
                    for u in range(U):
                        sums(i, p, u)
                        if u in after:
                            next(steps, None)
                    for _ in steps:
                        pass

        @block.scalar
        def _(act):
            def weights(i, p):
                act.wait_ge(diff_up, i + 1)
                act.activation(shrink[:, 0:H], old[:, 2, :], ACT.Exp).then_inc(shrink_up, 1)
                act.activation(el_of(p), diff[:, :].rearrange("p (h u) -> p h u", h=H), ACT.Exp).then_inc(weights_up, 1)

            weights(0, 0)
            with act.Fori(0, NI // 2) as j:
                for p in range(2):
                    i = j * 2 + p
                    act.wait_ge(weights_up, i + 1)
                    for u in range(U):
                        for h in range(H):
                            row = G[:, p, u, h * HW:h * HW + D]
                            ins = act.activation(row, row, ACT.Copy, scale=G[:, p, u, h * HW + D:h * HW + HW])
                        ins.then_inc(weighed, 1)
                        if u == 14:
                            weights(i + 1, 1 - p)

        @block.vector
        def _(dve):
            regs = [dve.alloc_register(f"dve{layer}_tile{u}") for u in range(U)]
            LINKS = 16

            def prepare(i, p, j):
                link = LoopLinked(dve, linked, i, LINKS)
                by_head = lambda t: t.rearrange("p (h u) -> p h u", h=H)
                dve.wait_ge(tables_up[p], j * (16 * TABLES) + 16 * TABLES)
                dve.tensor_scalar(hotT[:, :, :].rearrange("p u e -> p (u e)"), local_b[:, p, :], K.row[:, 0:1], None, ALU.is_equal)\
                    .then_inc(hotT_up, 1)
                link.run(dve.tensor_scalar(through[:, 0, :], goes_on[:, p, 1:U + 1], -1.0, BIG, ALU.add, ALU.mult))
                dve.tensor_tensor(through[:, 1, :], through[:, 0, :], alike[:, p, :], ALU.add)
                yield
                dve.wait_ge(gathered[p], j * (16 * U) + 16 * U)
                dve.tensor_copy(by_head(el[:, :]), el_of(p)).then_inc(el_up, 1)
                yield
                dve.wait_ge(el_turned, i + 1)
                link.run(dve.tensor_tensor_scan(run[:, :], apart[:, p, 0:P], elT, -BIG, ALU.add, ALU.max))
                link.run(dve.tensor_tensor_scan(top[:, ::-1], apart[:, p, P:0:-1], run[:, ::-1], -BIG, ALU.add, ALU.max))
                dve.tensor_scalar(ends[:, 0, :], K.visit_of[:, :], run[:, P - 1:P], None, ALU.mult)
                dve.tensor_scalar(ends[:, 1, :], K.visit_of[:, :], top[:, 0:1], None, ALU.mult).then_inc(ends_up, 1)
                yield
                dve.wait_ge(ends_in, i + 1)
                link.run(dve.tensor_copy(last[:, :], carry[:, U:U + 1]))
                dve.tensor_copy(carry[:, 0:1], last[:, :])
                dve.tensor_tensor_scan(carry[:, 1:U + 1], whole[:, p, :], ends_p[:, 0:U], last[:, 0:1], ALU.add, ALU.max)
                link.run(dve.tensor_tensor_scan(back[:, U - 1::-1], through[:, 1, ::-1], ends_p[:, 2 * U - 1:U - 1:-1], -BIG, ALU.add, ALU.max))
                dve.tensor_copy(around[:, 0, :], carry[:, 0:U])
                dve.tensor_tensor(around[:, 1, :], through[:, 0, :], back[:, 1:U + 1], ALU.add).then_inc(around_up, 1)
                yield
                dve.wait_ge(er_up, i + 1)
                link.run(dve.tensor_reduce(by_head(er[:, :]), er_p.rearrange("p k h u -> p h u k"), AX.X, ALU.add))
                link.run(dve.tensor_tensor(low[:, :], el[:, :], er[:, :], ALU.add))
                dve.scalar_tensor_tensor(low2[:, :], low[:, :], SLOPE, low[:, :], ALU.mult, ALU.max)
                yield
                dve.wait_ge(start_in, i + 1)
                link.run(dve.tensor_tensor(spread[:, :, :], start_p.rearrange("r (k u) -> r k u", k=2),
                                           K.visit_of[:, :].unsqueeze(1).broadcast_to([R, 2, U]), ALU.mult))
                link.run(dve.tensor_reduce(start[:, :], spread[:, :, :], AX.X, ALU.add))
                link.run(dve.tensor_tensor_scan(run[:, :], apart[:, p, 0:P], elT, start[:, 0:1], ALU.add, ALU.max))
                dve.tensor_tensor_scan(top[:, ::-1], apart[:, p, P:0:-1], run[:, ::-1], start[:, 1:2], ALU.add, ALU.max).then_inc(top_up, 1)
                yield
                dve.wait_ge(top_turned, i + 1)
                link.run(dve.tensor_tensor(high[:, :], top_p, er[:, :], ALU.add))
                dve.tensor_tensor(old[:, 0, :], by_head(old_p)[:, :, 0], by_head(er[0:1, :])[:, :, 0], ALU.add)
                link.run(dve.scalar_tensor_tensor(high2[:, :], high[:, :], SLOPE, high[:, :], ALU.mult, ALU.max))
                link.run(dve.scalar_tensor_tensor(old[:, 1, :], old[:, 0, :], SLOPE, old[:, 0, :], ALU.mult, ALU.max))
                link.run(dve.tensor_tensor(old[:, 2, :], old[:, 1, :], by_head(high2[0:1, :])[:, :, 0], ALU.subtract))
                dve.tensor_scalar(old[:, 2, :], old[:, 2, :], 0.0, None, ALU.min)
                dve.tensor_tensor(diff[:, :], low2[:, :], high2[:, :], ALU.subtract).then_inc(diff_up, 1)
                yield
                for n in range(2):
                    half_of = slice(n * (U // 2), (n + 1) * (U // 2))
                    dve.tensor_tensor(hot[:, p, half_of, :], K.col[:, :].unsqueeze(1).broadcast_to([P, U // 2, P]),
                                      local_c[:, p, half_of].unsqueeze(2).broadcast_to([P, U // 2, P]), ALU.is_equal).then_inc(hot_up, 1)
                    yield
                dve.wait_ge(shrink_up, i + 1)
                dve.tensor_copy(shrink[:, H:2 * H], goes_on[0:1, p, 0:1].broadcast_to([1, H]))
                dve.tensor_scalar(shrink[:, 0:H], shrink[:, 0:H], goes_on[0:1, p, 0:1], None, ALU.mult).then_inc(shrunk_up, 1)
                yield
                link.run(dve.tensor_copy(first_n[:, :], hotT[:, 0, 0:1]))
                dve.wait_ge(keep_in, i + 1)
                dve.tensor_scalar(other[:, :], keep_p[:, H:2 * H], first_n[:, 0:1], -1.0, ALU.mult, ALU.mult)
                link.run(dve.tensor_scalar(same[:, :], keep_p[:, 0:H], first_n[:, 0:1], None, ALU.mult))
                dve.scalar_tensor_tensor(keep[:, p, :], other[:, :], 1.0, same[:, :], ALU.add, ALU.add).then_inc(keep_up, 1)
                assert link.n == LINKS, link.n
                yield

            def add(i, p, u):
                t = dve.snap(regs[u], min_val=0, max_val=S.NT - 1)
                if u == 0:
                    dve.wait_ge(keep_up, i + 1)
                dve.wait_ge(summed, i * U + u + 1)
                dve.wait_ge(added, i * U + (u + CREDIT))
                if u == 0:
                    for h in range(H):
                        s = acc[:, bass.ds(t * ROW + h * HW, HW)]
                        ins = dve.scalar_tensor_tensor(s, s, keep[:, p, h:h + 1], psP[:, u % BANKS, h * HW:h * HW + HW],
                                                       ALU.mult, ALU.add)
                else:
                    s = acc[:, bass.ds(t * ROW, ROW)]
                    ins = dve.tensor_tensor(s, s, psP[:, u % BANKS, 0:ROW], ALU.add)
                ins.then_inc(added, 1)

            dve.memset(apart[:, :, P:P + 1], 0.0)
            dve.memset(back[:, :], -BIG)
            dve.memset(carry[:, :], -BIG).then_inc(ready, 1)
            dve.wait_ge(ready, 1)
            dve.memset(acc[:, :], 0.0).then_inc(added, CREDIT)
            dve.wait_ge(tiles_up, 16)
            for _ in prepare(0, 0, 0):
                pass
            after = {0, 2, 4, 5, 6, 7, 8, 10, 12, 13, 14}
            with dve.Fori(0, NI // 2) as j:
                for p in range(2):
                    i = j * 2 + p
                    steps = prepare(i + 1, 1 - p, j + p)
                    dve.load(regs, tile_r[0:1, bass.ds(i * U, U)])
                    for u in range(U):
                        add(i, p, u)
                        if u in after:
                            next(steps, None)
                    for _ in steps:
                        pass
            dve.wait_ge(added, NI * U + CREDIT)


def renew_nodes(nc, S, K, M, x, acc):
    nodes = Nodes(S)
    with ExitStack() as ctx:
        sb, ps, sem = allocators(nc, ctx, "renew")
        xin = sb("xin", [P, 2, G4, F])
        hin = sb("hin", [P, 2, G4, F])
        r = sb("r", [P, 2, G4, F])
        low = sb("low", [P, 2, G4, F])
        h = sb("h", [P, 2, G4, F])
        xh = sb("xh", [P, 2, G4, F])
        stats = sb("stats", [P, 2, G4, nc.vector.BN_STATS_DIM])
        mv = sb("mv", [P, 2, G4, 2])
        den = sb("den", [P, 2, G4, H])
        dev = sb("dev", [P, 2, G4])
        scale = sb("scale", [P, 2, G4])
        shift = sb("shift", [P, 2, G4])
        used, moments, devs, scales, h_up, low_up, exp_up, xh_up, out_free, linked, cleared = (sem(n) for n in (
            "inputs_used", "moments", "devs", "scales", "h_up", "low_up", "exp_up", "xh_up", "out_free", "dve_linked", "cleared"))
        passed = sem("passed")
        loaded = [sem("loaded0"), sem("loaded1")]
        stored = [sem.lasting("stored0"), sem.lasting("stored1")]
        block = phase_block(nc, ctx, sem)

        @block.sync
        def _(sp):
            def group(tile, g, p, n, rows):
                sp.wait_ge(used, g + 1)
                if rows != P:
                    sp.wait_ge(cleared, 1)
                load_tiles(sp, xin, p, x, tile, n, rows, loaded[p])
                sp.dma_start(hin[:, p, 0:n, :], tiles_of(M.h2, tile, n)).then_inc(loaded[p], 16)
            nodes.run(sp, group)

        @block.gpsimd
        def _(pool):
            def group(tile, g, p, n, rows):
                pool.wait_ge(xh_up, tile + n)
                pool.wait_ge(h_up, tile + n)
                pool.dma_start(tiles_of(M.h3, tile, n), h[:, p, 0:n, :]).then_inc(stored[p], 16)
                pool.dma_start(tiles_of(M.xh, tile, n), xh[:, p, 0:n, :]).then_inc(stored[p], 16)
                pool.wait_ge(stored[p], half(g, p) * 32 + 32)
                pool.sem_inc(out_free, 1)
            nodes.run(pool, group)

        @block.scalar
        def _(act):
            def group(tile, g, p, n, rows):
                for k in range(n):
                    act.wait_ge(low_up, tile + k + 1)
                    act.activation(low[:, p, k, :], low[:, p, k, :], ACT.Exp).then_inc(exp_up, 1)
                act.wait_ge(moments, g + 1)
                act.activation(dev[:, p, 0:n], mv[:, p, 0:n, 1], ACT.Sqrt, bias=K.eps[:, 0:1]).then_inc(devs, 1)
                act.wait_ge(scales, g + 1)
                act.wait_ge(out_free, g + 1)
                for k in range(n):
                    act.activation(h[:, p, k, :], r[:, p, k, :], ACT.Relu, bias=shift[:, p, k:k + 1],
                                   scale=scale[:, p, k:k + 1]).then_inc(h_up, 1)
            nodes.run(act, group)

        @block.vector
        def _(dve):
            dve.sem_inc(used, 2)
            dve.sem_inc(out_free, 2)
            per = 4 * G4 + 4

            def group(tile, g, p, n, rows):
                link = LoopLinked(dve, linked, g, per)
                if rows != P:
                    dve.wait_ge(used, g + 1)
                    dve.memset(xin[:, p, n - 1, :], 0.0).then_inc(cleared, 1)
                dve.wait_ge(loaded[p], half(g, p) * 48 + 48)
                for k in range(n):
                    a = acc[:, bass.ds((tile + k) * ROW, ROW)].rearrange("p (h d) -> p h d", d=HW)
                    rk = r[:, p, k, :].rearrange("p (h d) -> p h d", d=D)
                    link.run(dve.tensor_scalar(den[:, p, k, :], a[:, :, D], 1e-30, None, ALU.max))
                    link.run(dve.reciprocal(den[:, p, k, :], den[:, p, k, :]))
                    link.run(dve.tensor_tensor(rk, a[:, :, 0:D], den[:, p, k, :].unsqueeze(2).broadcast_to([P, H, D]), ALU.mult))
                    link.run(dve.tensor_tensor(r[:, p, k, :], r[:, p, k, :], hin[:, p, k, :], ALU.add))
                    dve.tensor_scalar(low[:, p, k, :], r[:, p, k, :], 0.0, None, ALU.min).then_inc(low_up, 1)
                    ins = dve.scalar_tensor_tensor(r[:, p, k, :], r[:, p, k, :], 0.0, xin[:, p, k, :], ALU.max, ALU.add)
                link.run(ins)
                for k in range(n):
                    dve.wait_ge(exp_up, tile + k + 1)
                    ins = dve.scalar_tensor_tensor(r[:, p, k, :], low[:, p, k, :], -1.0, r[:, p, k, :], ALU.add, ALU.add)
                link.run(ins)
                dve.sem_inc(used, 1)
                for k in range(n):
                    ins = dve.bn_stats(stats[:, p, k, :], r[:, p, k, :])
                link.run(ins)
                dve.sem_inc(passed, 1)
                for k in range(n):
                    ins = dve.bn_aggr(mv[:, p, k, :], stats[:, p, k, :])
                ins.then_inc(moments, 1)
                dve.wait_ge(devs, g + 1)
                link.run(dve.reciprocal(scale[:, p, 0:n], dev[:, p, 0:n]))
                dve.scalar_tensor_tensor(shift[:, p, 0:n], mv[:, p, 0:n, 0], -1.0, scale[:, p, 0:n], ALU.mult, ALU.mult)\
                    .then_inc(scales, 1)
                dve.wait_ge(out_free, g + 1)
                for k in range(n):
                    dve.wait_ge(h_up, tile + k + 1)
                    dve.tensor_tensor(xh[:, p, k, :], r[:, p, k, :], h[:, p, k, :], ALU.add).then_inc(xh_up, 1)
            nodes.run(dve, group)


def split_bias(dve, link, K, out, b3, part, rest):
    link.run(dve.tensor_copy(part[:, :], b3[:, :]))
    for k in range(3):
        link.run(dve.tensor_scalar(rest[:, 1, :], part[:, :], K.col3[:, k:k + 1], None, ALU.mult))
        if k == 0:
            link.run(dve.tensor_copy(out[:, :], rest[:, 1, :]))
        else:
            link.run(dve.tensor_tensor(out[:, :], out[:, :], rest[:, 1, :], ALU.add))
        if k < 2:
            link.run(dve.tensor_tensor(b3[:, :], b3[:, :], part[:, :], ALU.subtract))
            link.run(dve.tensor_copy(part[:, :], b3[:, :]))


def pass_messages(nc, S, K, M, attr, W1_d, b1_d, W2_d, b2_d, acc):
    NI = S.NI
    Q = 4
    with ExitStack() as ctx:
        sb, ps, sem = allocators(nc, ctx, "messages")
        G = sb("G", [P, 2, U, F])
        hot = sb("hot", [P, 2, U, P])
        index = sb("index", [P, 2, U], I32)
        local_c = sb("local_c", [P, 2, U])
        rbf = sb("rbf", [P, 2, U, NR])
        rbfT = sb("rbfT", [NR, Q * P])
        hidden = sb("hidden", [P, 2, Q * P])
        weighed_credit = sem("gate_free")
        gate = sb("gate", [P, 2, 2, F])
        tile_r = sb("tile_r", [1, S.V], I32)
        block_r = sb("block_r", [1, S.V], I32)
        W1 = sb("W1", [NR, F])
        W2 = sb("W2", [P, 2, F])
        b1 = sb("b1", [P, 2])
        b2 = sb("b2", [3, F])
        b2_3 = sb("b2_3", [3, F], BF16)
        part = sb("part", [3, F], BF16)
        rest = sb("rest", [3, 2, F])
        psX = ps("psX", [NR, 512])
        psH = ps("psH", [P, 2, 512])
        psG = ps("psG", [P, 2, 512])
        psP = ps("psP", [P, 2, 2, F])
        index_up, tables_up = ([sem(f"{n}{p}") for p in range(2)] for n in ("index_up", "tables_up"))
        gathered = [sem.lasting(f"gathered{p}") for p in range(2)]
        (lists_up, weights_up, ready, hot_up, turned, rbfT_up, hidden_in, hidden_up, gate_in, gate_up, weighed, summed,
         added, linked) = (sem(n) for n in (
             "lists_up", "weights_up", "ready", "hot_up", "attributes_turned", "rbfT_up", "hidden_in", "hidden_up", "gate_in",
             "gate_up", "weighed", "summed", "added", "dve_linked"))
        passed_pe, passed_pool = sem("passed_pe"), sem("passed_pool")
        CREDIT = 4
        block = phase_block(nc, ctx, sem)

        @block.sync
        def _(sp):
            regs = [sp.alloc_register(f"sp_block{u}") for u in range(U)]
            sp.dma_start(tile_r[:, :], M.tile.rearrange("(o n) -> o n", o=1)).then_inc(lists_up, 16)
            sp.dma_start(block_r[:, :], M.block.rearrange("(o n) -> o n", o=1)).then_inc(lists_up, 16)
            sp.dma_start(W1[:, :], W1_d).then_inc(weights_up, 16)
            sp.dma_start(W2[:, :, :], W2_d.rearrange("(k p) f -> p k f", p=P)).then_inc(weights_up, 16)
            sp.dma_start(b1[:, :].unsqueeze(2), b1_d.rearrange("(k p o) -> p k o", p=P, o=1), allow_slow_non_contiguous=True)\
                .then_inc(weights_up, 16)
            sp.dma_start(b2[:, :], b2_d.rearrange("(o f) -> o f", o=1).broadcast_to([3, F])).then_inc(weights_up, 16)
            sp.wait_ge(lists_up, 32)

            def tables(i, p):
                sp.dma_start(index[:, p, :], M.src_col[:, bass.ds(i * U, U)]).then_inc(index_up[p], 16)
                sp.dma_start(local_c[:, p, :], M.local_col[:, bass.ds(i * U, U)]).then_inc(tables_up[p], 16)
                sp.load(regs, block_r[0:1, bass.ds(i * U, U)])
                for u in range(U):
                    b = sp.snap(regs[u], min_val=0, max_val=S.EB - 1)
                    sp.dma_start(rbf[:, p, u, :], attr[bass.ds(b * P, P), :]).then_inc(tables_up[p], 16)

            tables(0, 0)
            tables(1, 1)
            with sp.Fori(0, NI // 2) as j:
                for p in range(2):
                    i = j * 2 + p
                    sp.wait_ge(gathered[p], j * (16 * U) + 16 * U)
                    sp.wait_ge(hot_up, i + 1)
                    sp.wait_ge(turned, i * (U // Q) + U // Q)
                    tables(i + 2, p)
            for p in range(2):
                sp.wait_ge(tables_up[p], (NI // 2 + 1) * 16 * (U + 1))
                sp.wait_ge(index_up[p], (NI // 2 + 1) * 16)

        @block.gpsimd
        def _(pool):
            def gather(j, p, before=None):
                hold(pool, index_up[p], j * 16 + 16, passed_pool)
                for u in range(U):
                    if before is not None:
                        hold(pool, summed, before * U + u + 1, passed_pool)
                    pool.indirect_dma_start(G[:, p, u, :], None, M.h3, bass.IndirectOffsetOnAxis(index[:, p, u:u + 1], 0))\
                        .then_inc(gathered[p], 16)
            gather(0, 0)
            gather(0, 1)
            with pool.Fori(0, NI // 2) as j:
                for p in range(2):
                    gather(j + 1, p, j * 2 + p)
            for p in range(2):
                pool.wait_ge(gathered[p], (NI // 2 + 1) * 16 * U)

        @block.tensor
        def _(pe):
            def turn(q, p, s, j):
                if s == 0:
                    pe.wait_ge(tables_up[p], j * (16 * (U + 1)) + 16 * (U + 1))
                if not (isinstance(q, int) and q == 0):
                    hold(pe, rbfT_up, q, passed_pe)
                for k in range(Q):
                    mm = pe.transpose(psX[:, k * P:k * P + P], rbf[:, p, s * Q + k, :], K.ident[:, :])
                mm.then_inc(turned, 1)

            def first(q):
                pe.wait_ge(rbfT_up, q + 1)
                if not (isinstance(q, int) and q == 0):
                    pe.wait_ge(hidden_up, 2 * q)
                for m in range(2):
                    pe.matmul(psH[:, m, :], W1[:, m * P:m * P + P], rbfT[:, :], start=True, stop=True).then_inc(hidden_in, 1)

            def second(q, c):
                if c == 0:
                    pe.wait_ge(hidden_up, 2 * q + 2)
                pe.wait_ge(gate_up, 2 * q + c + 1)
                for k in range(2):
                    out = psG[:, c, k * F:k * F + F]
                    e = (c * 2 + k) * P
                    pe.matmul(out, K.ones3[:, :], b2_3[:, :], start=True, stop=False)
                    for m in range(2):
                        mm = pe.matmul(out, hidden[:, m, e:e + P], W2[:, m, :], start=False, stop=(m == 1))
                mm.then_inc(gate_in, 1)

            def sums(q, p, s, c):
                pe.wait_ge(weighed, 2 * q + c + 1)
                pe.wait_ge(added, Q * q + (2 * c + 2))
                for k in range(2):
                    v = 2 * c + k
                    pe.matmul(psP[:, c, k, :], hot[:, p, s * Q + v, :], G[:, p, s * Q + v, :], start=True, stop=True).then_inc(summed, 1)

            pe.wait_ge(weights_up, 64)
            pe.wait_ge(ready, 1)
            turn(0, 0, 0, 0)
            first(0)
            with pe.Fori(0, NI // 2) as j:
                for p in range(2):
                    for s in range(U // Q):
                        q = j * (2 * U // Q) + (p * (U // Q) + s)
                        wraps = s == U // Q - 1
                        second(q, 0)
                        second(q, 1)
                        turn(q + 1, (1 - p) if wraps else p, 0 if wraps else s + 1, j + 1 if p and wraps else j)
                        if s == 0:
                            pe.wait_ge(hot_up, j * 2 + p + 1)
                        sums(q, p, s, 0)
                        first(q + 1)
                        sums(q, p, s, 1)

        @block.scalar
        def _(act):
            def silus(q):
                for m in range(2):
                    act.wait_ge(hidden_in, 2 * q + m + 1)
                    act.activation(hidden[:, m, :], psH[:, m, :], ACT.Silu, bias=b1[:, m:m + 1]).then_inc(hidden_up, 1)

            act.sem_inc(gate_up, 2)
            act.wait_ge(weights_up, 64)
            silus(0)
            with act.Fori(0, NI // 2 * 2 * (U // Q)) as q:
                for c in range(2):
                    act.wait_ge(gate_in, 2 * q + c + 1)
                    act.wait_ge(weighed_credit, 2 * q + c + 1)
                    act.activation(gate[:, c, :, :], psG[:, c, :], ACT.Tanh, scale=0.5).then_inc(gate_up, 1)
                silus(q + 1)

        @block.vector
        def _(dve):
            link = Linked(dve, linked)
            dve.wait_ge(weights_up, 64)
            split_bias(dve, link, K, b2_3, b2, part, rest)
            dve.memset(acc[:, :], 0.0).then_inc(added, CREDIT)
            dve.sem_inc(weighed_credit, 2)
            dve.sem_inc(ready, 1)
            dve.wait_ge(lists_up, 32)
            regs = [dve.alloc_register(f"dve_block{u}") for u in range(U)]

            def turn(q):
                dve.wait_ge(turned, q + 1)
                if not (isinstance(q, int) and q == 0):
                    dve.wait_ge(hidden_in, 2 * q)
                dve.tensor_copy(rbfT[:, :], psX[:, :]).then_inc(rbfT_up, 1)

            turn(0)
            with dve.Fori(0, NI // 2) as j:
                for p in range(2):
                    i = j * 2 + p
                    dve.load(regs, tile_r[0:1, bass.ds(i * U, U)])
                    dve.wait_ge(tables_up[p], j * (16 * (U + 1)) + 16 * (U + 1))
                    dve.tensor_tensor(hot[:, p, :, :], K.col[:, :].unsqueeze(1).broadcast_to([P, U, P]),
                                      local_c[:, p, :].unsqueeze(2).broadcast_to([P, U, P]), ALU.is_equal).then_inc(hot_up, 1)
                    dve.wait_ge(gathered[p], j * (16 * U) + 16 * U)
                    for s in range(U // Q):
                        q = j * (2 * U // Q) + (p * (U // Q) + s)
                        for c in range(2):
                            u = s * Q + 2 * c
                            dve.wait_ge(gate_up, 2 * q + c + 3)
                            dve.scalar_tensor_tensor(G[:, p, u:u + 2, :], gate[:, c, :, :], 1.0, G[:, p, u:u + 2, :],
                                                     ALU.add, ALU.mult).then_inc(weighed, 1)
                            dve.wait_ge(weighed, 2 * q + c + 1)
                            dve.sem_inc(weighed_credit, 1)
                        turn(q + 1)
                        for v in range(Q):
                            t = dve.snap(regs[s * Q + v], min_val=0, max_val=S.NT - 1)
                            dve.wait_ge(summed, Q * q + (v // 2 * 2 + 2))
                            dve.wait_ge(added, Q * q + (v + CREDIT))
                            a = acc[:, bass.ds(t * F, F)]
                            dve.tensor_tensor(a, a, psP[:, v // 2, v % 2, :], ALU.add).then_inc(added, 1)
            dve.wait_ge(added, NI * U + CREDIT)


def finish_nodes(nc, S, K, M, U1_d, c1_d, U2_d, c2_d, acc, out):
    nodes = Nodes(S)
    with ExitStack() as ctx:
        sb, ps, sem = allocators(nc, ctx, "finish")
        hin = sb("hin", [P, 2, G4, F])
        xh = sb("xh", [P, 2, G4, F])
        agg = sb("agg", [P, 2, G4, F])
        both = sb("both", [P, 2, 4, P])
        act1 = sb("act1", [P, 2, 2, P])
        res = sb("res", [P, 2, G4, F])
        U1 = sb("U1", [P, 4, F])
        U2 = sb("U2", [P, 2, F])
        c1 = sb("c1", [P, 2])
        c2 = sb("c2", [3, F])
        c2_3 = sb("c2_3", [3, F], BF16)
        part = sb("part", [3, F], BF16)
        rest = sb("rest", [3, 2, F])
        psT = ps("psT", [P, 2, 512])
        psH = ps("psH", [P, 2, 512])
        psO = ps("psO", [P, 2, 512])
        (weights_up, ready, agg_up, turned, both_up, hidden_in, hidden_up, products, res_up, out_free, in_free, linked) = (
            sem(n) for n in ("weights_up", "ready", "agg_up", "turned", "both_up", "hidden_in", "hidden_up", "products", "res_up",
                             "out_free", "in_free", "dve_linked"))
        both_free = sem("both_free")
        loaded = [sem("loaded0"), sem("loaded1")]
        stored = [sem.lasting("stored0"), sem.lasting("stored1")]
        block = phase_block(nc, ctx, sem)

        @block.sync
        def _(sp):
            sp.dma_start(U1[:, :, :], U1_d.rearrange("(k p) f -> p k f", p=P)).then_inc(weights_up, 16)
            sp.dma_start(U2[:, :, :], U2_d.rearrange("(k p) f -> p k f", p=P)).then_inc(weights_up, 16)
            sp.dma_start(c1[:, :].unsqueeze(2), c1_d.rearrange("(k p o) -> p k o", p=P, o=1), allow_slow_non_contiguous=True)\
                .then_inc(weights_up, 16)
            sp.dma_start(c2[:, :], c2_d.rearrange("(o f) -> o f", o=1).broadcast_to([3, F])).then_inc(weights_up, 16)

            def group(tile, g, p, n, rows):
                sp.wait_ge(in_free, g + 1)
                sp.dma_start(hin[:, p, 0:n, :], tiles_of(M.h3, tile, n)).then_inc(loaded[p], 16)
                sp.dma_start(xh[:, p, 0:n, :], tiles_of(M.xh, tile, n)).then_inc(loaded[p], 16)
            nodes.run(sp, group)

        @block.gpsimd
        def _(pool):
            def group(tile, g, p, n, rows):
                pool.wait_ge(res_up, tile + n + 2)
                pool.sem_inc(in_free, 1)
                pool.dma_start(tiles_of(out, tile, n - 1), res[:, p, 0:n - 1, :]).then_inc(stored[p], 16)
                pool.dma_start(out[bass.ds((tile + n - 1) * P, rows), :], res[0:rows, p, n - 1, :]).then_inc(stored[p], 16)
                pool.wait_ge(stored[p], half(g, p) * 32 + 32)
                pool.sem_inc(out_free, 1)
            nodes.run(pool, group)

        @block.tensor
        def _(pe):
            pe.wait_ge(ready, 1)

            def turn(T, p, k):
                pe.wait_ge(agg_up, T + 1)
                pe.wait_ge(both_up, T + 1)
                for c in range(4):
                    rows = hin if c < 2 else agg
                    mm = pe.transpose(psT[:, k % 2, c * P:c * P + P], rows[:, p, k, c % 2 * P:c % 2 * P + P], K.ident[:, :])
                mm.then_inc(turned, 1)

            def first(T, k):
                pe.wait_ge(both_up, T + 3)
                pe.wait_ge(hidden_up, T + 1)
                for m in range(2):
                    for c in range(4):
                        mm = pe.matmul(psH[:, k % 2, m * P:m * P + P], U1[:, c, m * P:m * P + P], both[:, k % 2, c, :],
                                       start=(c == 0), stop=(c == 3))
                mm.then_inc(hidden_in, 1)
                pe.wait_ge(hidden_in, T + 1)
                pe.sem_inc(both_free, 1)

            def second(T, k):
                pe.wait_ge(hidden_up, T + 3)
                pe.wait_ge(res_up, T + 1)
                pe.matmul(psO[:, k % 2, 0:F], K.ones3[:, :], c2_3[:, :], start=True, stop=False)
                for m in range(2):
                    mm = pe.matmul(psO[:, k % 2, 0:F], act1[:, k % 2, m, :], U2[:, m, :], start=False, stop=(m == 1))
                mm.then_inc(products, 1)

            def group(tile, g, p, n, rows):
                pe.wait_ge(loaded[p], half(g, p) * 32 + 32)
                turn(tile, p, 0)
                for k in range(n):
                    if k + 1 < n:
                        turn(tile + k + 1, p, k + 1)
                    first(tile + k, k)
                    if k:
                        second(tile + k - 1, k - 1)
                second(tile + n - 1, n - 1)
            nodes.run(pe, group)

        @block.scalar
        def _(act):
            act.sem_inc(hidden_up, 2)
            act.wait_ge(weights_up, 64)

            def group(tile, g, p, n, rows):
                for k in range(n):
                    T = tile + k
                    act.wait_ge(hidden_in, T + 1)
                    for m in range(2):
                        ins = act.activation(act1[:, k % 2, m, :], psH[:, k % 2, m * P:m * P + P], ACT.Silu, bias=c1[:, m:m + 1])
                    ins.then_inc(hidden_up, 1)
            nodes.run(act, group)

        @block.vector
        def _(dve):
            link = Linked(dve, linked)
            dve.wait_ge(weights_up, 64)
            split_bias(dve, link, K, c2_3, c2, part, rest)
            dve.sem_inc(ready, 1)
            dve.sem_inc(both_up, 2)
            dve.sem_inc(both_free, 2)
            dve.sem_inc(res_up, 2)
            dve.sem_inc(in_free, 2)
            dve.sem_inc(out_free, 2)

            def group(tile, g, p, n, rows):
                dve.wait_ge(out_free, g + 1)
                for k in range(n):
                    dve.tensor_scalar(agg[:, p, k, :], acc[:, bass.ds((tile + k) * F, F)], 0.5, None, ALU.mult).then_inc(agg_up, 1)
                dve.wait_ge(loaded[p], half(g, p) * 32 + 32)
                for k in range(n + 1):
                    if k < n:
                        dve.wait_ge(turned, tile + k + 1)
                        dve.wait_ge(both_free, tile + k + 1)
                        dve.tensor_copy(both[:, k % 2, :, :], psT[:, k % 2, :].rearrange("p (c e) -> p c e", c=4)).then_inc(both_up, 1)
                    if k:
                        dve.wait_ge(products, tile + k)
                        dve.tensor_tensor(res[:, p, k - 1, :], psO[:, k % 2 ^ 1, 0:F], xh[:, p, k - 1, :], ALU.add).then_inc(res_up, 1)
            nodes.run(dve, group)


class Memory:

    def __init__(self, nc, S):
        def dram(name, shape, dt=F32):
            return nc.dram_tensor(name, shape, dt).ap()

        V = S.V
        self.dst_e = dram("dst_e", (S.EB * P,), I32)
        self.src_e = dram("src_e", (S.EB * P,), I32)
        self.dst_v = dram("dst_v", (1 + V * P,))
        self.tile = dram("tile", (V,), I32)
        self.block = dram("block", (V,), I32)
        self.local_row = dram("local_row", (V * P,), BF16)
        self.local_col = dram("local_col", (P, V))
        self.src_col = dram("src_col", (P, V), I32)
        self.apart = dram("apart", (V * P,))
        self.whole = dram("whole", (V,))
        self.alike = dram("alike", (V,))
        self.goes_on = dram("goes_on", (V,))
        self.table = dram("table", (S.NT * P, ROW))
        self.h2 = dram("h2", (S.NT * P, F))
        self.h3 = dram("h3", (S.NT * P, F))
        self.xh = dram("xh", (S.NT * P, F))
        self.attr = dram("attr", (S.EB * P, NR))


class Patterns:
    pass


def pad_attributes(nc, S, K, M, attr):
    tail = S.EB * P - S.E
    with ExitStack() as ctx:
        sb, ps, sem = allocators(nc, ctx, "pad")
        zeros = sb("zeros", [tail, NR])
        cleared, copied = sem("cleared"), sem("copied")
        block = phase_block(nc, ctx, sem)
        lines = 1600 if S.E % 1600 == 0 else 16

        @block.vector
        def _(dve):
            dve.memset(zeros[:, :], 0.0).then_inc(cleared, 1)

        @block.sync
        def _(sp):
            sp.dma_start(M.attr[0:S.E, :].rearrange("(a b) f -> a (b f)", a=lines), attr.rearrange("(a b) f -> a (b f)", a=lines))\
                .then_inc(copied, 16)
            sp.wait_ge(cleared, 1)
            sp.dma_start(M.attr[S.E:S.EB * P, :], zeros[:, :]).then_inc(copied, 16)
            sp.wait_ge(copied, 32)


def build(nc, x, src, dst, attr, W1, al1, ar1, W2, al2, ar2, V1, b1, V2, b2, U1, c1, U2, c2, out, upto=99):
    S = Sizes(x.shape[0], src.shape[0])
    M = Memory(nc, S)
    with ExitStack() as ctx:
        outer[0] = ctx
        sb, _, sem = allocators(nc, ctx, "all")
        K = Patterns()
        K.col = sb("col", [P, P])
        K.row = sb("rown", [P, 1])
        K.ident = sb("ident", [P, P])
        K.hu = sb("hu", [R, 2])
        K.head_of = sb("head_of", [R, H])
        K.visit_of = sb("visit_of", [R, U])
        K.rows_of = sb("rows_of", [H, R])
        K.ones = sb("ones", [1, P])
        K.ones3 = sb("ones3", [3, P], BF16)
        K.col3 = sb("col3", [3, 3])
        K.eps = sb("eps", [P, 1])
        constants(nc, K)
        pad_attributes(nc, S, K, M, attr)
        visit_tables(nc, S, K, M, src, dst)
        er3 = sb("er3", [P, S.NT, 3, H], BF16)
        acc = sb("acc", [P, S.NT * ROW])
        Waug = sb("Waug", [P, 2, ROW + H])
        attention_weights(nc, K, M, W1, al1, ar1, Waug, 1)
        project_nodes(nc, S, K, M, True, x, Waug, er3, acc)
        attend(nc, S, K, M, er3, acc, 1)
        attention_weights(nc, K, M, W2, al2, ar2, Waug, 2)
        project_nodes(nc, S, K, M, False, x, Waug, er3, acc)
        attend(nc, S, K, M, er3, acc, 2)
        renew_nodes(nc, S, K, M, x, acc)
        pass_messages(nc, S, K, M, M.attr, V1, b1, V2, b2, acc)
        finish_nodes(nc, S, K, M, U1, c1, U2, c2, acc, out)


_INS = ["x", "src", "dst", "edge_attr_64", "L0_gnn_W1", "L0_gnn_al1", "L0_gnn_ar1", "L0_gnn_W2", "L0_gnn_al2", "L0_gnn_ar2",
        "L1_gnn_W1", "L1_gnn_b1", "L1_gnn_W2", "L1_gnn_b2", "L1_gnn_U1", "L1_gnn_c1", "L1_gnn_U2", "L1_gnn_c2"]


def kernel(**inputs):
    import numpy as _np
    import concourse.bacc as _bacc
    from concourse import mybir as _mybir
    from concourse.bass_utils import run_bass_kernel_spmd as _run

    nc = _bacc.Bacc("TRN2", target_bir_lowering=False, num_devices=1)
    arrays, args = {}, []
    for name in _INS:
        a = _np.ascontiguousarray(inputs[name])
        arrays[f"in_{name}_dram"] = a
        args.append(nc.dram_tensor(f"in_{name}_dram", a.shape, _mybir.dt.from_np(a.dtype), kind="ExternalInput").ap())
    out = nc.dram_tensor("out_0_dram", tuple(inputs["x"].shape), _mybir.dt.float32, kind="ExternalOutput").ap()
    build(nc, *args, out)
    r = _run(nc, [arrays], core_ids=[0])
    return r.results[0]["out_0_dram"]
```

```python
from contextlib import ExitStack

import concourse.bass as bass
from concourse import mybir

P = 128
F = 256
H = 4
D = F // H
HW = D + 1
ROW = H * HW
NR = 64
U = 16
R = H * U
G4 = 4
BIG = 1.0e30
SLOPE = 0.2
EPS = 1.0e-5
BANKS = 4

F32 = mybir.dt.float32
F32R = mybir.dt.float32r
I32 = mybir.dt.int32
BF16 = mybir.dt.bfloat16
ALU = mybir.AluOpType
ACT = mybir.ActivationFunctionType
AX = mybir.AxisListType


class Linked:

    def __init__(self, eng, sem):
        self.eng, self.sem, self.n = eng, sem, 0

    def run(self, ins):
        self.n += 1
        ins.then_inc(self.sem, 1)
        self.eng.wait_ge(self.sem, self.n)


class LoopLinked:

    def __init__(self, eng, sem, turn, per):
        self.eng, self.sem, self.turn, self.per, self.n = eng, sem, turn, per, 0

    def run(self, ins):
        self.n += 1
        assert self.n <= self.per
        ins.then_inc(self.sem, 1)
        self.eng.wait_ge(self.sem, self.turn * self.per + self.n)


class Sizes:
    def __init__(self, n, e):
        self.N, self.E = n, e
        self.NT = -(-n // P)
        self.EB = -(-e // P)
        self.LAST = n - (self.NT - 1) * P
        assert self.LAST < P and self.NT % (2 * G4) == 2
        most = self.EB + self.NT - 1
        self.NI = 2 * -(-most // (2 * U))
        self.NC = -(-(self.NI + 2) * U // P)
        self.V = self.NC * P


outer = [None]


def allocators(nc, ctx, phase):
    def sb(name, shape, dt=F32):
        return ctx.enter_context(nc.sbuf_tensor(f"{phase}_{name}", shape, dt))

    def ps(name, shape):
        return ctx.enter_context(nc.psum_tensor(f"{phase}_{name}", shape, F32))

    def sem(name):
        made.append(ctx.enter_context(nc.semaphore(f"{phase}_{name}")))
        return made[-1]

    def lasting(name):
        return outer[0].enter_context(nc.semaphore(f"{phase}_{name}"))

    made = []
    sem.made, sem.lasting = made, lasting
    return sb, ps, sem


def phase_block(nc, ctx, sem):
    def clear():
        with nc.Block() as after:
            @after.gpsimd
            def _(pool):
                for s in sem.made:
                    pool.sem_clear(s)

    ctx.callback(clear)
    return ctx.enter_context(nc.Block())


def constants(nc, K):
    with ExitStack() as ctx:
        sb, ps, sem = allocators(nc, ctx, "constants")
        col_i, row_i, head_i, fill = (sb(n, s, I32) for n, s in
                                ((("col_i", [P, P])), ("row_i", [P, 1]), ("head_i", [H, R]), ("fill", [R, 2])))
        iotas, linked = sem("iotas"), sem("dve_linked")
        block = phase_block(nc, ctx, sem)

        @block.gpsimd
        def _(pool):
            pool.iota(col_i[:, :], [[1, P]], base=0, channel_multiplier=0).then_inc(iotas, 1)
            pool.iota(row_i[:, :], [[0, 1]], base=0, channel_multiplier=1).then_inc(iotas, 1)
            pool.iota(head_i[:, :], [[1, H], [0, U]], base=0, channel_multiplier=0).then_inc(iotas, 1)

        @block.vector
        def _(dve):
            link = Linked(dve, linked)
            dve.wait_ge(iotas, 3)
            link.run(dve.tensor_copy(K.col[:, :], col_i[:, :]))
            link.run(dve.tensor_copy(K.row[:, :], row_i[:, :]))
            link.run(dve.tensor_scalar(K.ident[:, :], K.col[:, :], K.row[:, 0:1], None, ALU.is_equal))
            dve.tensor_copy(K.ident_r[:, :], K.ident[:, :])
            link.run(dve.tensor_scalar(fill[:, 0:1], row_i[0:R, :], U.bit_length() - 1, None,
                                       ALU.logical_shift_right))
            link.run(dve.tensor_scalar(fill[:, 1:2], row_i[0:R, :], U - 1, None, ALU.bitwise_and))
            link.run(dve.tensor_copy(K.hu[:, :], fill[:, :]))
            link.run(dve.tensor_scalar(K.head_of[:, :], K.col[0:R, 0:H], K.hu[:, 0:1], None, ALU.is_equal))
            link.run(dve.tensor_scalar(K.visit_of[:, :], K.col[0:R, 0:U], K.hu[:, 1:2], None, ALU.is_equal))
            link.run(dve.tensor_copy(K.rows_of[:, :], head_i[:, :]))
            link.run(dve.tensor_scalar(K.rows_of[:, :], K.rows_of[:, :], K.row[0:H, 0:1], None, ALU.is_equal))
            link.run(dve.memset(K.ones[:, :], 1.0))
            link.run(dve.memset(K.every[:, :], 1.0))
            link.run(dve.memset(K.ones3[:, :], 1.0))
            link.run(dve.tensor_copy(K.col3[:, :], K.ident[0:3, 0:3]))
            link.run(dve.memset(K.eps[:, :], EPS))


def pad_edges(nc, S, K, M, src, dst, attr):
    EB, E = S.EB, S.E
    tail = EB * P - E
    with ExitStack() as ctx:
        sb, ps, sem = allocators(nc, ctx, "pad")
        nodes = sb("nodes", [1, 2, P + 1], I32)
        zeros = M.zeros
        here = sb("here", [P, EB], I32)
        ahead = sb("ahead", [P, EB], I32)
        falls = sb("falls", [P, EB])
        falls_p = sb("falls_p", [P, 1])
        sum_p = ps("sum", [1, 1])
        nodes_up, padded, loaded, falls_up, summed, linked = (sem(n) for n in (
            "nodes_up", "padded", "loaded", "falls_up", "summed", "dve_linked"))
        zeros_up = sem("zeros_up")
        block = phase_block(nc, ctx, sem)
        lines = 1600 if E % 1600 == 0 else 16

        @block.scalar
        def _(act):
            act.dma_start(M.attr[0:E, :].rearrange("(a b) f -> a (b f)", a=lines), attr.rearrange("(a b) f -> a (b f)", a=lines))\
                .then_inc(M.attr_up, 16)
            act.wait_ge(zeros_up, 1)
            act.dma_start(M.attr[E:EB * P, :], zeros[:, :]).then_inc(M.attr_up, 16)

        @block.sync
        def _(sp):
            for out, edges in ((M.dst_all, dst), (M.src_e, src)):
                sp.dma_start(out[0:E].rearrange("(a b) -> a b", a=16), edges.rearrange("(a b) -> a b", a=16)).then_inc(padded, 16)
            sp.wait_ge(nodes_up, 2)
            sp.dma_start(M.dst_all[E:EB * P + 1].rearrange("(a b) -> a b", a=1), nodes[:, 0, 0:tail + 1]).then_inc(padded, 16)
            sp.dma_start(M.src_e[E:EB * P].rearrange("(a b) -> a b", a=1), nodes[:, 1, 0:tail]).then_inc(padded, 16)
            sp.wait_ge(padded, 64)
            sp.dma_start(here[:, :], M.dst_all[0:EB * P].rearrange("(p c) -> p c", p=P)).then_inc(loaded, 16)
            sp.dma_start(ahead[:, :], M.dst_all[1:EB * P + 1].rearrange("(p c) -> p c", p=P)).then_inc(loaded, 16)

        @block.gpsimd
        def _(pool):
            pool.memset(nodes[:, 0, :], S.NT * P - 1).then_inc(nodes_up, 1)
            pool.memset(nodes[:, 1, :], 0).then_inc(nodes_up, 1)

        @block.tensor
        def _(pe):
            pe.wait_ge(falls_up, 1)
            pe.matmul(sum_p[:, :], falls_p[:, :], K.every[:, 0:1], start=True, stop=True).then_inc(summed, 1)

        @block.vector
        def _(dve):
            link = Linked(dve, linked)
            dve.memset(zeros[:, :], 0.0).then_inc(zeros_up, 1)
            dve.wait_ge(loaded, 32)
            link.run(dve.tensor_tensor(falls[:, :], ahead[:, :], here[:, :], ALU.is_lt))
            dve.tensor_reduce(falls_p[:, :], falls[:, :], AX.X, ALU.max).then_inc(falls_up, 1)
            dve.wait_ge(summed, 1)
            dve.tensor_copy(K.unsorted[:, :], sum_p[:, :])


def sort_edges(nc, S, K, M, attr):
    EB, E = S.EB, S.E
    with ExitStack() as ctx:
        sb, ps, sem = allocators(nc, ctx, "sort")
        record = sb("record", [P, EB, 4], I32)
        dst_s = sb("dst", [P, EB], I32)
        src_s = sb("src", [P, EB], I32)
        number = sb("number", [P, EB], I32)
        digit = sb("digit", [P, EB])
        digit_i = sb("digit_i", [P, EB], I32)
        counts = sb("counts", [P, P])
        total = sb("total", [P, P])
        upto = sb("upto", [P, P])
        base = sb("base", [P, P])
        hot = sb("hot", [P, P])
        place = sb("place", [P, P])
        own = sb("own", [P, P])
        place_f = sb("place_f", [P, 1])
        place_i = sb("place_i", [P, 1], I32)
        sent = sb("sent", [P, 4], I32)
        before = sb("before", [P, P])
        which = sb("which", [P, 1], I32)
        moved = sb("moved", [P, NR])
        total_p, before_p, chunk_p = (ps(n, [P, P]) for n in ("total_p", "before_p", "chunk_p"))
        numbered, loaded, split, resorted, stored, which_free, which_up, moved_up, attr_stored, linked = (sem(n) for n in (
            "numbered", "loaded", "split", "resorted", "stored", "which_free", "which_up", "moved_up", "attr_stored", "dve_linked"))
        gathered = sem.lasting("gathered")
        counts_up, totals_in, hot_up, ranked, sent_up, sent_free, count_linked, rank_linked = (
            [sem(f"{n}{d}") for d in range(2)] for n in (
                "counts_up", "totals_in", "hot_up", "ranked", "sent_up", "sent_free", "count_linked", "rank_linked"))
        scattered = [sem.lasting(f"scattered{d}") for d in range(2)]
        passed = sem("passed")
        block = phase_block(nc, ctx, sem)

        def where_unsorted(eng, name, body):
            falls = eng.alloc_register(f"{name}_falls")
            eng.load([falls], K.unsorted[0:1, 0:1])
            with eng.If_ne(falls, 0):
                body()
            eng.sem_inc(passed, 1)

        @block.sync
        def _(sp):
            def body():
                line = lambda t: t.rearrange("(p c) -> p c", p=P)
                sp.dma_start(dst_s[:, :], line(M.dst_e)).then_inc(loaded, 16)
                sp.dma_start(src_s[:, :], line(M.src_e)).then_inc(loaded, 16)
                sp.wait_ge(scattered[0], 16 * EB)
                sp.dma_start(record[:, :, :], M.record[0].rearrange("(c p) f -> p c f", p=P)).then_inc(loaded, 16)
                sp.wait_ge(scattered[1], 16 * EB)
                sp.dma_start(record[:, :, :], M.record[1].rearrange("(p c) f -> p c f", p=P)).then_inc(loaded, 16)
                sp.wait_ge(resorted, 1)
                sp.dma_start(line(M.dst_e), dst_s[:, :]).then_inc(stored, 16)
                sp.dma_start(line(M.src_e), src_s[:, :]).then_inc(stored, 16)
                sp.wait_ge(stored, 32)
                sp.wait_ge(M.attr_up, 32)
                rows = M.attr.rearrange("(p c) f -> p c f", p=P)
                with sp.Fori(0, EB) as c:
                    sp.wait_ge(moved_up, c + 1)
                    sp.dma_start(rows[:, bass.ds(c, 1), :], moved[:, :].unsqueeze(1)).then_inc(attr_stored, 16)
                    sp.wait_ge(attr_stored, c * 16 + 16)
                    sp.sem_inc(which_free, 1)
            where_unsorted(sp, "sp", body)

        @block.gpsimd
        def _(pool):
            def body():
                pool.iota(number[:, :], [[1, EB]], base=0, channel_multiplier=EB).then_inc(numbered, 1)
                for d in range(2):
                    with pool.Fori(0, EB) as c:
                        hold(pool, sent_up[d], c + 1, passed)
                        pool.indirect_dma_start(M.record[d], bass.IndirectOffsetOnAxis(place_i[:, :], 0), sent[:, :], None)\
                            .then_inc(scattered[d], 16)
                        pool.wait_ge(scattered[d], c * 16 + 16)
                        pool.sem_inc(sent_free[d], 1)
                with pool.Fori(0, EB) as c:
                    hold(pool, which_up, c + 1, passed)
                    pool.indirect_dma_start(moved[:, :], None, attr, bass.IndirectOffsetOnAxis(which[:, :], 0)).then_inc(gathered, 16)
                    pool.wait_ge(gathered, c * 16 + 16)
                    pool.sem_inc(moved_up, 1)
            where_unsorted(pool, "pool", body)

        @block.tensor
        def _(pe):
            def body():
                for d in range(2):
                    pe.wait_ge(counts_up[d], 1)
                    pe.matmul(total_p[:, :], K.every[:, :], counts[:, :], start=True, stop=True).then_inc(totals_in[d], 1)
                    with pe.Fori(0, EB) as c:
                        pe.wait_ge(hot_up[d], c + 1)
                        pe.matmul(before_p[:, :], before[:, :], hot[:, :], start=True, stop=True)
                        pe.matmul(chunk_p[:, :], K.every[:, :], hot[:, :], start=True, stop=True).then_inc(ranked[d], 1)
            where_unsorted(pe, "pe", body)

        @block.vector
        def _(dve):
            def body():
                link = Linked(dve, linked)
                link.run(dve.tensor_scalar(before[:, :], K.col[:, :], K.row[:, 0:1], None, ALU.is_gt))
                dve.wait_ge(loaded, 32)
                dve.wait_ge(numbered, 1)
                dve.tensor_copy(record[:, :, 0], dst_s[:, :])
                dve.tensor_copy(record[:, :, 1], src_s[:, :])
                dve.tensor_copy(record[:, :, 2], number[:, :])
                link.run(dve.tensor_copy(record[:, :, 3], number[:, :]))
                for d in range(2):
                    if d:
                        dve.wait_ge(loaded, 48)
                        link.run(dve.tensor_scalar(digit_i[:, :], record[:, :, 0], P.bit_length() - 1, None, ALU.logical_shift_right))
                    else:
                        link.run(dve.tensor_scalar(digit_i[:, :], record[:, :, 0], P - 1, None, ALU.bitwise_and))
                    link.run(dve.tensor_copy(digit[:, :], digit_i[:, :]))
                    link.run(dve.memset(counts[:, :], 0.0))
                    with dve.Fori(0, EB) as c:
                        each = LoopLinked(dve, count_linked[d], c, 1)
                        each.run(dve.scalar_tensor_tensor(counts[:, :], K.col[:, :], digit[:, bass.ds(c, 1)], counts[:, :],
                                                          ALU.is_equal, ALU.add))
                    dve.sem_inc(counts_up[d], 1)
                    dve.wait_ge(totals_in[d], 1)
                    link.run(dve.tensor_copy(total[:, :], total_p[:, :]))
                    link.run(dve.tensor_tensor_scan(upto[:, :], K.every[:, :], total[:, :], 0.0, ALU.mult, ALU.add))
                    link.run(dve.tensor_tensor(base[:, :], upto[:, :], total[:, :], ALU.subtract))
                    dve.sem_inc(sent_free[d], 1)
                    with dve.Fori(0, EB) as c:
                        each = LoopLinked(dve, rank_linked[d], c, 4)
                        dve.tensor_scalar(hot[:, :], K.col[:, :], digit[:, bass.ds(c, 1)], None, ALU.is_equal).then_inc(hot_up[d], 1)
                        dve.wait_ge(ranked[d], c + 1)
                        each.run(dve.tensor_tensor(place[:, :], before_p[:, :], base[:, :], ALU.add))
                        each.run(dve.tensor_tensor(own[:, :], place[:, :], hot[:, :], ALU.mult))
                        each.run(dve.tensor_reduce(place_f[:, :], own[:, :], AX.X, ALU.add))
                        each.run(dve.tensor_tensor(base[:, :], base[:, :], chunk_p[:, :], ALU.add))
                        dve.wait_ge(sent_free[d], c + 1)
                        dve.tensor_copy(sent[:, :].unsqueeze(1), record[:, bass.ds(c, 1), :])
                        dve.tensor_copy(place_i[:, :], place_f[:, :]).then_inc(sent_up[d], 1)
                dve.wait_ge(loaded, 64)
                dve.tensor_copy(dst_s[:, :], record[:, :, 0])
                dve.tensor_copy(src_s[:, :], record[:, :, 1]).then_inc(resorted, 1)
                link.run(dve.tensor_scalar(number[:, :], record[:, :, 2], E - 1, None, ALU.min))
                dve.sem_inc(which_free, 1)
                with dve.Fori(0, EB) as c:
                    dve.wait_ge(which_free, c + 1)
                    dve.tensor_copy(which[:, :], number[:, bass.ds(c, 1)]).then_inc(which_up, 1)
            where_unsorted(dve, "dve", body)


def visit_tables(nc, S, K, M):
    EB, V, NC, NT, E = S.EB, S.V, S.NC, S.NT, S.E
    W = EB + 1
    CH = 512
    with ExitStack() as ctx:
        sb, ps, sem = allocators(nc, ctx, "visits")
        ends = sb("ends", [1, 2, EB], I32)
        tiles = sb("tiles", [1, 2, EB])
        until = sb("until", [1, W])
        skip = sb("skip", [1, W])
        one = sb("one", [1, W])
        until_b = sb("until_b", [P, W])
        skip_b = sb("skip_b", [P, W])
        ones_b = sb("ones_b", [P, W])
        junk = sb("junk", [P, W])
        number = sb("number", [P, NC])
        count = sb("count", [P, NC])
        tile_v = sb("tile_v", [P, NC])
        tile_c = sb("tile_c", [P, NC])
        tile_m = sb("tile_m", [P, NC])
        tile_i = sb("tile_i", [P, NC], I32)
        block_f = sb("block_f", [P, NC])
        block_i = sb("block_i", [P, NC], I32)
        rows_d = sb("rows_d", [P, NC, P], I32)
        rows_s = sb("rows_s", [P, NC, P], I32)
        dst_f = sb("dst_f", [P, NC, P])
        src_f = sb("src_f", [P, NC, P])
        prev_f = sb("prev_f", [P, NC, P])
        local = sb("local", [P, NC, P])
        local_h = sb("local_h", [P, NC, P], BF16)
        same = sb("same", [P, NC, P])
        same0 = sb("same0", [P, NC])
        whole = sb("whole", [P, NC])
        alike = sb("alike", [P, NC])
        local_t = sb("local_t", [P, V])
        src_t = sb("src_t", [P, V], I32)
        bcast = ps("bcast", [P, 2, CH])
        turned = ps("turned", [P, 2, 512])
        got = sem.lasting("rows_got")
        (numbered, loaded, linked, rows_up, broad, lists, local_up, turned_up, kept, prevs,
         stored, cols, edges_in) = (sem(n) for n in (
             "numbered", "ends_loaded", "dve_linked", "rows_up", "broad", "lists", "local_up",
             "turned_up", "turned_kept", "prevs", "stored", "tables_up", "broad_up"))
        chunks = [(a, min(CH, W - a)) for a in range(0, W, CH)]
        turns = [(which, c, min(4, NC - c)) for which in range(2) for c in range(0, NC, 4)]
        block = phase_block(nc, ctx, sem)

        @block.sync
        def _(sp):
            blocks = M.dst_e.rearrange("(o b e) -> o b e", e=P, o=1)
            sp.dma_start(ends[:, 0, :].unsqueeze(2), blocks[:, :, 0:1], allow_slow_non_contiguous=True).then_inc(loaded, 16)
            sp.dma_start(ends[:, 1, :].unsqueeze(2), blocks[:, :, P - 1:P], allow_slow_non_contiguous=True).then_inc(loaded, 16)
            sp.wait_ge(local_up, 1)
            sp.dma_start(M.dst_v[1:1 + V * P].rearrange("(c p e) -> p c e", p=P, e=P), dst_f[:, :, :]).then_inc(stored, 16)
            sp.wait_ge(lists, 1)
            sp.dma_start(M.dst_v[0:1].rearrange("(a b) -> a b", a=1), until[0:1, 0:1]).then_inc(stored, 16)
            sp.wait_ge(stored, 32)
            sp.dma_start(prev_f[:, :, :], M.dst_v[0:V * P].rearrange("(c p e) -> p c e", p=P, e=P)).then_inc(prevs, 16)
            by_visit = lambda t: t.rearrange("(c p o) -> p c o", p=P, o=1)
            sp.wait_ge(lists, 3)
            sp.dma_start(by_visit(M.tile), tile_i[:, :].unsqueeze(2), allow_slow_non_contiguous=True).then_inc(stored, 16)
            sp.dma_start(by_visit(M.block), block_i[:, :].unsqueeze(2), allow_slow_non_contiguous=True).then_inc(stored, 16)
            sp.wait_ge(local_up, 3)
            sp.dma_start(M.local_row.rearrange("(c p e) -> p c e", p=P, e=P), local_h[:, :, :]).then_inc(stored, 16)
            sp.wait_ge(kept, len(turns))
            sp.dma_start(M.local_col, local_t[:, :]).then_inc(stored, 16)
            sp.dma_start(M.src_col, src_t[:, :]).then_inc(stored, 16)
            sp.wait_ge(cols, 1)
            sp.dma_start(M.apart.rearrange("(c p e) -> p c e", p=P, e=P), same[:, :, :]).then_inc(stored, 16)
            sp.dma_start(by_visit(M.alike), alike[:, :].unsqueeze(2), allow_slow_non_contiguous=True).then_inc(stored, 16)
            sp.dma_start(by_visit(M.whole), whole[:, :].unsqueeze(2), allow_slow_non_contiguous=True).then_inc(stored, 16)
            sp.dma_start(by_visit(M.goes_on), same0[:, :].unsqueeze(2), allow_slow_non_contiguous=True).then_inc(stored, 16)
            sp.wait_ge(stored, 32 + 9 * 16)

        @block.tensor
        def _(pe):
            pe.wait_ge(rows_up, 1)
            for n, (a, w) in enumerate(chunks * 2):
                row = until if n < len(chunks) else skip
                if n >= 2:
                    pe.wait_ge(broad, n - 1)
                pe.matmul(bcast[:, n % 2, 0:w], K.ones[0:1, :], row[0:1, a:a + w], start=True, stop=True).then_inc(edges_in, 1)
            pe.wait_ge(local_up, 3)
            for n, (which, c, w) in enumerate(turns):
                if n >= 2:
                    pe.wait_ge(kept, n - 1)
                for k in range(w):
                    mm = pe.transpose(turned[:, n % 2, k * P:k * P + P], (src_f if which else local)[:, c + k, :], K.ident[:, :])
                mm.then_inc(turned_up, 1)

        @block.gpsimd
        def _(pool):
            pool.iota(rows_d[:, 0, 0:NC], [[P, NC]], base=0, channel_multiplier=1).then_inc(numbered, 1)
            pool.wait_ge(lists, 3)
            for table, rows in ((M.dst_e, rows_d), (M.src_e, rows_s)):
                for c in range(NC):
                    pool.indirect_dma_start(rows[:, c, :], None, table.rearrange("(b e) -> b e", e=P),
                                            bass.IndirectOffsetOnAxis(block_i[:, c:c + 1], 0)).then_inc(got, 16)

        @block.scalar
        def _(act):
            for n, (which, c, w) in enumerate(turns):
                act.wait_ge(turned_up, n + 1)
                out = (src_t if which else local_t)[:, c * P:(c + w) * P]
                act.activation(out, turned[:, n % 2, 0:w * P], ACT.Copy).then_inc(kept, 1)

        @block.vector
        def _(dve):
            link = Linked(dve, linked)
            dve.wait_ge(numbered, 1)
            link.run(dve.tensor_copy(number[:, :], rows_d[:, 0, 0:NC]))
            link.run(dve.memset(ones_b[:, :], 1.0))
            link.run(dve.memset(one[:, :], 1.0))
            dve.wait_ge(loaded, 32)
            link.run(dve.tensor_scalar(ends[:, :, :], ends[:, :, :], P.bit_length() - 1, None, ALU.logical_shift_right))
            link.run(dve.tensor_copy(tiles[:, :, :], ends[:, :, :]))
            link.run(dve.memset(until[:, :], -1.0))
            link.run(dve.memset(skip[:, :], 0.0))
            link.run(dve.scalar_tensor_tensor(junk[0:1, 0:EB], tiles[:, 1, :], 1.0, tiles[:, 0, :], ALU.add, ALU.subtract))
            link.run(dve.tensor_tensor_scan(until[:, 1:W], one[:, 1:W], junk[0:1, 0:EB], 0.0, ALU.mult, ALU.add))
            link.run(dve.tensor_copy(skip[:, 0:1], tiles[:, 0, 0:1]))
            if EB > 1:
                link.run(dve.scalar_tensor_tensor(skip[:, 1:EB], tiles[:, 0, 1:EB], -1.0, tiles[:, 1, 0:EB - 1],
                                                  ALU.add, ALU.subtract))
            dve.sem_inc(rows_up, 1)
            for n, (a, w) in enumerate(chunks * 2):
                dve.wait_ge(edges_in, n + 1)
                out = until_b if n < len(chunks) else skip_b
                dve.tensor_copy(out[:, a:a + w], bcast[:, n % 2, 0:w]).then_inc(broad, 1)
            dve.wait_ge(broad, 2 * len(chunks))
            dve.sem_inc(lists, 1)
            for c in range(NC):
                link.run(dve.scalar_tensor_tensor(junk[:, :], until_b[:, :], number[:, c:c + 1], ones_b[:, :],
                                                  ALU.is_le, ALU.mult, accum_out=count[:, c:c + 1]))
                link.run(dve.scalar_tensor_tensor(junk[:, :], until_b[:, :], number[:, c:c + 1], skip_b[:, :],
                                                  ALU.is_le, ALU.mult, accum_out=tile_v[:, c:c + 1]))
            link.run(dve.tensor_scalar(block_f[:, :], count[:, :], -1.0, EB - 1.0, ALU.add, ALU.min))
            dve.tensor_copy(block_i[:, :], block_f[:, :]).then_inc(lists, 1)
            link.run(dve.tensor_tensor(tile_v[:, :], tile_v[:, :], number[:, :], ALU.add))
            link.run(dve.tensor_scalar(tile_c[:, :], tile_v[:, :], NT - 1.0, None, ALU.min))
            link.run(dve.tensor_scalar(tile_m[:, :], tile_v[:, :], -float(P), None, ALU.mult))
            dve.tensor_copy(tile_i[:, :], tile_c[:, :]).then_inc(lists, 1)
            dve.wait_ge(got, 2 * NC * 16)
            dve.tensor_copy(dst_f[:, :, :], rows_d[:, :, :]).then_inc(local_up, 1)
            link.run(dve.tensor_copy(src_f[:, :, :], rows_s[:, :, :]))
            dve.wait_ge(local_up, 1)
            link.run(dve.tensor_tensor(local[:, :, :], dst_f[:, :, :], tile_m[:, :].unsqueeze(2).broadcast_to([P, NC, P]), ALU.add))
            dve.tensor_copy(local_h[:, :, :], local[:, :, :]).then_inc(local_up, 2)
            dve.wait_ge(prevs, 16)
            link.run(dve.tensor_tensor(same[:, :, :], dst_f[:, :, :], prev_f[:, :, :], ALU.is_equal))
            link.run(dve.tensor_copy(same0[:, :], same[:, :, 0]))
            link.run(dve.tensor_scalar(same[:, :, :], same[:, :, :], -1.0, BIG, ALU.add, ALU.mult))
            dve.tensor_reduce(alike[:, :], same[:, :, 1:P], AX.X, ALU.min)
            dve.tensor_reduce(whole[:, :], same[:, :, :], AX.X, ALU.min).then_inc(cols, 1)


def attention_weights(nc, K, M, W_dram, al, ar, Waug, layer):
    with ExitStack() as ctx:
        sb, ps, sem = allocators(nc, ctx, f"weights{layer}")
        w = sb("w", [P, 2, F])
        a = sb("a", [P, 2, F])
        prod = sb("prod", [P, 2, 2, F])
        loaded, linked = sem("w_loaded"), sem("dve_linked")
        block = phase_block(nc, ctx, sem)

        @block.sync
        def _(sp):
            sp.dma_start(w[:, :, :], W_dram.rearrange("(k p) f -> p k f", p=P)).then_inc(loaded, 16)
            for n, v in enumerate((al, ar)):
                row = v.rearrange("(o h) d -> o (h d)", o=1)
                sp.dma_start(a[:, n, :], row.broadcast_to([P, F])).then_inc(loaded, 16)

        @block.vector
        def _(dve):
            link = Linked(dve, linked)
            dve.wait_ge(loaded, 48)
            for k in range(2):
                row = Waug[:, k, 0:ROW].rearrange("p (h d) -> p h d", d=HW)
                dve.tensor_copy(row[:, :, 0:D], w[:, k, :].rearrange("p (h d) -> p h d", d=D))
                for n in range(2):
                    link.run(dve.tensor_tensor(prod[:, k, n, :], w[:, k, :], a[:, n, :], ALU.mult))
                    out = row[:, :, D] if n == 0 else Waug[:, k, ROW:ROW + H]
                    link.run(dve.tensor_reduce(out, prod[:, k, n, :].rearrange("p (h d) -> p h d", d=D), AX.X, ALU.add))


class Nodes:

    def __init__(self, S):
        self.S, self.turns = S, (S.NT - 2) // (2 * G4)

    def run(self, eng, group):
        with eng.Fori(0, self.turns) as j:
            for p in range(2):
                group(j * (2 * G4) + p * G4, j * 2 + p, p, G4, P)
        group(self.S.NT - 2, 2 * self.turns, 0, 2, self.S.LAST)


def hold(eng, sem, value, passed):
    eng.wait_ge(sem, value)
    eng.sem_inc(passed, 1)


def half(g, p):
    return g // 2 if isinstance(g, int) else (g - p) // 2


def tiles_of(table, tile, n):
    return table[bass.ds(tile * P, n * P), :].rearrange("(k p) f -> p k f", p=P)


def load_tiles(eng, buf, p, table, tile, n, rows, done):
    eng.dma_start(buf[:, p, 0:n - 1, :], tiles_of(table, tile, n - 1)).then_inc(done, 16)
    eng.dma_start(buf[0:rows, p, n - 1, :], table[bass.ds((tile + n - 1) * P, rows), :]).then_inc(done, 16)


def project_nodes(nc, S, K, M, first, x, Waug, er3, acc):
    NT = S.NT
    nodes = Nodes(S)
    with ExitStack() as ctx:
        sb, ps, sem = allocators(nc, ctx, "project1" if first else "project2")
        xin = sb("xin", [P, 2, G4, F]) if first else None
        stats = sb("stats", [P, 2, G4, nc.vector.BN_STATS_DIM])
        mv = sb("mv", [P, 2, G4, 2])
        den = sb("den", [P, 2, G4, H])
        dev = sb("dev", [P, 2, G4])
        scale = sb("scale", [P, 2, G4])
        shift = sb("shift", [P, 2, G4])
        low = sb("low", [P, 2, G4, F])
        h = sb("h", [P, 2, G4, F])
        hT = sb("hT", [P, 2, G4, F])
        row = sb("row", [P, 2, G4, ROW])
        er = sb("er", [P, NT, H])
        rest = sb("rest", [P, NT, H])
        psT = ps("psT", [P, 2, 512])
        psF = ps("psF", [P, G4, 512])
        (used, moments, devs, scales, h_up, low_up, exp_up, turned, hT_up, products, kept, out_free,
         linked, cleared) = (sem(n) for n in (
             "x_used", "moments", "devs", "scales", "h_up", "low_up", "exp_up", "turned", "hT_up",
             "products", "rows_kept", "out_free", "dve_linked", "cleared"))
        split, passed = sem("split"), sem("passed")
        loaded = [sem("loaded0"), sem("loaded1")]
        stored = [sem.lasting("stored0"), sem.lasting("stored1")]
        block = phase_block(nc, ctx, sem)

        @block.sync
        def _(sp):
            def group(tile, g, p, n, rows):
                sp.wait_ge(used, g + 1)
                if rows != P:
                    sp.wait_ge(cleared, 1)
                load_tiles(sp, xin, p, x, tile, n, rows, loaded[p])
            if first:
                nodes.run(sp, group)

        @block.gpsimd
        def _(pool):
            def group(tile, g, p, n, rows):
                pool.wait_ge(kept, tile + n + G4)
                pool.dma_start(tiles_of(M.table, tile, n), row[:, p, 0:n, :]).then_inc(stored[p], 16)
                if not first:
                    pool.dma_start(tiles_of(M.h2, tile, n), h[:, p, 0:n, :]).then_inc(stored[p], 16)
                each = 16 if first else 32
                pool.wait_ge(stored[p], half(g, p) * each + each)
                pool.sem_inc(out_free, 1)
            nodes.run(pool, group)

        @block.tensor
        def _(pe):
            def product(T, p, k):
                pe.wait_ge(hT_up, T + 3)
                pe.wait_ge(kept, T + 1)
                for c in range(2):
                    mm = pe.matmul(psF[:, k, 0:ROW + H], hT[:, p, k, c * P:c * P + P], Waug[:, c, :],
                                   start=(c == 0), stop=(c == 1))
                mm.then_inc(products, 1)

            def group(tile, g, p, n, rows):
                for k in range(n):
                    T = tile + k
                    pe.wait_ge(h_up, T + 1)
                    pe.wait_ge(hT_up, T + 1)
                    for c in range(2):
                        mm = pe.transpose(psT[:, k % 2, c * P:c * P + P], h[:, p, k, c * P:c * P + P], K.ident[:, :])
                    mm.then_inc(turned, 1)
                    if k:
                        product(T - 1, p, k - 1)
                product(tile + n - 1, p, n - 1)
            nodes.run(pe, group)

        @block.scalar
        def _(act):
            act.sem_inc(hT_up, 2)
            if first:
                act.sem_inc(used, 2)

            def group(tile, g, p, n, rows):
                if first:
                    act.wait_ge(moments, g + 1)
                    act.activation(dev[:, p, 0:n], mv[:, p, 0:n, 1], ACT.Sqrt, bias=K.eps[:, 0:1]).then_inc(devs, 1)
                    act.wait_ge(scales, g + 1)
                    act.wait_ge(out_free, g + 1)
                    for k in range(n):
                        act.activation(h[:, p, k, :], xin[:, p, k, :], ACT.Relu, bias=shift[:, p, k:k + 1],
                                       scale=scale[:, p, k:k + 1]).then_inc(h_up, 1)
                    act.wait_ge(h_up, tile + n)
                    act.sem_inc(used, 1)
                else:
                    for k in range(n):
                        act.wait_ge(low_up, tile + k + 1)
                        act.activation(low[:, p, k, :], low[:, p, k, :], ACT.Exp).then_inc(exp_up, 1)
                for k in range(n):
                    act.wait_ge(turned, tile + k + 1)
                    act.activation(hT[:, p, k, :], psT[:, k % 2, 0:F], ACT.Copy).then_inc(hT_up, 1)
            nodes.run(act, group)

        @block.vector
        def _(dve):
            dve.sem_inc(kept, G4)
            dve.sem_inc(out_free, 2)
            per = 2 if first else 4 * G4

            def group(tile, g, p, n, rows):
                link = LoopLinked(dve, linked, g, per)
                if first:
                    if rows != P:
                        dve.wait_ge(used, g + 1)
                        dve.memset(xin[:, p, n - 1, :], 0.0).then_inc(cleared, 1)
                    dve.wait_ge(loaded[p], half(g, p) * 32 + 32)
                    for k in range(n):
                        ins = dve.bn_stats(stats[:, p, k, :], xin[:, p, k, :])
                    link.run(ins)
                    dve.sem_inc(passed, 1)
                    for k in range(n):
                        ins = dve.bn_aggr(mv[:, p, k, :], stats[:, p, k, :])
                    ins.then_inc(moments, 1)
                    dve.wait_ge(devs, g + 1)
                    dve.wait_ge(moments, g + 1)
                    link.run(dve.reciprocal(scale[:, p, 0:n], dev[:, p, 0:n]))
                    dve.scalar_tensor_tensor(shift[:, p, 0:n], mv[:, p, 0:n, 0], -1.0, scale[:, p, 0:n], ALU.mult, ALU.mult)\
                        .then_inc(scales, 1)
                else:
                    dve.wait_ge(out_free, g + 1)
                    for k in range(n):
                        a = acc[:, bass.ds((tile + k) * ROW, ROW)].rearrange("p (h d) -> p h d", d=HW)
                        hk = h[:, p, k, :].rearrange("p (h d) -> p h d", d=D)
                        link.run(dve.tensor_scalar(den[:, p, k, :], a[:, :, D], 1e-30, None, ALU.max))
                        link.run(dve.reciprocal(den[:, p, k, :], den[:, p, k, :]))
                        link.run(dve.tensor_tensor(hk, a[:, :, 0:D], den[:, p, k, :].unsqueeze(2).broadcast_to([P, H, D]), ALU.mult))
                        dve.tensor_scalar(low[:, p, k, :], h[:, p, k, :], 0.0, None, ALU.min).then_inc(low_up, 1)
                        link.run(dve.tensor_scalar(h[:, p, k, :], h[:, p, k, :], 0.0, None, ALU.max))
                    for k in range(n):
                        dve.wait_ge(exp_up, tile + k + 1)
                        dve.scalar_tensor_tensor(h[:, p, k, :], low[:, p, k, :], -1.0, h[:, p, k, :], ALU.add, ALU.add)\
                            .then_inc(h_up, 1)
                if first:
                    dve.wait_ge(out_free, g + 1)
                for k in range(n):
                    dve.wait_ge(products, tile + k + 1)
                    dve.tensor_copy(er[:, bass.ds(tile + k, 1), :], psF[:, k, ROW:ROW + H].unsqueeze(1))
                    dve.tensor_copy(row[:, p, k, :], psF[:, k, 0:ROW]).then_inc(kept, 1)
            nodes.run(dve, group)
            dve.wait_ge(kept, NT + G4)
            link = Linked(dve, split)
            link.run(dve.tensor_copy(er3[:, :, 0, :], er[:, :, :]))
            link.run(dve.tensor_tensor(rest[:, :, :], er[:, :, :], er3[:, :, 0, :], ALU.subtract))
            link.run(dve.tensor_copy(er3[:, :, 1, :], rest[:, :, :]))
            link.run(dve.tensor_tensor(er3[:, :, 2, :], rest[:, :, :], er3[:, :, 1, :], ALU.subtract))


def attend(nc, S, K, M, er3, acc, layer):
    NI = S.NI
    TABLES = 9
    with ExitStack() as ctx:
        sb, ps, sem = allocators(nc, ctx, f"attend{layer}")
        G = sb("G", [P, 2, U, ROW])
        hot = sb("hot", [P, 2, U, P])
        hotT = sb("hotT", [P, U, P], BF16)
        index = sb("index", [P, 2, U], I32)
        local_b = sb("local_b", [P, 2, U * P], BF16)
        local_c = sb("local_c", [P, 2, U])
        apart = sb("apart", [R, 2, P + 1])
        whole = sb("whole", [H, 2, U])
        alike = sb("alike", [H, 2, U])
        goes_on = sb("goes_on", [H, 2, U + 1])
        tile_r = sb("tile_r", [1, S.V], I32)
        el = sb("el", [P, R])
        er = sb("er", [P, R])
        run = sb("run", [R, P])
        top = sb("top", [R, P])
        ends = sb("ends", [R, 2, U])
        last = sb("last", [H, 1])
        carry = sb("carry", [H, U + 1])
        back = sb("back", [H, U + 1])
        around = sb("around", [H, 2, U])
        through = sb("through", [H, 2, U])
        spread = sb("spread", [R, 2, U])
        start = sb("start", [R, 2])
        low = sb("low", [P, R])
        high = sb("high", [P, R])
        low2 = sb("low2", [P, R])
        high2 = sb("high2", [P, R])
        diff = sb("diff", [P, R])
        old = sb("old", [1, 3, H])
        shrink = sb("shrink", [1, 2 * H])
        first_n = sb("first_n", [P, 1])
        other = sb("other", [P, H])
        same = sb("same", [P, H])
        keep = sb("keep", [P, 2, H])
        psP = ps("psP", [P, BANKS, 512])
        psA = ps("psA", [P, 512])
        psE = ps("psE", [P, 512])
        psR = ps("psR", [P, 512])
        psS = ps("psS", [P, 512])
        elT, ends_p, start_p = psA[0:R, 0:P], psA[0:H, P:P + 2 * U], psA[0:R, 2 * P:2 * P + 2 * U]
        er_p = psE[:, 0:3 * R].rearrange("p (u k h) -> p k h u", k=3, h=H)
        top_p, old_p, keep_p = psR[:, 0:R], psR[0:1, P:P + R], psS[:, 0:2 * H]
        index_up, tables_up = ([sem(f"{n}{p}") for p in range(2)] for n in ("index_up", "tables_up"))
        gathered = [sem.lasting(f"gathered{p}") for p in range(2)]
        (tiles_up, el_up, hotT_up, hot_up, el_turned, er_up, ends_up, ends_in, around_up, start_in, top_up, top_turned,
         diff_up, weights_up, shrink_up, shrunk_up, keep_in, keep_up, weighed, summed, added, linked) = (sem(n) for n in (
             "tiles_up", "el_up", "hotT_up", "hot_up", "el_turned", "er_up", "ends_up", "ends_in", "around_up", "start_in",
             "top_up", "top_turned", "diff_up", "weights_up", "shrink_up", "shrunk_up", "keep_in", "keep_up", "weighed",
             "summed", "added", "dve_linked"))
        ready = sem("ready")
        passed_pe, passed_pool = sem("passed_pe"), sem("passed_pool")
        CREDIT = BANKS
        block = phase_block(nc, ctx, sem)

        def el_of(p):
            return G[:, p, :, :].rearrange("p u (h d) -> p h u d", d=HW)[:, :, :, D]

        @block.sync
        def _(sp):
            def tables(i, p):
                v = i * U
                sp.dma_start(index[:, p, :], M.src_col[:, bass.ds(v, U)]).then_inc(index_up[p], 16)
                row = M.local_row[bass.ds(v * P, U * P)].rearrange("(o n) -> o n", o=1)
                sp.dma_start(local_b[:, p, :], row.broadcast_to([P, U * P])).then_inc(tables_up[p], 16)
                sp.dma_start(local_c[:, p, :], M.local_col[:, bass.ds(v, U)]).then_inc(tables_up[p], 16)
                rows = M.apart[bass.ds(v * P, U * P)].rearrange("(u e) -> u e", e=P)
                for h in range(H):
                    sp.dma_start(apart[h * U:h * U + U, p, 0:P], rows).then_inc(tables_up[p], 16)
                for out, table, w in ((whole, M.whole, U), (alike, M.alike, U), (goes_on, M.goes_on, U + 1)):
                    line = table[bass.ds(v, w)].rearrange("(o n) -> o n", o=1)
                    sp.dma_start(out[:, p, :], line.broadcast_to([H, w])).then_inc(tables_up[p], 16)

            sp.dma_start(tile_r[:, :], M.tile.rearrange("(o n) -> o n", o=1)).then_inc(tiles_up, 16)
            tables(0, 0)
            tables(1, 1)
            with sp.Fori(0, NI // 2) as j:
                for p in range(2):
                    i = j * 2 + p
                    sp.wait_ge(gathered[p], j * (16 * U) + 16 * U)
                    sp.wait_ge(shrunk_up, i + 1)
                    sp.wait_ge(hot_up, 2 * i + 2)
                    tables(i + 2, p)
            sp.wait_ge(tiles_up, 16)
            for p in range(2):
                sp.wait_ge(tables_up[p], (NI // 2 + 1) * 16 * TABLES)
                sp.wait_ge(index_up[p], (NI // 2 + 1) * 16)

        @block.gpsimd
        def _(pool):
            def gather(j, p, before=None):
                hold(pool, index_up[p], j * 16 + 16, passed_pool)
                for u in range(U):
                    if before is not None and u % 2 == 0:
                        hold(pool, summed, before * U + u + 2, passed_pool)
                    pool.indirect_dma_start(G[:, p, u, :], None, M.table, bass.IndirectOffsetOnAxis(index[:, p, u:u + 1], 0))\
                        .then_inc(gathered[p], 16)
            gather(0, 0)
            gather(0, 1)
            with pool.Fori(0, NI // 2) as j:
                for p in range(2):
                    gather(j + 1, p, j * 2 + p)
            for p in range(2):
                pool.wait_ge(gathered[p], (NI // 2 + 1) * 16 * U)

        @block.tensor
        def _(pe):
            regs = [pe.alloc_register(f"pe{layer}_tile{u}") for u in range(U)]
            parts = er3.rearrange("p t k h -> p (t k h)")

            def prepare(i, p):
                pe.load(regs, tile_r[0:1, bass.ds(i * U, U)])
                hold(pe, el_up, i + 1, passed_pe)
                pe.transpose(elT, el[:, :], K.ident[:, :]).then_inc(el_turned, 1)
                yield
                pe.wait_ge(hotT_up, i + 1)
                for u in range(U):
                    t = pe.snap(regs[u], min_val=0, max_val=S.NT - 1)
                    mm = pe.matmul(psE[:, u * 3 * H:u * 3 * H + 3 * H], hotT[:, u, :], parts[:, bass.ds(t * (3 * H), 3 * H)],
                                   start=True, stop=True)
                mm.then_inc(er_up, 1)
                yield
                hold(pe, ends_up, i + 1, passed_pe)
                pe.matmul(ends_p, K.head_of[:, :], ends[:, :, :], start=True, stop=True).then_inc(ends_in, 1)
                yield
                hold(pe, around_up, i + 1, passed_pe)
                pe.matmul(start_p, K.rows_of[:, :], around[:, :, :], start=True, stop=True).then_inc(start_in, 1)
                yield
                hold(pe, top_up, i + 1, passed_pe)
                pe.transpose(top_p, top[:, :], K.ident[0:R, 0:R])
                pe.transpose(old_p, start[:, 0:1], K.ident[0:R, 0:R]).then_inc(top_turned, 1)
                yield
                hold(pe, shrunk_up, i + 1, passed_pe)
                pe.matmul(keep_p, K.ones[:, :], shrink[:, :], start=True, stop=True).then_inc(keep_in, 1)
                yield

            def sums(i, p, u):
                pe.wait_ge(weighed, i * U + u + 1)
                pe.wait_ge(added, i * U + u + 1)
                pe.matmul(psP[:, u % BANKS, 0:ROW], hot[:, p, u, :], G[:, p, u, :], start=True, stop=True).then_inc(summed, 1)

            pe.wait_ge(tiles_up, 16)
            pe.wait_ge(ready, 1)
            for _ in prepare(0, 0):
                pass
            after = {5, 6, 7, 8, 9, 15}
            with pe.Fori(0, NI // 2) as j:
                for p in range(2):
                    i = j * 2 + p
                    steps = prepare(i + 1, 1 - p)
                    pe.wait_ge(hot_up, 2 * i + 2)
                    for u in range(U):
                        sums(i, p, u)
                        if u in after:
                            next(steps, None)
                    for _ in steps:
                        pass

        @block.scalar
        def _(act):
            def weights(i, p):
                act.wait_ge(diff_up, i + 1)
                act.activation(shrink[:, 0:H], old[:, 2, :], ACT.Exp).then_inc(shrink_up, 1)
                act.activation(el_of(p), diff[:, :].rearrange("p (h u) -> p h u", h=H), ACT.Exp).then_inc(weights_up, 1)

            weights(0, 0)
            with act.Fori(0, NI // 2) as j:
                for p in range(2):
                    i = j * 2 + p
                    act.wait_ge(weights_up, i + 1)
                    for u in range(U):
                        for h in range(H):
                            row = G[:, p, u, h * HW:h * HW + D]
                            ins = act.activation(row, row, ACT.Copy, scale=G[:, p, u, h * HW + D:h * HW + HW])
                        ins.then_inc(weighed, 1)
                        if u == 14:
                            weights(i + 1, 1 - p)

        @block.vector
        def _(dve):
            regs = [dve.alloc_register(f"dve{layer}_tile{u}") for u in range(U)]
            LINKS = 16

            def prepare(i, p, j):
                link = LoopLinked(dve, linked, i, LINKS)
                by_head = lambda t: t.rearrange("p (h u) -> p h u", h=H)
                dve.wait_ge(tables_up[p], j * (16 * TABLES) + 16 * TABLES)
                dve.tensor_scalar(hotT[:, :, :].rearrange("p u e -> p (u e)"), local_b[:, p, :], K.row[:, 0:1], None, ALU.is_equal)\
                    .then_inc(hotT_up, 1)
                link.run(dve.tensor_scalar(through[:, 0, :], goes_on[:, p, 1:U + 1], -1.0, BIG, ALU.add, ALU.mult))
                dve.tensor_tensor(through[:, 1, :], through[:, 0, :], alike[:, p, :], ALU.add)
                yield
                dve.wait_ge(gathered[p], j * (16 * U) + 16 * U)
                dve.tensor_copy(by_head(el[:, :]), el_of(p)).then_inc(el_up, 1)
                yield
                dve.wait_ge(el_turned, i + 1)
                link.run(dve.tensor_tensor_scan(run[:, :], apart[:, p, 0:P], elT, -BIG, ALU.add, ALU.max))
                link.run(dve.tensor_tensor_scan(top[:, ::-1], apart[:, p, P:0:-1], run[:, ::-1], -BIG, ALU.add, ALU.max))
                dve.tensor_scalar(ends[:, 0, :], K.visit_of[:, :], run[:, P - 1:P], None, ALU.mult)
                dve.tensor_scalar(ends[:, 1, :], K.visit_of[:, :], top[:, 0:1], None, ALU.mult).then_inc(ends_up, 1)
                yield
                dve.wait_ge(ends_in, i + 1)
                link.run(dve.tensor_copy(last[:, :], carry[:, U:U + 1]))
                dve.tensor_copy(carry[:, 0:1], last[:, :])
                dve.tensor_tensor_scan(carry[:, 1:U + 1], whole[:, p, :], ends_p[:, 0:U], last[:, 0:1], ALU.add, ALU.max)
                link.run(dve.tensor_tensor_scan(back[:, U - 1::-1], through[:, 1, ::-1], ends_p[:, 2 * U - 1:U - 1:-1], -BIG, ALU.add, ALU.max))
                dve.tensor_copy(around[:, 0, :], carry[:, 0:U])
                dve.tensor_tensor(around[:, 1, :], through[:, 0, :], back[:, 1:U + 1], ALU.add).then_inc(around_up, 1)
                yield
                dve.wait_ge(er_up, i + 1)
                link.run(dve.tensor_reduce(by_head(er[:, :]), er_p.rearrange("p k h u -> p h u k"), AX.X, ALU.add))
                link.run(dve.tensor_tensor(low[:, :], el[:, :], er[:, :], ALU.add))
                dve.scalar_tensor_tensor(low2[:, :], low[:, :], SLOPE, low[:, :], ALU.mult, ALU.max)
                yield
                dve.wait_ge(start_in, i + 1)
                link.run(dve.tensor_tensor(spread[:, :, :], start_p.rearrange("r (k u) -> r k u", k=2),
                                           K.visit_of[:, :].unsqueeze(1).broadcast_to([R, 2, U]), ALU.mult))
                link.run(dve.tensor_reduce(start[:, :], spread[:, :, :], AX.X, ALU.add))
                link.run(dve.tensor_tensor_scan(run[:, :], apart[:, p, 0:P], elT, start[:, 0:1], ALU.add, ALU.max))
                dve.tensor_tensor_scan(top[:, ::-1], apart[:, p, P:0:-1], run[:, ::-1], start[:, 1:2], ALU.add, ALU.max).then_inc(top_up, 1)
                yield
                dve.wait_ge(top_turned, i + 1)
                link.run(dve.tensor_tensor(high[:, :], top_p, er[:, :], ALU.add))
                dve.tensor_tensor(old[:, 0, :], by_head(old_p)[:, :, 0], by_head(er[0:1, :])[:, :, 0], ALU.add)
                link.run(dve.scalar_tensor_tensor(high2[:, :], high[:, :], SLOPE, high[:, :], ALU.mult, ALU.max))
                link.run(dve.scalar_tensor_tensor(old[:, 1, :], old[:, 0, :], SLOPE, old[:, 0, :], ALU.mult, ALU.max))
                link.run(dve.tensor_tensor(old[:, 2, :], old[:, 1, :], by_head(high2[0:1, :])[:, :, 0], ALU.subtract))
                dve.tensor_scalar(old[:, 2, :], old[:, 2, :], 0.0, None, ALU.min)
                dve.tensor_tensor(diff[:, :], low2[:, :], high2[:, :], ALU.subtract).then_inc(diff_up, 1)
                yield
                for n in range(2):
                    half_of = slice(n * (U // 2), (n + 1) * (U // 2))
                    dve.tensor_tensor(hot[:, p, half_of, :], K.col[:, :].unsqueeze(1).broadcast_to([P, U // 2, P]),
                                      local_c[:, p, half_of].unsqueeze(2).broadcast_to([P, U // 2, P]), ALU.is_equal).then_inc(hot_up, 1)
                    yield
                dve.wait_ge(shrink_up, i + 1)
                dve.tensor_copy(shrink[:, H:2 * H], goes_on[0:1, p, 0:1].broadcast_to([1, H]))
                dve.tensor_scalar(shrink[:, 0:H], shrink[:, 0:H], goes_on[0:1, p, 0:1], None, ALU.mult).then_inc(shrunk_up, 1)
                yield
                link.run(dve.tensor_copy(first_n[:, :], hotT[:, 0, 0:1]))
                dve.wait_ge(keep_in, i + 1)
                dve.tensor_scalar(other[:, :], keep_p[:, H:2 * H], first_n[:, 0:1], -1.0, ALU.mult, ALU.mult)
                link.run(dve.tensor_scalar(same[:, :], keep_p[:, 0:H], first_n[:, 0:1], None, ALU.mult))
                dve.scalar_tensor_tensor(keep[:, p, :], other[:, :], 1.0, same[:, :], ALU.add, ALU.add).then_inc(keep_up, 1)
                assert link.n == LINKS, link.n
                yield

            def add(i, p, u):
                t = dve.snap(regs[u], min_val=0, max_val=S.NT - 1)
                if u == 0:
                    dve.wait_ge(keep_up, i + 1)
                dve.wait_ge(summed, i * U + u + 1)
                dve.wait_ge(added, i * U + (u + CREDIT))
                if u == 0:
                    for h in range(H):
                        s = acc[:, bass.ds(t * ROW + h * HW, HW)]
                        ins = dve.scalar_tensor_tensor(s, s, keep[:, p, h:h + 1], psP[:, u % BANKS, h * HW:h * HW + HW],
                                                       ALU.mult, ALU.add)
                else:
                    s = acc[:, bass.ds(t * ROW, ROW)]
                    ins = dve.tensor_tensor(s, s, psP[:, u % BANKS, 0:ROW], ALU.add)
                ins.then_inc(added, 1)

            dve.memset(apart[:, :, P:P + 1], 0.0)
            dve.memset(back[:, :], -BIG)
            dve.memset(carry[:, :], -BIG).then_inc(ready, 1)
            dve.wait_ge(ready, 1)
            dve.memset(acc[:, :], 0.0).then_inc(added, CREDIT)
            dve.wait_ge(tiles_up, 16)
            for _ in prepare(0, 0, 0):
                pass
            after = {0, 2, 4, 5, 6, 7, 8, 10, 12, 13, 14}
            with dve.Fori(0, NI // 2) as j:
                for p in range(2):
                    i = j * 2 + p
                    steps = prepare(i + 1, 1 - p, j + p)
                    dve.load(regs, tile_r[0:1, bass.ds(i * U, U)])
                    for u in range(U):
                        add(i, p, u)
                        if u in after:
                            next(steps, None)
                    for _ in steps:
                        pass
            dve.wait_ge(added, NI * U + CREDIT)


def renew_nodes(nc, S, K, M, x, acc):
    nodes = Nodes(S)
    with ExitStack() as ctx:
        sb, ps, sem = allocators(nc, ctx, "renew")
        xin = sb("xin", [P, 2, G4, F])
        hin = sb("hin", [P, 2, G4, F])
        r = sb("r", [P, 2, G4, F])
        low = sb("low", [P, 2, G4, F])
        h = sb("h", [P, 2, G4, F])
        xh = sb("xh", [P, 2, G4, F])
        stats = sb("stats", [P, 2, G4, nc.vector.BN_STATS_DIM])
        mv = sb("mv", [P, 2, G4, 2])
        den = sb("den", [P, 2, G4, H])
        dev = sb("dev", [P, 2, G4])
        scale = sb("scale", [P, 2, G4])
        shift = sb("shift", [P, 2, G4])
        used, moments, devs, scales, h_up, low_up, exp_up, xh_up, out_free, linked, cleared = (sem(n) for n in (
            "inputs_used", "moments", "devs", "scales", "h_up", "low_up", "exp_up", "xh_up", "out_free", "dve_linked", "cleared"))
        passed = sem("passed")
        loaded = [sem("loaded0"), sem("loaded1")]
        stored = [sem.lasting("stored0"), sem.lasting("stored1")]
        block = phase_block(nc, ctx, sem)

        @block.sync
        def _(sp):
            def group(tile, g, p, n, rows):
                sp.wait_ge(used, g + 1)
                if rows != P:
                    sp.wait_ge(cleared, 1)
                load_tiles(sp, xin, p, x, tile, n, rows, loaded[p])
                sp.dma_start(hin[:, p, 0:n, :], tiles_of(M.h2, tile, n)).then_inc(loaded[p], 16)
            nodes.run(sp, group)

        @block.gpsimd
        def _(pool):
            def group(tile, g, p, n, rows):
                pool.wait_ge(xh_up, tile + n)
                pool.wait_ge(h_up, tile + n)
                pool.dma_start(tiles_of(M.h3, tile, n), h[:, p, 0:n, :]).then_inc(stored[p], 16)
                pool.dma_start(tiles_of(M.xh, tile, n), xh[:, p, 0:n, :]).then_inc(stored[p], 16)
                pool.wait_ge(stored[p], half(g, p) * 32 + 32)
                pool.sem_inc(out_free, 1)
            nodes.run(pool, group)

        @block.scalar
        def _(act):
            def group(tile, g, p, n, rows):
                for k in range(n):
                    act.wait_ge(low_up, tile + k + 1)
                    act.activation(low[:, p, k, :], low[:, p, k, :], ACT.Exp).then_inc(exp_up, 1)
                act.wait_ge(moments, g + 1)
                act.activation(dev[:, p, 0:n], mv[:, p, 0:n, 1], ACT.Sqrt, bias=K.eps[:, 0:1]).then_inc(devs, 1)
                act.wait_ge(scales, g + 1)
                act.wait_ge(out_free, g + 1)
                for k in range(n):
                    act.activation(h[:, p, k, :], r[:, p, k, :], ACT.Relu, bias=shift[:, p, k:k + 1],
                                   scale=scale[:, p, k:k + 1]).then_inc(h_up, 1)
            nodes.run(act, group)

        @block.vector
        def _(dve):
            dve.sem_inc(used, 2)
            dve.sem_inc(out_free, 2)
            per = 4 * G4 + 4

            def group(tile, g, p, n, rows):
                link = LoopLinked(dve, linked, g, per)
                if rows != P:
                    dve.wait_ge(used, g + 1)
                    dve.memset(xin[:, p, n - 1, :], 0.0).then_inc(cleared, 1)
                dve.wait_ge(loaded[p], half(g, p) * 48 + 48)
                for k in range(n):
                    a = acc[:, bass.ds((tile + k) * ROW, ROW)].rearrange("p (h d) -> p h d", d=HW)
                    rk = r[:, p, k, :].rearrange("p (h d) -> p h d", d=D)
                    link.run(dve.tensor_scalar(den[:, p, k, :], a[:, :, D], 1e-30, None, ALU.max))
                    link.run(dve.reciprocal(den[:, p, k, :], den[:, p, k, :]))
                    link.run(dve.tensor_tensor(rk, a[:, :, 0:D], den[:, p, k, :].unsqueeze(2).broadcast_to([P, H, D]), ALU.mult))
                    link.run(dve.tensor_tensor(r[:, p, k, :], r[:, p, k, :], hin[:, p, k, :], ALU.add))
                    dve.tensor_scalar(low[:, p, k, :], r[:, p, k, :], 0.0, None, ALU.min).then_inc(low_up, 1)
                    ins = dve.scalar_tensor_tensor(r[:, p, k, :], r[:, p, k, :], 0.0, xin[:, p, k, :], ALU.max, ALU.add)
                link.run(ins)
                for k in range(n):
                    dve.wait_ge(exp_up, tile + k + 1)
                    ins = dve.scalar_tensor_tensor(r[:, p, k, :], low[:, p, k, :], -1.0, r[:, p, k, :], ALU.add, ALU.add)
                link.run(ins)
                dve.sem_inc(used, 1)
                for k in range(n):
                    ins = dve.bn_stats(stats[:, p, k, :], r[:, p, k, :])
                link.run(ins)
                dve.sem_inc(passed, 1)
                for k in range(n):
                    ins = dve.bn_aggr(mv[:, p, k, :], stats[:, p, k, :])
                ins.then_inc(moments, 1)
                dve.wait_ge(devs, g + 1)
                link.run(dve.reciprocal(scale[:, p, 0:n], dev[:, p, 0:n]))
                dve.scalar_tensor_tensor(shift[:, p, 0:n], mv[:, p, 0:n, 0], -1.0, scale[:, p, 0:n], ALU.mult, ALU.mult)\
                    .then_inc(scales, 1)
                dve.wait_ge(out_free, g + 1)
                for k in range(n):
                    dve.wait_ge(h_up, tile + k + 1)
                    dve.tensor_tensor(xh[:, p, k, :], r[:, p, k, :], h[:, p, k, :], ALU.add).then_inc(xh_up, 1)
            nodes.run(dve, group)


def split_bias(dve, link, K, out, b3, part, rest):
    link.run(dve.tensor_copy(part[:, :], b3[:, :]))
    for k in range(3):
        link.run(dve.tensor_scalar(rest[:, 1, :], part[:, :], K.col3[:, k:k + 1], None, ALU.mult))
        if k == 0:
            link.run(dve.tensor_copy(out[:, :], rest[:, 1, :]))
        else:
            link.run(dve.tensor_tensor(out[:, :], out[:, :], rest[:, 1, :], ALU.add))
        if k < 2:
            link.run(dve.tensor_tensor(b3[:, :], b3[:, :], part[:, :], ALU.subtract))
            link.run(dve.tensor_copy(part[:, :], b3[:, :]))


def split_exactly(dve, link, high, low, rest, x, done=None):
    link.run(dve.tensor_scalar(rest.bitcast(I32), x.bitcast(I32), -4096, None, ALU.bitwise_and))
    dve.tensor_copy(high, rest)
    ins = dve.tensor_tensor(low, x, rest, ALU.subtract)
    if done is None:
        link.run(ins)
    else:
        ins.then_inc(done, 1)


def pass_messages(nc, S, K, M, attr, W1_d, b1_d, W2_d, b2_d, acc):
    NI = S.NI
    Q = 4
    with ExitStack() as ctx:
        sb, ps, sem = allocators(nc, ctx, "messages")
        G = sb("G", [P, 2, U, F])
        hot = sb("hot", [P, 2, U, P])
        index = sb("index", [P, 2, U], I32)
        local_c = sb("local_c", [P, 2, U])
        rbf = sb("rbf", [P, 2, U, NR])
        halves = sb("halves", [P, 2, Q, 2, NR], F32R)
        leading = sb("leading", [P, Q, NR])
        rbfT = sb("rbfT", [P, Q * P], F32R)
        hidden = sb("hidden", [P, 2, 2, Q * P])
        gate_free = sem("gate_free")
        gate = sb("gate", [P, 2, 2, F])
        tile_r = sb("tile_r", [1, S.V], I32)
        block_r = sb("block_r", [1, S.V], I32)
        W1 = sb("W1", [P, F])
        W1_part = sb("W1_part", [P, 2, F], F32R)
        W1_high = sb("W1_high", [P, F])
        W2 = sb("W2", [P, 2, F])
        b1 = sb("b1", [P, 2])
        b2 = sb("b2", [3, F])
        b2_3 = sb("b2_3", [3, F], BF16)
        part = sb("part", [3, F], BF16)
        rest = sb("rest", [3, 2, F])
        psX = ps("psX", [P, 512])
        psH = ps("psH", [P, 2, 512])
        psG = ps("psG", [P, 2, 512])
        psP = ps("psP", [P, 2, 2, F])
        index_up, tables_up = ([sem(f"{n}{p}") for p in range(2)] for n in ("index_up", "tables_up"))
        gathered = [sem.lasting(f"gathered{p}") for p in range(2)]
        (lists_up, weights_up, ready, hot_up, halves_up, turned, rbfT_up, hidden_in, hidden_up, gate_in, gate_up, weighed, summed,
         added, linked) = (sem(n) for n in (
             "lists_up", "weights_up", "ready", "hot_up", "halves_up", "attributes_turned", "rbfT_up", "hidden_in", "hidden_up", "gate_in",
             "gate_up", "weighed", "summed", "added", "dve_linked"))
        passed_pool, halved = sem("passed_pool"), sem("halved")
        CREDIT = 4
        block = phase_block(nc, ctx, sem)

        @block.sync
        def _(sp):
            regs = [sp.alloc_register(f"sp_block{u}") for u in range(U)]
            sp.dma_start(tile_r[:, :], M.tile.rearrange("(o n) -> o n", o=1)).then_inc(lists_up, 16)
            sp.dma_start(block_r[:, :], M.block.rearrange("(o n) -> o n", o=1)).then_inc(lists_up, 16)
            for n in range(2):
                sp.dma_start(W1[n * NR:n * NR + NR, :], W1_d).then_inc(weights_up, 16)
            sp.dma_start(W2[:, :, :], W2_d.rearrange("(k p) f -> p k f", p=P)).then_inc(weights_up, 16)
            sp.dma_start(b1[:, :].unsqueeze(2), b1_d.rearrange("(k p o) -> p k o", p=P, o=1), allow_slow_non_contiguous=True)\
                .then_inc(weights_up, 16)
            sp.dma_start(b2[:, :], b2_d.rearrange("(o f) -> o f", o=1).broadcast_to([3, F])).then_inc(weights_up, 16)
            sp.wait_ge(lists_up, 32)
            sp.wait_ge(M.attr_up, 32)

            def tables(i, p):
                sp.dma_start(index[:, p, :], M.src_col[:, bass.ds(i * U, U)]).then_inc(index_up[p], 16)
                sp.dma_start(local_c[:, p, :], M.local_col[:, bass.ds(i * U, U)]).then_inc(tables_up[p], 16)
                sp.load(regs, block_r[0:1, bass.ds(i * U, U)])
                for u in range(U):
                    b = sp.snap(regs[u], min_val=0, max_val=S.EB - 1)
                    sp.dma_start(rbf[:, p, u, :], attr[bass.ds(b * P, P), :]).then_inc(tables_up[p], 16)

            tables(0, 0)
            tables(1, 1)
            with sp.Fori(0, NI // 2) as j:
                for p in range(2):
                    i = j * 2 + p
                    sp.wait_ge(gathered[p], j * (16 * U) + 16 * U)
                    sp.wait_ge(hot_up, i * (U // Q) + U // Q)
                    sp.wait_ge(halves_up, i * (U // Q) + U // Q)
                    tables(i + 2, p)
            for p in range(2):
                sp.wait_ge(tables_up[p], (NI // 2 + 1) * 16 * (U + 1))
                sp.wait_ge(index_up[p], (NI // 2 + 1) * 16)

        @block.gpsimd
        def _(pool):
            def gather(j, p, before=None):
                hold(pool, index_up[p], j * 16 + 16, passed_pool)
                for u in range(U):
                    if before is not None:
                        hold(pool, summed, before * U + u + 1, passed_pool)
                    pool.indirect_dma_start(G[:, p, u, :], None, M.h3, bass.IndirectOffsetOnAxis(index[:, p, u:u + 1], 0))\
                        .then_inc(gathered[p], 16)
            gather(0, 0)
            gather(0, 1)
            with pool.Fori(0, NI // 2) as j:
                for p in range(2):
                    gather(j + 1, p, j * 2 + p)
            for p in range(2):
                pool.wait_ge(gathered[p], (NI // 2 + 1) * 16 * U)

        @block.tensor
        def _(pe):
            def turn(q, s):
                if not (isinstance(q, int) and q == 0):
                    pe.wait_ge(rbfT_up, q)
                pe.wait_ge(halves_up, q + 1)
                for k in range(Q):
                    both = halves[:, s % 2, k, :, :].rearrange("p a r -> p (a r)")
                    mm = pe.matmul(psX[:, k * P:k * P + P], both, K.ident_r[:, :], start=True, stop=True)
                mm.then_inc(turned, 1)

            def first(q):
                pe.wait_ge(rbfT_up, q + 1)
                if not (isinstance(q, int) and q == 0):
                    pe.wait_ge(hidden_up, 2 * q)
                for m in range(2):
                    for n in range(2):
                        mm = pe.matmul(psH[:, m, :], W1_part[:, n, m * P:m * P + P], rbfT[:, :],
                                       start=(n == 0), stop=(n == 1))
                    mm.then_inc(hidden_in, 1)

            def second(q, c, s):
                if c == 0:
                    pe.wait_ge(hidden_up, 2 * q + 2)
                pe.wait_ge(gate_up, 2 * q + c + 1)
                for k in range(2):
                    out = psG[:, c, k * F:k * F + F]
                    e = (c * 2 + k) * P
                    pe.matmul(out, K.ones3[:, :], b2_3[:, :], start=True, stop=False)
                    for m in range(2):
                        mm = pe.matmul(out, hidden[:, s % 2, m, e:e + P], W2[:, m, :], start=False, stop=(m == 1))
                mm.then_inc(gate_in, 1)

            def sums(q, p, s, c):
                pe.wait_ge(weighed, 2 * q + c + 1)
                pe.wait_ge(added, Q * q + (2 * c + 2))
                for k in range(2):
                    v = 2 * c + k
                    pe.matmul(psP[:, c, k, :], hot[:, p, s * Q + v, :], G[:, p, s * Q + v, :], start=True, stop=True).then_inc(summed, 1)

            pe.wait_ge(weights_up, 80)
            pe.wait_ge(ready, 1)
            turn(0, 0)
            first(0)
            turn(1, 1)
            second(0, 0, 0)
            first(1)
            second(0, 1, 0)
            with pe.Fori(0, NI // 2) as j:
                for p in range(2):
                    for s in range(U // Q):
                        q = j * (2 * U // Q) + (p * (U // Q) + s)
                        turn(q + 2, s)
                        second(q + 1, 0, s + 1)
                        pe.wait_ge(hot_up, q + 1)
                        sums(q, p, s, 0)
                        first(q + 2)
                        second(q + 1, 1, s + 1)
                        sums(q, p, s, 1)

        @block.scalar
        def _(act):
            def silus(q, s):
                for m in range(2):
                    act.wait_ge(hidden_in, 2 * q + m + 1)
                    act.activation(hidden[:, s, m, :], psH[:, m, :], ACT.Silu, bias=b1[:, m:m + 1]).then_inc(hidden_up, 1)

            def gates(q, c):
                act.wait_ge(gate_in, 2 * q + c + 1)
                act.wait_ge(gate_free, 2 * q + c + 1)
                act.activation(gate[:, c, :, :], psG[:, c, :], ACT.Tanh, scale=0.5).then_inc(gate_up, 1)

            def quad(q, s):
                gates(q, 0)
                silus(q + 1, 1 - s)
                gates(q, 1)

            act.sem_inc(gate_up, 2)
            act.wait_ge(weights_up, 80)
            silus(0, 0)
            with act.Fori(0, NI * (U // Q) // 2) as pair:
                for s in range(2):
                    quad(pair * 2 + s, s)
            quad(NI * (U // Q), 0)

        @block.vector
        def _(dve):
            link = Linked(dve, linked)
            dve.wait_ge(weights_up, 80)
            split_bias(dve, link, K, b2_3, b2, part, rest)
            dve.memset(acc[:, :], 0.0).then_inc(added, CREDIT)
            dve.sem_inc(gate_free, 2)
            split_exactly(dve, link, W1_part[:, 0, :], W1_part[:, 1, :], W1_high[:, :], W1[:, :])
            dve.sem_inc(ready, 1)
            dve.wait_ge(lists_up, 32)
            regs = [dve.alloc_register(f"dve_block{u}") for u in range(U)]

            def halve(q, p, s, j):
                if s == 0:
                    dve.wait_ge(tables_up[p], j * (16 * (U + 1)) + 16 * (U + 1))
                if not (isinstance(q, int) and q < 2):
                    dve.wait_ge(turned, q - 1)
                if not (isinstance(q, int) and q == 0):
                    dve.wait_ge(halves_up, q)
                own = rbf[:, p, s * Q:s * Q + Q, :]
                high, low = (halves[:, s % 2, :, n, :] for n in range(2))
                split_exactly(dve, LoopLinked(dve, halved, q, 1), high, low, leading[:, :, :], own, halves_up)

            def turn(q):
                dve.wait_ge(turned, q + 1)
                if not (isinstance(q, int) and q == 0):
                    dve.wait_ge(hidden_in, 2 * q)
                dve.tensor_copy(rbfT[:, :], psX[:, :]).then_inc(rbfT_up, 1)

            def weigh(q, c, p, s, j):
                if s == 0 and c == 0:
                    dve.wait_ge(gathered[p], j * (16 * U) + 16 * U)
                u = s * Q + 2 * c
                dve.wait_ge(gate_up, 2 * q + c + 3)
                dve.scalar_tensor_tensor(G[:, p, u:u + 2, :], gate[:, c, :, :], 1.0, G[:, p, u:u + 2, :], ALU.add, ALU.mult)\
                    .then_inc(weighed, 1)

            def freed(q, c):
                dve.wait_ge(weighed, 2 * q + c + 1)
                dve.sem_inc(gate_free, 1)

            def one_hot(p, s):
                dve.tensor_tensor(hot[:, p, s * Q:s * Q + Q, :], K.col[:, :].unsqueeze(1).broadcast_to([P, Q, P]),
                                  local_c[:, p, s * Q:s * Q + Q].unsqueeze(2).broadcast_to([P, Q, P]), ALU.is_equal).then_inc(hot_up, 1)

            def add(q, c, s, regs):
                for v in range(2 * c, 2 * c + 2):
                    t = dve.snap(regs[s * Q + v], min_val=0, max_val=S.NT - 1)
                    dve.wait_ge(summed, Q * q + (2 * c + 2))
                    dve.wait_ge(added, Q * q + (v + CREDIT))
                    a = acc[:, bass.ds(t * F, F)]
                    dve.tensor_tensor(a, a, psP[:, c, v % 2, :], ALU.add).then_inc(added, 1)

            halve(0, 0, 0, 0)
            halve(1, 0, 1, 0)
            turn(0)
            halve(2, 0, 2, 0)
            turn(1)
            for s in range(U // Q):
                one_hot(0, s)
            for c in range(2):
                weigh(0, c, 0, 0, 0)
                freed(0, c)
            with dve.Fori(0, NI // 2) as j:
                for p in range(2):
                    i = j * 2 + p
                    dve.load(regs, tile_r[0:1, bass.ds(i * U, U)])
                    for s in range(U // Q):
                        q = j * (2 * U // Q) + (p * (U // Q) + s)

                        def at(ahead):
                            k = p * (U // Q) + s + ahead
                            return k // (U // Q) % 2, k % (U // Q), j + 1 if k >= 2 * (U // Q) else j

                        turn(q + 2)
                        weigh(q + 1, 0, *at(1))
                        if s == 0:
                            dve.wait_ge(tables_up[1 - p], (j + p) * (16 * (U + 1)) + 16 * (U + 1))
                        one_hot(1 - p, s)
                        freed(q + 1, 0)
                        add(q, 0, s, regs)
                        halve(q + 3, *at(3))
                        weigh(q + 1, 1, *at(1))
                        freed(q + 1, 1)
                        add(q, 1, s, regs)
            dve.wait_ge(added, NI * U + CREDIT)


def finish_nodes(nc, S, K, M, U1_d, c1_d, U2_d, c2_d, acc, out):
    nodes = Nodes(S)
    with ExitStack() as ctx:
        sb, ps, sem = allocators(nc, ctx, "finish")
        hin = sb("hin", [P, 2, G4, F])
        xh = sb("xh", [P, 2, G4, F])
        agg = sb("agg", [P, 2, G4, F])
        both = sb("both", [P, 2, 4, P])
        act1 = sb("act1", [P, 2, 2, P])
        res = sb("res", [P, 2, G4, F])
        U1 = sb("U1", [P, 4, F])
        U2 = sb("U2", [P, 2, F])
        c1 = sb("c1", [P, 2])
        c2 = sb("c2", [3, F])
        c2_3 = sb("c2_3", [3, F], BF16)
        part = sb("part", [3, F], BF16)
        rest = sb("rest", [3, 2, F])
        psT = ps("psT", [P, 2, 512])
        psH = ps("psH", [P, 2, 512])
        psO = ps("psO", [P, 2, 512])
        (weights_up, ready, agg_up, turned, both_up, hidden_in, hidden_up, products, res_up, out_free, in_free, linked) = (
            sem(n) for n in ("weights_up", "ready", "agg_up", "turned", "both_up", "hidden_in", "hidden_up", "products", "res_up",
                             "out_free", "in_free", "dve_linked"))
        both_free = sem("both_free")
        loaded = [sem("loaded0"), sem("loaded1")]
        stored = [sem.lasting("stored0"), sem.lasting("stored1")]
        block = phase_block(nc, ctx, sem)

        @block.sync
        def _(sp):
            sp.dma_start(U1[:, :, :], U1_d.rearrange("(k p) f -> p k f", p=P)).then_inc(weights_up, 16)
            sp.dma_start(U2[:, :, :], U2_d.rearrange("(k p) f -> p k f", p=P)).then_inc(weights_up, 16)
            sp.dma_start(c1[:, :].unsqueeze(2), c1_d.rearrange("(k p o) -> p k o", p=P, o=1), allow_slow_non_contiguous=True)\
                .then_inc(weights_up, 16)
            sp.dma_start(c2[:, :], c2_d.rearrange("(o f) -> o f", o=1).broadcast_to([3, F])).then_inc(weights_up, 16)

            def group(tile, g, p, n, rows):
                sp.wait_ge(in_free, g + 1)
                sp.dma_start(hin[:, p, 0:n, :], tiles_of(M.h3, tile, n)).then_inc(loaded[p], 16)
                sp.dma_start(xh[:, p, 0:n, :], tiles_of(M.xh, tile, n)).then_inc(loaded[p], 16)
            nodes.run(sp, group)

        @block.gpsimd
        def _(pool):
            def group(tile, g, p, n, rows):
                pool.wait_ge(res_up, tile + n + 2)
                pool.sem_inc(in_free, 1)
                pool.dma_start(tiles_of(out, tile, n - 1), res[:, p, 0:n - 1, :]).then_inc(stored[p], 16)
                pool.dma_start(out[bass.ds((tile + n - 1) * P, rows), :], res[0:rows, p, n - 1, :]).then_inc(stored[p], 16)
                pool.wait_ge(stored[p], half(g, p) * 32 + 32)
                pool.sem_inc(out_free, 1)
            nodes.run(pool, group)

        @block.tensor
        def _(pe):
            pe.wait_ge(ready, 1)

            def turn(T, p, k):
                pe.wait_ge(agg_up, T + 1)
                pe.wait_ge(both_up, T + 1)
                for c in range(4):
                    rows = hin if c < 2 else agg
                    mm = pe.transpose(psT[:, k % 2, c * P:c * P + P], rows[:, p, k, c % 2 * P:c % 2 * P + P], K.ident[:, :])
                mm.then_inc(turned, 1)

            def first(T, k):
                pe.wait_ge(both_up, T + 3)
                pe.wait_ge(hidden_up, T + 1)
                for m in range(2):
                    for c in range(4):
                        mm = pe.matmul(psH[:, k % 2, m * P:m * P + P], U1[:, c, m * P:m * P + P], both[:, k % 2, c, :],
                                       start=(c == 0), stop=(c == 3))
                mm.then_inc(hidden_in, 1)
                pe.wait_ge(hidden_in, T + 1)
                pe.sem_inc(both_free, 1)

            def second(T, k):
                pe.wait_ge(hidden_up, T + 3)
                pe.wait_ge(res_up, T + 1)
                pe.matmul(psO[:, k % 2, 0:F], K.ones3[:, :], c2_3[:, :], start=True, stop=False)
                for m in range(2):
                    mm = pe.matmul(psO[:, k % 2, 0:F], act1[:, k % 2, m, :], U2[:, m, :], start=False, stop=(m == 1))
                mm.then_inc(products, 1)

            def group(tile, g, p, n, rows):
                pe.wait_ge(loaded[p], half(g, p) * 32 + 32)
                turn(tile, p, 0)
                for k in range(n):
                    if k + 1 < n:
                        turn(tile + k + 1, p, k + 1)
                    first(tile + k, k)
                    if k:
                        second(tile + k - 1, k - 1)
                second(tile + n - 1, n - 1)
            nodes.run(pe, group)

        @block.scalar
        def _(act):
            act.sem_inc(hidden_up, 2)
            act.wait_ge(weights_up, 64)

            def group(tile, g, p, n, rows):
                for k in range(n):
                    T = tile + k
                    act.wait_ge(hidden_in, T + 1)
                    for m in range(2):
                        ins = act.activation(act1[:, k % 2, m, :], psH[:, k % 2, m * P:m * P + P], ACT.Silu, bias=c1[:, m:m + 1])
                    ins.then_inc(hidden_up, 1)
            nodes.run(act, group)

        @block.vector
        def _(dve):
            link = Linked(dve, linked)
            dve.wait_ge(weights_up, 64)
            split_bias(dve, link, K, c2_3, c2, part, rest)
            dve.sem_inc(ready, 1)
            dve.sem_inc(both_up, 2)
            dve.sem_inc(both_free, 2)
            dve.sem_inc(res_up, 2)
            dve.sem_inc(in_free, 2)
            dve.sem_inc(out_free, 2)

            def group(tile, g, p, n, rows):
                dve.wait_ge(out_free, g + 1)
                for k in range(n):
                    dve.tensor_scalar(agg[:, p, k, :], acc[:, bass.ds((tile + k) * F, F)], 0.5, None, ALU.mult).then_inc(agg_up, 1)
                dve.wait_ge(loaded[p], half(g, p) * 32 + 32)
                for k in range(n + 1):
                    if k < n:
                        dve.wait_ge(turned, tile + k + 1)
                        dve.wait_ge(both_free, tile + k + 1)
                        dve.tensor_copy(both[:, k % 2, :, :], psT[:, k % 2, :].rearrange("p (c e) -> p c e", c=4)).then_inc(both_up, 1)
                    if k:
                        dve.wait_ge(products, tile + k)
                        dve.tensor_tensor(res[:, p, k - 1, :], psO[:, k % 2 ^ 1, 0:F], xh[:, p, k - 1, :], ALU.add).then_inc(res_up, 1)
            nodes.run(dve, group)


class Memory:

    def __init__(self, nc, S):
        def dram(name, shape, dt=F32):
            return nc.dram_tensor(name, shape, dt).ap()

        V = S.V
        self.dst_all = dram("dst_e", (S.EB * P + 1,), I32)
        self.dst_e = self.dst_all[0:S.EB * P]
        self.src_e = dram("src_e", (S.EB * P,), I32)
        self.dst_v = dram("dst_v", (1 + V * P,))
        self.tile = dram("tile", (V,), I32)
        self.block = dram("block", (V,), I32)
        self.local_row = dram("local_row", (V * P,), BF16)
        self.local_col = dram("local_col", (P, V))
        self.src_col = dram("src_col", (P, V), I32)
        self.apart = dram("apart", (V * P,))
        self.whole = dram("whole", (V,))
        self.alike = dram("alike", (V,))
        self.goes_on = dram("goes_on", (V,))
        self.table = dram("table", (S.NT * P, ROW))
        self.h2 = dram("h2", (S.NT * P, F))
        self.h3 = dram("h3", (S.NT * P, F))
        self.xh = dram("xh", (S.NT * P, F))
        self.attr = dram("attr", (S.EB * P, NR))
        self.record = [dram(f"record{d}", (S.EB * P, 4), I32) for d in range(2)]


class Patterns:
    pass


def build(nc, x, src, dst, attr, W1, al1, ar1, W2, al2, ar2, V1, b1, V2, b2, U1, c1, U2, c2, out):
    S = Sizes(x.shape[0], src.shape[0])
    M = Memory(nc, S)
    with ExitStack() as ctx:
        outer[0] = ctx
        sb, _, sem = allocators(nc, ctx, "all")
        K = Patterns()
        K.col = sb("col", [P, P])
        K.row = sb("rown", [P, 1])
        K.ident = sb("ident", [P, P])
        K.hu = sb("hu", [R, 2])
        K.head_of = sb("head_of", [R, H])
        K.visit_of = sb("visit_of", [R, U])
        K.rows_of = sb("rows_of", [H, R])
        K.ones = sb("ones", [1, P])
        K.ones3 = sb("ones3", [3, P], BF16)
        K.col3 = sb("col3", [3, 3])
        K.eps = sb("eps", [P, 1])
        K.every = sb("every", [P, P])
        K.ident_r = sb("ident_r", [P, P], F32R)
        K.unsorted = sb("unsorted", [1, 1], I32)
        M.zeros = sb("zeros", [S.EB * P - S.E, NR])
        M.attr_up = sem("attributes_up")
        constants(nc, K)
        pad_edges(nc, S, K, M, src, dst, attr)
        sort_edges(nc, S, K, M, attr)
        visit_tables(nc, S, K, M)
        er3 = sb("er3", [P, S.NT, 3, H], BF16)
        acc = sb("acc", [P, S.NT * ROW])
        Waug = sb("Waug", [P, 2, ROW + H])
        attention_weights(nc, K, M, W1, al1, ar1, Waug, 1)
        project_nodes(nc, S, K, M, True, x, Waug, er3, acc)
        attend(nc, S, K, M, er3, acc, 1)
        attention_weights(nc, K, M, W2, al2, ar2, Waug, 2)
        project_nodes(nc, S, K, M, False, x, Waug, er3, acc)
        attend(nc, S, K, M, er3, acc, 2)
        renew_nodes(nc, S, K, M, x, acc)
        pass_messages(nc, S, K, M, M.attr, V1, b1, V2, b2, acc)
        finish_nodes(nc, S, K, M, U1, c1, U2, c2, acc, out)


_INS = ["x", "src", "dst", "edge_attr_64", "L0_gnn_W1", "L0_gnn_al1", "L0_gnn_ar1", "L0_gnn_W2", "L0_gnn_al2", "L0_gnn_ar2",
        "L1_gnn_W1", "L1_gnn_b1", "L1_gnn_W2", "L1_gnn_b2", "L1_gnn_U1", "L1_gnn_c1", "L1_gnn_U2", "L1_gnn_c2"]


def kernel(**inputs):
    import numpy as _np
    import concourse.bacc as _bacc
    from concourse import mybir as _mybir
    from concourse.bass_utils import run_bass_kernel_spmd as _run

    nc = _bacc.Bacc("TRN2", target_bir_lowering=False, num_devices=1)
    arrays, args = {}, []
    for name in _INS:
        a = _np.ascontiguousarray(inputs[name])
        arrays[f"in_{name}_dram"] = a
        args.append(nc.dram_tensor(f"in_{name}_dram", a.shape, _mybir.dt.from_np(a.dtype), kind="ExternalInput").ap())
    out = nc.dram_tensor("out_0_dram", tuple(inputs["x"].shape), _mybir.dt.float32, kind="ExternalOutput").ap()
    build(nc, *args, out)
    r = _run(nc, [arrays], core_ids=[0])
    return r.results[0]["out_0_dram"]
```

```python
from contextlib import ExitStack

import concourse.bass as bass
from concourse import mybir

P = 128
F = 256
H = 4
D = F // H
HW = D + 1
ROW = H * HW
NR = 64
U = 16
R = H * U
G4 = 4
BIG = 1.0e30
SLOPE = 0.2
EPS = 1.0e-5
BANKS = 4

F32 = mybir.dt.float32
F32R = mybir.dt.float32r
I32 = mybir.dt.int32
BF16 = mybir.dt.bfloat16
ALU = mybir.AluOpType
ACT = mybir.ActivationFunctionType
AX = mybir.AxisListType


class Linked:

    def __init__(self, eng, sem):
        self.eng, self.sem, self.n = eng, sem, 0

    def run(self, ins):
        self.n += 1
        ins.then_inc(self.sem, 1)
        self.eng.wait_ge(self.sem, self.n)


class LoopLinked:

    def __init__(self, eng, sem, turn, per):
        self.eng, self.sem, self.turn, self.per, self.n = eng, sem, turn, per, 0

    def run(self, ins):
        self.n += 1
        assert self.n <= self.per
        ins.then_inc(self.sem, 1)
        self.eng.wait_ge(self.sem, self.turn * self.per + self.n)


class Sizes:
    def __init__(self, n, e):
        self.N, self.E = n, e
        self.NT = -(-n // P)
        self.EB = -(-e // P)
        self.LAST = n - (self.NT - 1) * P
        assert self.LAST < P and self.NT % (2 * G4) == 2
        most = self.EB + self.NT - 1
        self.NI = 2 * -(-most // (2 * U))
        self.share = e // self.NI // 16 * 16
        self.attr_copies = self.NI + 1 + (self.NI * self.share < e)
        self.NC = -(-(self.NI + 2) * U // P)
        self.V = self.NC * P


def allocators(nc, ctx, phase, lasts=None):
    def sb(name, shape, dt=F32):
        return ctx.enter_context(nc.sbuf_tensor(f"{phase}_{name}", shape, dt))

    def ps(name, shape):
        return ctx.enter_context(nc.psum_tensor(f"{phase}_{name}", shape, F32))

    def sem(name):
        made.append(ctx.enter_context(nc.semaphore(f"{phase}_{name}")))
        return made[-1]

    def lasting(name):
        return lasts.enter_context(nc.semaphore(f"{phase}_{name}"))

    made = []
    sem.made, sem.lasting = made, lasting
    return sb, ps, sem


def phase_block(nc, ctx, sem):
    def clear():
        with nc.Block() as after:
            @after.gpsimd
            def _(pool):
                for s in sem.made:
                    pool.sem_clear(s)

    ctx.callback(clear)
    return ctx.enter_context(nc.Block())


def constants(nc, K):
    with ExitStack() as ctx:
        sb, ps, sem = allocators(nc, ctx, "constants")
        col_i, row_i, head_i, fill = (sb(n, s, I32) for n, s in
                                ((("col_i", [P, P])), ("row_i", [P, 1]), ("head_i", [H, R]), ("fill", [R, 2])))
        iotas, linked = sem("iotas"), sem("dve_linked")
        block = phase_block(nc, ctx, sem)

        @block.gpsimd
        def _(pool):
            pool.iota(col_i[:, :], [[1, P]], base=0, channel_multiplier=0).then_inc(iotas, 1)
            pool.iota(row_i[:, :], [[0, 1]], base=0, channel_multiplier=1).then_inc(iotas, 1)
            pool.iota(head_i[:, :], [[0, U], [1, H]], base=0, channel_multiplier=0).then_inc(iotas, 1)

        @block.vector
        def _(dve):
            link = Linked(dve, linked)
            dve.wait_ge(iotas, 3)
            link.run(dve.tensor_copy(K.col[:, :], col_i[:, :]))
            link.run(dve.tensor_copy(K.row[:, :], row_i[:, :]))
            link.run(dve.tensor_scalar(K.ident[:, :], K.col[:, :], K.row[:, 0:1], None, ALU.is_equal))
            dve.tensor_copy(K.ident_r[:, :], K.ident[:, :])
            link.run(dve.tensor_scalar(fill[:, 0:1], row_i[0:R, :], H - 1, None, ALU.bitwise_and))
            link.run(dve.tensor_scalar(fill[:, 1:2], row_i[0:R, :], H.bit_length() - 1, None,
                                       ALU.logical_shift_right))
            link.run(dve.tensor_copy(K.hu[:, :], fill[:, :]))
            link.run(dve.tensor_scalar(K.head_of[:, :], K.col[0:R, 0:H], K.hu[:, 0:1], None, ALU.is_equal))
            link.run(dve.tensor_scalar(K.visit_of[:, :], K.col[0:R, 0:U], K.hu[:, 1:2], None, ALU.is_equal))
            link.run(dve.tensor_copy(K.rows_of[:, :], head_i[:, :]))
            link.run(dve.tensor_scalar(K.rows_of[:, :], K.rows_of[:, :], K.row[0:H, 0:1], None, ALU.is_equal))
            link.run(dve.memset(K.ones[:, :], 1.0))
            link.run(dve.memset(K.every[:, :], 1.0))
            link.run(dve.memset(K.ones3[:, :], 1.0))
            link.run(dve.tensor_copy(K.col3[:, :], K.ident[0:3, 0:3]))
            link.run(dve.memset(K.eps[:, :], EPS))


def pad_edges(nc, S, K, M, src, dst):
    EB, E = S.EB, S.E
    tail = EB * P - E
    with ExitStack() as ctx:
        sb, ps, sem = allocators(nc, ctx, "pad", M.context)
        nodes = sb("nodes", [1, 2, P + 1], I32)
        here = sb("here", [P, EB], I32)
        ahead = sb("ahead", [P, EB], I32)
        falls = sb("falls", [P, EB])
        falls_p = sb("falls_p", [P, 1])
        sum_p = ps("sum", [1, 1])
        nodes_up, padded, loaded, falls_up, summed, linked = (sem(n) for n in (
            "nodes_up", "padded", "loaded", "falls_up", "summed", "dve_linked"))
        zeros_up = sem("zeros_up")
        block = phase_block(nc, ctx, sem)

        @block.scalar
        def _(act):
            act.wait_ge(zeros_up, 1)
            act.dma_start(M.attr[E:EB * P, :], M.zeros[:, :]).then_inc(M.attr_up, 16)

        @block.sync
        def _(sp):
            for out, edges in ((M.dst_all, dst), (M.src_e, src)):
                sp.dma_start(out[0:E].rearrange("(a b) -> a b", a=16), edges.rearrange("(a b) -> a b", a=16)).then_inc(padded, 16)
            sp.wait_ge(nodes_up, 2)
            sp.dma_start(M.dst_all[E:EB * P + 1].rearrange("(a b) -> a b", a=1), nodes[:, 0, 0:tail + 1]).then_inc(padded, 16)
            sp.dma_start(M.src_e[E:EB * P].rearrange("(a b) -> a b", a=1), nodes[:, 1, 0:tail]).then_inc(padded, 16)
            sp.wait_ge(padded, 64)
            sp.dma_start(here[:, :], M.dst_all[0:EB * P].rearrange("(p c) -> p c", p=P)).then_inc(loaded, 16)
            sp.dma_start(ahead[:, :], M.dst_all[1:EB * P + 1].rearrange("(p c) -> p c", p=P)).then_inc(loaded, 16)

        @block.gpsimd
        def _(pool):
            pool.memset(nodes[:, 0, :], S.NT * P - 1).then_inc(nodes_up, 1)
            pool.memset(nodes[:, 1, :], 0).then_inc(nodes_up, 1)

        @block.tensor
        def _(pe):
            pe.wait_ge(falls_up, 1)
            pe.matmul(sum_p[:, :], falls_p[:, :], K.every[:, 0:1], start=True, stop=True).then_inc(summed, 1)

        @block.vector
        def _(dve):
            link = Linked(dve, linked)
            dve.memset(M.zeros[:, :], 0.0).then_inc(zeros_up, 1)
            dve.wait_ge(loaded, 32)
            link.run(dve.tensor_tensor(falls[:, :], ahead[:, :], here[:, :], ALU.is_lt))
            dve.tensor_reduce(falls_p[:, :], falls[:, :], AX.X, ALU.max).then_inc(falls_up, 1)
            dve.wait_ge(summed, 1)
            dve.tensor_copy(K.unsorted[:, :], sum_p[:, :])


def where_unsorted(eng, K, name, passed, body):
    falls = eng.alloc_register(f"{name}_falls")
    eng.load([falls], K.unsorted[0:1, 0:1])
    with eng.If_ne(falls, 0):
        body()
    eng.sem_inc(passed, 1)


def sort_edges(nc, S, K, M):
    EB = S.EB
    with ExitStack() as ctx:
        sb, ps, sem = allocators(nc, ctx, "sort", M.context)
        record = sb("record", [P, EB, 4], I32)
        dst_s = sb("dst", [P, EB], I32)
        src_s = sb("src", [P, EB], I32)
        number = sb("number", [P, EB], I32)
        digit = sb("digit", [P, EB])
        digit_i = sb("digit_i", [P, EB], I32)
        counts = sb("counts", [P, P])
        total = sb("total", [P, P])
        upto = sb("upto", [P, P])
        base = sb("base", [P, P])
        hot = sb("hot", [P, P])
        place = sb("place", [P, P])
        own = sb("own", [P, P])
        place_f = sb("place_f", [P, 1])
        place_i = sb("place_i", [P, 1], I32)
        sent = sb("sent", [P, 4], I32)
        before = sb("before", [P, P])
        total_p, before_p, chunk_p = (ps(n, [P, P]) for n in ("total_p", "before_p", "chunk_p"))
        numbered, loaded, resorted, stored, linked = (sem(n) for n in (
            "numbered", "loaded", "resorted", "stored", "dve_linked"))
        counts_up, totals_in, hot_up, ranked, sent_up, sent_free, count_linked, rank_linked = (
            [sem(f"{n}{d}") for d in range(2)] for n in (
                "counts_up", "totals_in", "hot_up", "ranked", "sent_up", "sent_free", "count_linked", "rank_linked"))
        scattered = [sem.lasting(f"scattered{d}") for d in range(2)]
        passed = sem("passed")
        block = phase_block(nc, ctx, sem)

        @block.sync
        def _(sp):
            def body():
                line = lambda t: t.rearrange("(p c) -> p c", p=P)
                sp.dma_start(dst_s[:, :], line(M.dst_e)).then_inc(loaded, 16)
                sp.dma_start(src_s[:, :], line(M.src_e)).then_inc(loaded, 16)
                sp.wait_ge(scattered[0], 16 * EB)
                sp.dma_start(record[:, :, :], M.record[0].rearrange("(c p) f -> p c f", p=P)).then_inc(loaded, 16)
                sp.wait_ge(scattered[1], 16 * EB)
                sp.dma_start(record[:, :, :], M.record[1].rearrange("(p c) f -> p c f", p=P)).then_inc(loaded, 16)
                sp.wait_ge(resorted, 1)
                sp.dma_start(line(M.dst_e), dst_s[:, :]).then_inc(stored, 16)
                sp.dma_start(line(M.src_e), src_s[:, :]).then_inc(stored, 16)
                sp.wait_ge(stored, 32)
            where_unsorted(sp, K, "sp", passed, body)

        @block.gpsimd
        def _(pool):
            def body():
                pool.iota(number[:, :], [[1, EB]], base=0, channel_multiplier=EB).then_inc(numbered, 1)
                for d in range(2):
                    with pool.Fori(0, EB) as c:
                        hold(pool, sent_up[d], c + 1, passed)
                        pool.indirect_dma_start(M.record[d], bass.IndirectOffsetOnAxis(place_i[:, :], 0), sent[:, :], None)\
                            .then_inc(scattered[d], 16)
                        pool.wait_ge(scattered[d], c * 16 + 16)
                        pool.sem_inc(sent_free[d], 1)
            where_unsorted(pool, K, "pool", passed, body)

        @block.tensor
        def _(pe):
            def body():
                for d in range(2):
                    pe.wait_ge(counts_up[d], 1)
                    pe.matmul(total_p[:, :], K.every[:, :], counts[:, :], start=True, stop=True).then_inc(totals_in[d], 1)
                    with pe.Fori(0, EB) as c:
                        pe.wait_ge(hot_up[d], c + 1)
                        pe.matmul(before_p[:, :], before[:, :], hot[:, :], start=True, stop=True)
                        pe.matmul(chunk_p[:, :], K.every[:, :], hot[:, :], start=True, stop=True).then_inc(ranked[d], 1)
            where_unsorted(pe, K, "pe", passed, body)

        @block.vector
        def _(dve):
            def body():
                link = Linked(dve, linked)
                link.run(dve.tensor_scalar(before[:, :], K.col[:, :], K.row[:, 0:1], None, ALU.is_gt))
                dve.wait_ge(loaded, 32)
                dve.wait_ge(numbered, 1)
                dve.tensor_copy(record[:, :, 0], dst_s[:, :])
                dve.tensor_copy(record[:, :, 1], src_s[:, :])
                dve.tensor_copy(record[:, :, 2], number[:, :])
                link.run(dve.tensor_copy(record[:, :, 3], number[:, :]))
                for d in range(2):
                    if d:
                        dve.wait_ge(loaded, 48)
                        link.run(dve.tensor_scalar(digit_i[:, :], record[:, :, 0], P.bit_length() - 1, None, ALU.logical_shift_right))
                    else:
                        link.run(dve.tensor_scalar(digit_i[:, :], record[:, :, 0], P - 1, None, ALU.bitwise_and))
                    link.run(dve.tensor_copy(digit[:, :], digit_i[:, :]))
                    link.run(dve.memset(counts[:, :], 0.0))
                    with dve.Fori(0, EB) as c:
                        each = LoopLinked(dve, count_linked[d], c, 1)
                        each.run(dve.scalar_tensor_tensor(counts[:, :], K.col[:, :], digit[:, bass.ds(c, 1)], counts[:, :],
                                                          ALU.is_equal, ALU.add))
                    dve.sem_inc(counts_up[d], 1)
                    dve.wait_ge(totals_in[d], 1)
                    link.run(dve.tensor_copy(total[:, :], total_p[:, :]))
                    link.run(dve.tensor_tensor_scan(upto[:, :], K.every[:, :], total[:, :], 0.0, ALU.mult, ALU.add))
                    link.run(dve.tensor_tensor(base[:, :], upto[:, :], total[:, :], ALU.subtract))
                    dve.sem_inc(sent_free[d], 1)
                    with dve.Fori(0, EB) as c:
                        each = LoopLinked(dve, rank_linked[d], c, 4)
                        dve.tensor_scalar(hot[:, :], K.col[:, :], digit[:, bass.ds(c, 1)], None, ALU.is_equal).then_inc(hot_up[d], 1)
                        dve.wait_ge(ranked[d], c + 1)
                        each.run(dve.tensor_tensor(place[:, :], before_p[:, :], base[:, :], ALU.add))
                        each.run(dve.tensor_tensor(own[:, :], place[:, :], hot[:, :], ALU.mult))
                        each.run(dve.tensor_reduce(place_f[:, :], own[:, :], AX.X, ALU.add))
                        each.run(dve.tensor_tensor(base[:, :], base[:, :], chunk_p[:, :], ALU.add))
                        dve.wait_ge(sent_free[d], c + 1)
                        dve.tensor_copy(sent[:, :].unsqueeze(1), record[:, bass.ds(c, 1), :])
                        dve.tensor_copy(place_i[:, :], place_f[:, :]).then_inc(sent_up[d], 1)
                dve.wait_ge(loaded, 64)
                dve.tensor_copy(dst_s[:, :], record[:, :, 0])
                dve.tensor_copy(src_s[:, :], record[:, :, 1]).then_inc(resorted, 1)
            where_unsorted(dve, K, "dve", passed, body)


def sort_attributes(nc, S, K, M, attr):
    EB, E = S.EB, S.E
    with ExitStack() as ctx:
        sb, _, sem = allocators(nc, ctx, "sort_attributes", M.context)
        record = sb("record", [P, EB, 4], I32)
        number = sb("number", [P, EB], I32)
        which = sb("which", [P, 1], I32)
        moved = sb("moved", [P, NR])
        loaded, numbers_up, which_free, which_up, moved_up, stored, passed = (sem(n) for n in (
            "loaded", "numbers_up", "which_free", "which_up", "moved_up", "stored", "passed"))
        gathered = sem.lasting("gathered")
        block = phase_block(nc, ctx, sem)

        @block.sync
        def _(sp):
            def body():
                sp.dma_start(record[:, :, :], M.record[1].rearrange("(p c) f -> p c f", p=P)).then_inc(loaded, 16)
                sp.wait_ge(M.attr_up, S.attr_copies * 16)
                rows = M.attr.rearrange("(p c) f -> p c f", p=P)
                with sp.Fori(0, EB) as c:
                    sp.wait_ge(moved_up, c + 1)
                    sp.dma_start(rows[:, bass.ds(c, 1), :], moved[:, :].unsqueeze(1)).then_inc(stored, 16)
                    sp.wait_ge(stored, c * 16 + 16)
                    sp.sem_inc(which_free, 1)
            where_unsorted(sp, K, "sp_attributes", passed, body)

        @block.gpsimd
        def _(pool):
            def body():
                with pool.Fori(0, EB) as c:
                    hold(pool, which_up, c + 1, passed)
                    pool.indirect_dma_start(moved[:, :], None, attr, bass.IndirectOffsetOnAxis(which[:, :], 0)).then_inc(gathered, 16)
                    pool.wait_ge(gathered, c * 16 + 16)
                    pool.sem_inc(moved_up, 1)
            where_unsorted(pool, K, "pool_attributes", passed, body)

        @block.vector
        def _(dve):
            def body():
                dve.wait_ge(loaded, 16)
                dve.tensor_scalar(number[:, :], record[:, :, 2], E - 1, None, ALU.min).then_inc(numbers_up, 1)
                dve.wait_ge(numbers_up, 1)
                dve.sem_inc(which_free, 1)
                with dve.Fori(0, EB) as c:
                    dve.wait_ge(which_free, c + 1)
                    dve.tensor_copy(which[:, :], number[:, bass.ds(c, 1)]).then_inc(which_up, 1)
            where_unsorted(dve, K, "dve_attributes", passed, body)


def visit_tables(nc, S, K, M):
    EB, V, NC = S.EB, S.V, S.NC
    W = EB + 1
    CH = 512
    with ExitStack() as ctx:
        sb, ps, sem = allocators(nc, ctx, "visits", M.context)
        ends = sb("ends", [1, 2, EB], I32)
        tiles = sb("tiles", [1, 2, EB])
        until = sb("until", [1, W])
        skip = sb("skip", [1, W])
        one = sb("one", [1, W])
        until_b = sb("until_b", [P, W])
        skip_b = sb("skip_b", [P, W])
        ones_b = sb("ones_b", [P, W])
        junk = sb("junk", [P, W])
        number = sb("number", [P, NC])
        count = sb("count", [P, NC])
        tile_v = sb("tile_v", [P, NC])
        tile_c = sb("tile_c", [P, NC])
        tile_m = sb("tile_m", [P, NC])
        tile_i = sb("tile_i", [P, NC], I32)
        block_f = sb("block_f", [P, NC])
        block_i = sb("block_i", [P, NC], I32)
        rows_d = sb("rows_d", [P, NC, P], I32)
        rows_s = sb("rows_s", [P, NC, P], I32)
        dst_f = sb("dst_f", [P, NC, P])
        src_f = sb("src_f", [P, NC, P])
        prev_f = sb("prev_f", [P, NC, P])
        local = sb("local", [P, NC, P])
        local_h = sb("local_h", [P, NC, P], BF16)
        same = sb("same", [P, NC, P])
        same0 = sb("same0", [P, NC])
        whole = sb("whole", [P, NC])
        alike = sb("alike", [P, NC])
        local_t = sb("local_t", [P, V])
        src_t = sb("src_t", [P, V], I32)
        bcast = ps("bcast", [P, 2, CH])
        turned = ps("turned", [P, 2, 512])
        got = sem.lasting("rows_got")
        (numbered, loaded, linked, rows_up, broad, lists, local_up, turned_up, kept, prevs,
         stored, cols, edges_in) = (sem(n) for n in (
             "numbered", "ends_loaded", "dve_linked", "rows_up", "broad", "lists", "local_up",
             "turned_up", "turned_kept", "prevs", "stored", "tables_up", "broad_up"))
        chunks = [(a, min(CH, W - a)) for a in range(0, W, CH)]
        turns = [(which, c, min(4, NC - c)) for which in range(2) for c in range(0, NC, 4)]
        block = phase_block(nc, ctx, sem)

        @block.sync
        def _(sp):
            blocks = M.dst_e.rearrange("(o b e) -> o b e", e=P, o=1)
            sp.dma_start(ends[:, 0, :].unsqueeze(2), blocks[:, :, 0:1], allow_slow_non_contiguous=True).then_inc(loaded, 16)
            sp.dma_start(ends[:, 1, :].unsqueeze(2), blocks[:, :, P - 1:P], allow_slow_non_contiguous=True).then_inc(loaded, 16)
            sp.wait_ge(local_up, 1)
            sp.dma_start(M.dst_v[1:1 + V * P].rearrange("(c p e) -> p c e", p=P, e=P), dst_f[:, :, :]).then_inc(stored, 16)
            sp.wait_ge(lists, 1)
            sp.dma_start(M.dst_v[0:1].rearrange("(a b) -> a b", a=1), until[0:1, 0:1]).then_inc(stored, 16)
            sp.wait_ge(stored, 32)
            sp.dma_start(prev_f[:, :, :], M.dst_v[0:V * P].rearrange("(c p e) -> p c e", p=P, e=P)).then_inc(prevs, 16)
            by_visit = lambda t: t.rearrange("(c p o) -> p c o", p=P, o=1)
            sp.wait_ge(lists, 3)
            sp.dma_start(by_visit(M.tile), tile_i[:, :].unsqueeze(2), allow_slow_non_contiguous=True).then_inc(stored, 16)
            sp.dma_start(by_visit(M.block), block_i[:, :].unsqueeze(2), allow_slow_non_contiguous=True).then_inc(stored, 16)
            sp.wait_ge(local_up, 3)
            sp.dma_start(M.local_row.rearrange("(c p e) -> p c e", p=P, e=P), local_h[:, :, :]).then_inc(stored, 16)
            sp.wait_ge(kept, len(turns))
            sp.dma_start(M.local_col, local_t[:, :]).then_inc(stored, 16)
            sp.dma_start(M.src_col, src_t[:, :]).then_inc(stored, 16)
            sp.wait_ge(cols, 1)
            for h in range(H):
                sp.dma_start(M.apart.rearrange("(c p h) e -> h p c e", p=P, h=H)[h], same[:, :, :]).then_inc(stored, 16)
            sp.dma_start(by_visit(M.alike), alike[:, :].unsqueeze(2), allow_slow_non_contiguous=True).then_inc(stored, 16)
            sp.dma_start(by_visit(M.whole), whole[:, :].unsqueeze(2), allow_slow_non_contiguous=True).then_inc(stored, 16)
            sp.dma_start(by_visit(M.goes_on), same0[:, :].unsqueeze(2), allow_slow_non_contiguous=True).then_inc(stored, 16)
            sp.wait_ge(stored, 32 + (8 + H) * 16)

        @block.tensor
        def _(pe):
            pe.wait_ge(rows_up, 1)
            for n, (a, w) in enumerate(chunks * 2):
                row = until if n < len(chunks) else skip
                if n >= 2:
                    pe.wait_ge(broad, n - 1)
                pe.matmul(bcast[:, n % 2, 0:w], K.ones[0:1, :], row[0:1, a:a + w], start=True, stop=True).then_inc(edges_in, 1)
            pe.wait_ge(local_up, 3)
            for n, (which, c, w) in enumerate(turns):
                if n >= 2:
                    pe.wait_ge(kept, n - 1)
                for k in range(w):
                    mm = pe.transpose(turned[:, n % 2, k * P:k * P + P], (src_f if which else local)[:, c + k, :], K.ident[:, :])
                mm.then_inc(turned_up, 1)

        @block.gpsimd
        def _(pool):
            pool.iota(rows_d[:, 0, 0:NC], [[P, NC]], base=0, channel_multiplier=1).then_inc(numbered, 1)
            pool.wait_ge(lists, 3)
            for table, rows in ((M.dst_e, rows_d), (M.src_e, rows_s)):
                for c in range(NC):
                    pool.indirect_dma_start(rows[:, c, :], None, table.rearrange("(b e) -> b e", e=P),
                                            bass.IndirectOffsetOnAxis(block_i[:, c:c + 1], 0)).then_inc(got, 16)

        @block.scalar
        def _(act):
            for n, (which, c, w) in enumerate(turns):
                act.wait_ge(turned_up, n + 1)
                out = (src_t if which else local_t)[:, c * P:(c + w) * P]
                act.activation(out, turned[:, n % 2, 0:w * P], ACT.Copy).then_inc(kept, 1)

        @block.vector
        def _(dve):
            link = Linked(dve, linked)
            dve.wait_ge(numbered, 1)
            link.run(dve.tensor_copy(number[:, :], rows_d[:, 0, 0:NC]))
            link.run(dve.memset(ones_b[:, :], 1.0))
            link.run(dve.memset(one[:, :], 1.0))
            dve.wait_ge(loaded, 32)
            link.run(dve.tensor_scalar(ends[:, :, :], ends[:, :, :], P.bit_length() - 1, None, ALU.logical_shift_right))
            link.run(dve.tensor_copy(tiles[:, :, :], ends[:, :, :]))
            link.run(dve.memset(until[:, :], -1.0))
            link.run(dve.memset(skip[:, :], 0.0))
            link.run(dve.scalar_tensor_tensor(junk[0:1, 0:EB], tiles[:, 1, :], 1.0, tiles[:, 0, :], ALU.add, ALU.subtract))
            link.run(dve.tensor_tensor_scan(until[:, 1:W], one[:, 1:W], junk[0:1, 0:EB], 0.0, ALU.mult, ALU.add))
            link.run(dve.tensor_copy(skip[:, 0:1], tiles[:, 0, 0:1]))
            if EB > 1:
                link.run(dve.scalar_tensor_tensor(skip[:, 1:EB], tiles[:, 0, 1:EB], -1.0, tiles[:, 1, 0:EB - 1],
                                                  ALU.add, ALU.subtract))
            dve.sem_inc(rows_up, 1)
            for n, (a, w) in enumerate(chunks * 2):
                dve.wait_ge(edges_in, n + 1)
                out = until_b if n < len(chunks) else skip_b
                dve.tensor_copy(out[:, a:a + w], bcast[:, n % 2, 0:w]).then_inc(broad, 1)
            dve.wait_ge(broad, 2 * len(chunks))
            dve.sem_inc(lists, 1)
            for c in range(NC):
                link.run(dve.scalar_tensor_tensor(junk[:, :], until_b[:, :], number[:, c:c + 1], ones_b[:, :],
                                                  ALU.is_le, ALU.mult, accum_out=count[:, c:c + 1]))
                link.run(dve.scalar_tensor_tensor(junk[:, :], until_b[:, :], number[:, c:c + 1], skip_b[:, :],
                                                  ALU.is_le, ALU.mult, accum_out=tile_v[:, c:c + 1]))
            link.run(dve.tensor_scalar(block_f[:, :], count[:, :], -1.0, EB - 1.0, ALU.add, ALU.min))
            dve.tensor_copy(block_i[:, :], block_f[:, :]).then_inc(lists, 1)
            link.run(dve.tensor_tensor(tile_v[:, :], tile_v[:, :], number[:, :], ALU.add))
            link.run(dve.tensor_scalar(tile_c[:, :], tile_v[:, :], S.NT - 1.0, None, ALU.min))
            link.run(dve.tensor_scalar(tile_m[:, :], tile_v[:, :], -float(P), None, ALU.mult))
            dve.tensor_copy(tile_i[:, :], tile_c[:, :]).then_inc(lists, 1)
            dve.wait_ge(got, 2 * NC * 16)
            dve.tensor_copy(dst_f[:, :, :], rows_d[:, :, :]).then_inc(local_up, 1)
            link.run(dve.tensor_copy(src_f[:, :, :], rows_s[:, :, :]))
            dve.wait_ge(local_up, 1)
            link.run(dve.tensor_tensor(local[:, :, :], dst_f[:, :, :], tile_m[:, :].unsqueeze(2).broadcast_to([P, NC, P]), ALU.add))
            dve.tensor_copy(local_h[:, :, :], local[:, :, :]).then_inc(local_up, 2)
            dve.wait_ge(prevs, 16)
            link.run(dve.tensor_tensor(same[:, :, :], dst_f[:, :, :], prev_f[:, :, :], ALU.is_equal))
            link.run(dve.tensor_copy(same0[:, :], same[:, :, 0]))
            link.run(dve.tensor_scalar(same[:, :, :], same[:, :, :], -1.0, BIG, ALU.add, ALU.mult))
            dve.tensor_reduce(alike[:, :], same[:, :, 1:P], AX.X, ALU.min)
            dve.tensor_reduce(whole[:, :], same[:, :, :], AX.X, ALU.min).then_inc(cols, 1)


def attention_weights(nc, K, M, W_dram, al, ar, Waug, layer):
    with ExitStack() as ctx:
        sb, ps, sem = allocators(nc, ctx, f"weights{layer}", M.context)
        w = sb("w", [P, 2, F])
        a = sb("a", [P, 2, F])
        prod = sb("prod", [P, 2, 2, F])
        loaded, linked = sem("w_loaded"), sem("dve_linked")
        block = phase_block(nc, ctx, sem)

        @block.sync
        def _(sp):
            sp.dma_start(w[:, :, :], W_dram.rearrange("(k p) f -> p k f", p=P)).then_inc(loaded, 16)
            for n, v in enumerate((al, ar)):
                row = v.rearrange("(o h) d -> o (h d)", o=1)
                sp.dma_start(a[:, n, :], row.broadcast_to([P, F])).then_inc(loaded, 16)

        @block.vector
        def _(dve):
            link = Linked(dve, linked)
            dve.wait_ge(loaded, 48)
            for k in range(2):
                row = Waug[:, k, 0:ROW].rearrange("p (h d) -> p h d", d=HW)
                dve.tensor_copy(row[:, :, 0:D], w[:, k, :].rearrange("p (h d) -> p h d", d=D))
                for n in range(2):
                    link.run(dve.tensor_tensor(prod[:, k, n, :], w[:, k, :], a[:, n, :], ALU.mult))
                    out = row[:, :, D] if n == 0 else Waug[:, k, ROW:ROW + H]
                    link.run(dve.tensor_reduce(out, prod[:, k, n, :].rearrange("p (h d) -> p h d", d=D), AX.X, ALU.add))


class Nodes:

    def __init__(self, S):
        self.S, self.turns = S, (S.NT - 2) // (2 * G4)
        self.last = (S.NT - 2, 2 * self.turns, 0, 2, S.LAST)

    def at(self, j, k):
        return j * (2 * G4) + k * G4, j * 2 + k, k % 2, G4, P

    def run(self, eng, group):
        with eng.Fori(0, self.turns) as j:
            for k in range(2):
                group(*self.at(j, k))
        group(*self.last)

    def skewed(self, eng, stages):
        first, second, third = [stages[n] if n < len(stages) else lambda *_: None for n in range(3)]

        def together(*runs):
            runs = [r for r in runs if r is not None]
            while runs:
                runs = [r for r in runs if next(r, self) is not self]

        together(first(*self.at(0, 0)))
        together(first(*self.at(0, 1)), second(*self.at(0, 0)))
        with eng.Fori(0, self.turns - 1) as j:
            for k in range(2):
                together(first(*self.at(j, k + 2)), second(*self.at(j, k + 1)))
                third(*self.at(j, k))
        j = self.turns - 1
        together(first(*self.last), second(*self.at(j, 1)))
        third(*self.at(j, 0))
        together(second(*self.last))
        third(*self.at(j, 1))
        third(*self.last)


def hold(eng, sem, value, passed):
    eng.wait_ge(sem, value)
    eng.sem_inc(passed, 1)


def half(g, p):
    return g // 2 if isinstance(g, int) else (g - p) // 2


def tiles_of(table, tile, n):
    return table[bass.ds(tile * P, n * P), :].rearrange("(k p) f -> p k f", p=P)


def load_tiles(eng, buf, p, table, tile, n, rows, done):
    eng.dma_start(buf[:, p, 0:n - 1, :], tiles_of(table, tile, n - 1)).then_inc(done, 16)
    eng.dma_start(buf[0:rows, p, n - 1, :], table[bass.ds((tile + n - 1) * P, rows), :]).then_inc(done, 16)


def by_tile_and_head(acc, tile, n):
    return acc[:, bass.ds(tile * ROW, n * ROW)].rearrange("p (k h d) -> p k h d", h=H, d=HW)


def project_nodes(nc, S, K, M, first, x, Waug, er3, acc):
    NT = S.NT
    nodes = Nodes(S)
    with ExitStack() as ctx:
        sb, ps, sem = allocators(nc, ctx, "project1" if first else "project2", M.context)
        xin = sb("xin", [P, 2, G4, F]) if first else None
        stats = sb("stats", [P, 2, G4, nc.vector.BN_STATS_DIM])
        mv = sb("mv", [P, 2, G4, 2])
        den = sb("den", [P, 2, G4, H])
        dev = sb("dev", [P, 2, G4])
        scale = sb("scale", [P, 2, G4])
        shift = sb("shift", [P, 2, G4])
        low = sb("low", [P, 2, G4, F])
        h = sb("h", [P, 2, G4, F])
        hT = sb("hT", [P, 2, G4, F])
        row = sb("row", [P, 2, G4, ROW])
        er = sb("er", [P, NT, H])
        rest = sb("rest", [P, NT, H])
        psT = ps("psT", [P, 2, 512])
        psF = ps("psF", [P, G4, 512])
        (used, moments, devs, scales, h_up, low_up, exp_up, turned, hT_up, products, kept, h_free, row_free,
         linked, cleared) = (sem(n) for n in (
             "x_used", "moments", "devs", "scales", "h_up", "low_up", "exp_up", "turned", "hT_up",
             "products", "rows_kept", "h_free", "row_free", "dve_linked", "cleared"))
        split, passed = sem("split"), sem("passed")
        loaded = [sem("loaded0"), sem("loaded1")]
        h_stored, row_stored = ([sem.lasting(f"{n}_stored{p}") for p in range(2)] for n in ("h", "row"))
        TURNED = 2 * G4
        block = phase_block(nc, ctx, sem)

        @block.sync
        def _(sp):
            def group(tile, g, p, n, rows):
                sp.wait_ge(used, g + 1)
                if rows != P:
                    sp.wait_ge(cleared, 1)
                load_tiles(sp, xin, p, x, tile, n, rows, loaded[p])
            if first:
                nodes.run(sp, group)

        @block.gpsimd
        def _(pool):
            def output(tile, g, p, n, rows):
                if not first:
                    hold(pool, h_up, g + 1, passed)
                    pool.dma_start(tiles_of(M.h2, tile, n), h[:, p, 0:n, :]).then_inc(h_stored[p], 16)
                    pool.wait_ge(h_stored[p], half(g, p) * 16 + 16)
                    pool.sem_inc(h_free, 1)

            def table(tile, g, p, n, rows):
                hold(pool, kept, tile + n + G4, passed)
                pool.dma_start(tiles_of(M.table, tile, n), row[:, p, 0:n, :]).then_inc(row_stored[p], 16)
                pool.wait_ge(row_stored[p], half(g, p) * 16 + 16)
                pool.sem_inc(row_free, 1)
            nodes.skewed(pool, [output, table])

        @block.tensor
        def _(pe):
            def product(T, p, k):
                pe.wait_ge(hT_up, T + 3)
                pe.wait_ge(kept, T + 1)
                for c in range(2):
                    mm = pe.matmul(psF[:, k, 0:ROW + H], hT[:, p, k, c * P:c * P + P], Waug[:, c, :],
                                   start=(c == 0), stop=(c == 1))
                mm.then_inc(products, 1)

            def turn(T, g, p, k):
                pe.wait_ge(h_up, T + 1 if first else g + 1)
                if not (isinstance(T, int) and T < 2):
                    pe.wait_ge(hT_up, T + 1)
                for c in range(2):
                    mm = pe.transpose(psT[:, k % 2, c * P:c * P + P], h[:, p, k, c * P:c * P + P], K.ident[:, :])
                mm.then_inc(turned, 1)

            turn(0, 0, 0, 0)
            turn(1, 0, 0, 1)

            def group(tile, g, p, n, rows):
                for k in range(n):
                    if k + 2 < n:
                        turn(tile + (k + 2), g, p, k + 2)
                    elif n == G4:
                        turn(tile + (k + 2), g + 1, 1 - p, k + 2 - n)
                    product(tile + k, p, k)
            nodes.run(pe, group)

        @block.scalar
        def _(act):
            act.sem_inc(hT_up, 2)
            if first:
                act.sem_inc(used, 2)

            def front(tile, g, p, n, rows):
                if first:
                    act.wait_ge(moments, g + 1)
                    act.activation(dev[:, p, 0:n], mv[:, p, 0:n, 1], ACT.Sqrt, bias=K.eps[:, 0:1]).then_inc(devs, 1)
                    act.wait_ge(scales, g + 1)
                    act.wait_ge(turned, tile + (TURNED - G4))
                    for k in range(n):
                        act.activation(h[:, p, k, :], xin[:, p, k, :], ACT.Relu, bias=shift[:, p, k:k + 1],
                                       scale=scale[:, p, k:k + 1]).then_inc(h_up, 1)
                        yield
                    act.wait_ge(h_up, tile + n)
                    act.sem_inc(used, 1)
                else:
                    act.wait_ge(low_up, g + 1)
                    act.activation(low[:, p, 0:n, :], low[:, p, 0:n, :], ACT.Exp).then_inc(exp_up, 1)

            def back(tile, g, p, n, rows):
                for k in range(n):
                    act.wait_ge(turned, tile + k + (1 + TURNED))
                    act.activation(hT[:, p, k, :], psT[:, k % 2, 0:F], ACT.Copy).then_inc(hT_up, 1)
                    yield
            nodes.skewed(act, [front, back])

        @block.vector
        def _(dve):
            dve.sem_inc(kept, G4)
            dve.sem_inc(turned, TURNED)
            dve.sem_inc(h_free, 2)
            dve.sem_inc(row_free, 2)
            per = 2 if first else 3

            def normal(tile, g, p, n, rows):
                link = LoopLinked(dve, linked, g, per)
                if rows != P:
                    dve.wait_ge(used, g + 1)
                    dve.memset(xin[:, p, n - 1, :], 0.0).then_inc(cleared, 1)
                dve.wait_ge(loaded[p], half(g, p) * 32 + 32)
                for k in range(n):
                    ins = dve.bn_stats(stats[:, p, k, :], xin[:, p, k, :])
                link.run(ins)
                dve.sem_inc(passed, 1)
                for k in range(n):
                    ins = dve.bn_aggr(mv[:, p, k, :], stats[:, p, k, :])
                ins.then_inc(moments, 1)
                dve.wait_ge(devs, g + 1)
                dve.wait_ge(moments, g + 1)
                link.run(dve.reciprocal(scale[:, p, 0:n], dev[:, p, 0:n]))
                dve.scalar_tensor_tensor(shift[:, p, 0:n], mv[:, p, 0:n, 0], -1.0, scale[:, p, 0:n], ALU.mult, ALU.mult)\
                    .then_inc(scales, 1)

            def mean(tile, g, p, n, rows):
                link = LoopLinked(dve, linked, g, per)
                dve.wait_ge(h_free, g + 1)
                dve.wait_ge(turned, tile + (TURNED - G4))
                sums = by_tile_and_head(acc, tile, n)
                link.run(dve.tensor_scalar(den[:, p, 0:n, :], sums[:, :, :, D], 1e-30, None, ALU.max))
                link.run(dve.reciprocal(den[:, p, 0:n, :], den[:, p, 0:n, :]))
                link.run(dve.tensor_tensor(h[:, p, 0:n, :].rearrange("p k (h d) -> p k h d", d=D), sums[:, :, :, 0:D],
                                           den[:, p, 0:n, :].unsqueeze(3).broadcast_to([P, n, H, D]), ALU.mult))
                dve.tensor_scalar(low[:, p, 0:n, :], h[:, p, 0:n, :], 0.0, None, ALU.min).then_inc(low_up, 1)

            def elu(tile, g, p, n, rows):
                dve.wait_ge(exp_up, g + 1)
                dve.scalar_tensor_tensor(h[:, p, 0:n, :], low[:, p, 0:n, :], -1.0, h[:, p, 0:n, :], ALU.add, ALU.max).then_inc(h_up, 1)

            def keep(tile, g, p, n, rows):
                dve.wait_ge(row_free, g + 1)
                for k in range(n):
                    dve.wait_ge(products, tile + k + 1)
                    dve.tensor_copy(er[:, bass.ds(tile + k, 1), :], psF[:, k, ROW:ROW + H].unsqueeze(1))
                    dve.tensor_copy(row[:, p, k, :], psF[:, k, 0:ROW]).then_inc(kept, 1)

            if first:
                nodes.skewed(dve, [normal, keep])
            else:
                nodes.skewed(dve, [mean, elu, keep])
            dve.wait_ge(kept, NT + G4)
            link = Linked(dve, split)
            link.run(dve.tensor_copy(er3[:, :, 0, :], er[:, :, :]))
            link.run(dve.tensor_tensor(rest[:, :, :], er[:, :, :], er3[:, :, 0, :], ALU.subtract))
            link.run(dve.tensor_copy(er3[:, :, 1, :], rest[:, :, :]))
            link.run(dve.tensor_tensor(er3[:, :, 2, :], rest[:, :, :], er3[:, :, 1, :], ALU.subtract))


def attend(nc, S, K, M, er3, acc, layer, attr=None):
    NI = S.NI
    TABLES = 6
    with ExitStack() as ctx:
        sb, ps, sem = allocators(nc, ctx, f"attend{layer}", M.context)
        G = sb("G", [P, 2, U, ROW])
        hot = sb("hot", [P, 2, U, P])
        hotT = sb("hotT", [P, U, P], BF16)
        index = sb("index", [P, 2, U], I32)
        local_b = sb("local_b", [P, 2, U * P], BF16)
        local_c = sb("local_c", [P, 2, U])
        apart = sb("apart", [R, 2, P + 1])
        whole = sb("whole", [H, 2, U])
        alike = sb("alike", [H, 2, U])
        goes_on = sb("goes_on", [H, 2, U + 1])
        tile_r = sb("tile_r", [1, S.V], I32)
        er = sb("er", [P, R])
        run = sb("run", [R, P])
        top = sb("top", [R, P])
        ends = sb("ends", [R, 2, U])
        last = sb("last", [H, 1])
        carry = sb("carry", [H, U + 1])
        back = sb("back", [H, U + 1])
        around = sb("around", [H, 2, U])
        through = sb("through", [H, 2, U])
        spread = sb("spread", [R, 2, U])
        start = sb("start", [R, 2])
        low = sb("low", [P, R])
        high = sb("high", [P, R])
        low2 = sb("low2", [P, R])
        high2 = sb("high2", [P, R])
        diff = sb("diff", [P, R])
        old = sb("old", [1, 3, H])
        shrink = sb("shrink", [1, 2 * H])
        first_n = sb("first_n", [P, 1])
        other = sb("other", [P, H])
        same = sb("same", [P, H])
        keep = sb("keep", [P, 2, H])
        psP = ps("psP", [P, BANKS, 512])
        psA = ps("psA", [P, 512])
        psE = ps("psE", [P, 512])
        psR = ps("psR", [P, 512])
        psS = ps("psS", [P, 512])
        elT, ends_p, start_p = psA[0:R, 0:P], psA[0:H, P:P + 2 * U], psA[0:R, 2 * P:2 * P + 2 * U]
        er_p = psE[:, 0:3 * R].rearrange("p (u k h) -> p u h k", k=3, h=H)
        top_p, old_p, keep_p = psR[:, 0:R], psR[0:1, P:P + R], psS[:, 0:2 * H]
        index_up, tables_up = ([sem(f"{n}{p}") for p in range(2)] for n in ("index_up", "tables_up"))
        gathered = [sem.lasting(f"gathered{p}") for p in range(2)]
        (tiles_up, hotT_up, hot_up, el_turned, er_up, ends_up, ends_in, around_up, start_in, top_up, top_turned,
         diff_up, weights_up, shrink_up, shrunk_up, keep_in, keep_up, weighed, summed, added, linked) = (sem(n) for n in (
             "tiles_up", "hotT_up", "hot_up", "el_turned", "er_up", "ends_up", "ends_in", "around_up", "start_in",
             "top_up", "top_turned", "diff_up", "weights_up", "shrink_up", "shrunk_up", "keep_in", "keep_up", "weighed",
             "summed", "added", "dve_linked"))
        ready = sem("ready")
        passed_pe, passed_pool = sem("passed_pe"), sem("passed_pool")
        CREDIT = BANKS
        block = phase_block(nc, ctx, sem)

        def el_of(p):
            return G[:, p, :, :].rearrange("p u (h d) -> p (u h) d", d=HW)[:, :, D]

        @block.sync
        def _(sp):
            def tables(i, p):
                v = i * U
                sp.dma_start(index[:, p, :], M.src_col[:, bass.ds(v, U)]).then_inc(index_up[p], 16)
                row = M.local_row[bass.ds(v * P, U * P)].rearrange("(o n) -> o n", o=1)
                sp.dma_start(local_b[:, p, :], row.broadcast_to([P, U * P])).then_inc(tables_up[p], 16)
                sp.dma_start(local_c[:, p, :], M.local_col[:, bass.ds(v, U)]).then_inc(tables_up[p], 16)
                sp.dma_start(apart[:, p, 0:P], M.apart[bass.ds(v * H, R), :]).then_inc(tables_up[p], 16)
                for out, table, w in ((whole, M.whole, U), (alike, M.alike, U), (goes_on, M.goes_on, U + 1)):
                    line = table[bass.ds(v, w)].rearrange("(o n) -> o n", o=1)
                    sp.dma_start(out[:, p, :], line.broadcast_to([H, w])).then_inc(tables_up[p], 16)

            sp.dma_start(tile_r[:, :], M.tile.rearrange("(o n) -> o n", o=1)).then_inc(tiles_up, 16)
            tables(0, 0)
            tables(1, 1)
            with sp.Fori(0, NI // 2) as j:
                for p in range(2):
                    i = j * 2 + p
                    sp.wait_ge(gathered[p], j * (16 * U) + 16 * U)
                    sp.wait_ge(shrunk_up, i + 1)
                    sp.wait_ge(hot_up, 4 * i + 4)
                    tables(i + 2, p)
                    if attr is not None:
                        share = bass.ds(i * S.share, S.share)
                        sp.dma_start(M.attr[share, :].rearrange("(a b) f -> a (b f)", a=16),
                                     attr[share, :].rearrange("(a b) f -> a (b f)", a=16)).then_inc(M.attr_up, 16)
            if attr is not None and NI * S.share < S.E:
                sp.dma_start(M.attr[NI * S.share:S.E, :], attr[NI * S.share:S.E, :]).then_inc(M.attr_up, 16)
            sp.wait_ge(tiles_up, 16)
            for p in range(2):
                sp.wait_ge(tables_up[p], (NI // 2 + 1) * 16 * TABLES)
                sp.wait_ge(index_up[p], (NI // 2 + 1) * 16)

        @block.gpsimd
        def _(pool):
            def gather(j, p, before=None):
                hold(pool, index_up[p], j * 16 + 16, passed_pool)
                for u in range(U):
                    if before is not None and u % 2 == 0:
                        hold(pool, summed, before * U + u + 2, passed_pool)
                    pool.indirect_dma_start(G[:, p, u, :], None, M.table, bass.IndirectOffsetOnAxis(index[:, p, u:u + 1], 0))\
                        .then_inc(gathered[p], 16)
            gather(0, 0)
            gather(0, 1)
            with pool.Fori(0, NI // 2) as j:
                for p in range(2):
                    gather(j + 1, p, j * 2 + p)
            for p in range(2):
                pool.wait_ge(gathered[p], (NI // 2 + 1) * 16 * U)

        @block.tensor
        def _(pe):
            regs = [pe.alloc_register(f"pe{layer}_tile{u}") for u in range(U)]
            parts = er3.rearrange("p t k h -> p (t k h)")

            def prepare(i, p, j):
                pe.load(regs, tile_r[0:1, bass.ds(i * U, U)])
                hold(pe, gathered[p], j * (16 * U) + 16 * U, passed_pe)
                pe.transpose(elT, el_of(p), K.ident[:, :]).then_inc(el_turned, 1)
                yield
                pe.wait_ge(hotT_up, i + 1)
                for u in range(U):
                    t = pe.snap(regs[u], min_val=0, max_val=S.NT - 1)
                    mm = pe.matmul(psE[:, u * 3 * H:u * 3 * H + 3 * H], hotT[:, u, :], parts[:, bass.ds(t * (3 * H), 3 * H)],
                                   start=True, stop=True)
                mm.then_inc(er_up, 1)
                yield
                hold(pe, ends_up, i + 1, passed_pe)
                pe.matmul(ends_p, K.head_of[:, :], ends[:, :, :], start=True, stop=True).then_inc(ends_in, 1)
                yield
                hold(pe, around_up, i + 1, passed_pe)
                pe.matmul(start_p, K.rows_of[:, :], around[:, :, :], start=True, stop=True).then_inc(start_in, 1)
                yield
                hold(pe, top_up, i + 1, passed_pe)
                pe.transpose(top_p, top[:, :], K.ident[0:R, 0:R])
                pe.transpose(old_p, start[:, 0:1], K.ident[0:R, 0:R]).then_inc(top_turned, 1)
                yield
                hold(pe, shrunk_up, i + 1, passed_pe)
                pe.matmul(keep_p, K.ones[:, :], shrink[:, :], start=True, stop=True).then_inc(keep_in, 1)
                yield

            def sums(i, p, u):
                pe.wait_ge(weighed, i * U + u + 1)
                pe.wait_ge(added, i * U + u + 1)
                pe.matmul(psP[:, u % BANKS, 0:ROW], hot[:, p, u, :], G[:, p, u, :], start=True, stop=True).then_inc(summed, 1)

            pe.wait_ge(tiles_up, 16)
            pe.wait_ge(ready, 1)
            for _ in prepare(0, 0, 0):
                pass
            after = {5, 6, 7, 9, 11, 15}
            with pe.Fori(0, NI // 2) as j:
                for p in range(2):
                    i = j * 2 + p
                    steps = prepare(i + 1, 1 - p, j + p)
                    pe.wait_ge(hot_up, 4 * i + 4)
                    for u in range(U):
                        sums(i, p, u)
                        if u in after:
                            next(steps, None)
                    for _ in steps:
                        pass

        @block.scalar
        def _(act):
            def weights(i, p):
                act.wait_ge(diff_up, i + 1)
                act.activation(shrink[:, 0:H], old[:, 2, :], ACT.Exp).then_inc(shrink_up, 1)
                act.activation(el_of(p), diff[:, :], ACT.Exp).then_inc(weights_up, 1)

            weights(0, 0)
            with act.Fori(0, NI // 2) as j:
                for p in range(2):
                    i = j * 2 + p
                    act.wait_ge(weights_up, i + 1)
                    for u in range(U):
                        for h in range(H):
                            row = G[:, p, u, h * HW:h * HW + D]
                            ins = act.activation(row, row, ACT.Copy, scale=G[:, p, u, h * HW + D:h * HW + HW])
                        ins.then_inc(weighed, 1)
                        if u == U - 1:
                            weights(i + 1, 1 - p)

        @block.vector
        def _(dve):
            regs = [dve.alloc_register(f"dve{layer}_tile{u}") for u in range(U)]
            LINKS = 16

            def one_hot(p, j):
                dve.wait_ge(tables_up[p], j * (16 * TABLES) + 16 * TABLES)
                for n in range(0, U, U // 4):
                    part = slice(n, n + U // 4)
                    dve.tensor_tensor(hot[:, p, part, :], K.col[:, :].unsqueeze(1).broadcast_to([P, U // 4, P]),
                                      local_c[:, p, part].unsqueeze(2).broadcast_to([P, U // 4, P]), ALU.is_equal).then_inc(hot_up, 1)
                    yield

            def prepare(i, p, j):
                link = LoopLinked(dve, linked, i, LINKS)
                dve.wait_ge(tables_up[p], j * (16 * TABLES) + 16 * TABLES)
                dve.tensor_scalar(hotT[:, :, :].rearrange("p u e -> p (u e)"), local_b[:, p, :], K.row[:, 0:1], None, ALU.is_equal)\
                    .then_inc(hotT_up, 1)
                link.run(dve.tensor_scalar(through[:, 0, :], goes_on[:, p, 1:U + 1], -1.0, BIG, ALU.add, ALU.mult))
                dve.tensor_tensor(through[:, 1, :], through[:, 0, :], alike[:, p, :], ALU.add)
                yield
                dve.wait_ge(el_turned, i + 1)
                link.run(dve.tensor_tensor_scan(run[:, :], apart[:, p, 0:P], elT, -BIG, ALU.add, ALU.max))
                link.run(dve.tensor_tensor_scan(top[:, ::-1], apart[:, p, P:0:-1], run[:, ::-1], -BIG, ALU.add, ALU.max))
                dve.tensor_scalar(ends[:, 0, :], K.visit_of[:, :], run[:, P - 1:P], None, ALU.mult)
                dve.tensor_scalar(ends[:, 1, :], K.visit_of[:, :], top[:, 0:1], None, ALU.mult).then_inc(ends_up, 1)
                yield
                dve.wait_ge(ends_in, i + 1)
                link.run(dve.tensor_copy(last[:, :], carry[:, U:U + 1]))
                dve.tensor_copy(carry[:, 0:1], last[:, :])
                dve.tensor_tensor_scan(carry[:, 1:U + 1], whole[:, p, :], ends_p[:, 0:U], last[:, 0:1], ALU.add, ALU.max)
                link.run(dve.tensor_tensor_scan(back[:, U - 1::-1], through[:, 1, ::-1], ends_p[:, 2 * U - 1:U - 1:-1], -BIG, ALU.add, ALU.max))
                dve.tensor_copy(around[:, 0, :], carry[:, 0:U])
                dve.tensor_tensor(around[:, 1, :], through[:, 0, :], back[:, 1:U + 1], ALU.add).then_inc(around_up, 1)
                yield
                dve.wait_ge(er_up, i + 1)
                link.run(dve.tensor_reduce(er[:, :].rearrange("p (u h) -> p u h", h=H), er_p, AX.X, ALU.add))
                link.run(dve.tensor_tensor(low[:, :], el_of(p), er[:, :], ALU.add))
                dve.scalar_tensor_tensor(low2[:, :], low[:, :], SLOPE, low[:, :], ALU.mult, ALU.max)
                yield
                dve.wait_ge(start_in, i + 1)
                link.run(dve.tensor_tensor(spread[:, :, :], start_p.rearrange("r (k u) -> r k u", k=2),
                                           K.visit_of[:, :].unsqueeze(1).broadcast_to([R, 2, U]), ALU.mult))
                link.run(dve.tensor_reduce(start[:, :], spread[:, :, :], AX.X, ALU.add))
                link.run(dve.tensor_tensor_scan(run[:, :], apart[:, p, 0:P], elT, start[:, 0:1], ALU.add, ALU.max))
                dve.tensor_tensor_scan(top[:, ::-1], apart[:, p, P:0:-1], run[:, ::-1], start[:, 1:2], ALU.add, ALU.max).then_inc(top_up, 1)
                yield
                dve.wait_ge(top_turned, i + 1)
                link.run(dve.tensor_tensor(high[:, :], top_p, er[:, :], ALU.add))
                dve.tensor_tensor(old[:, 0, :], old_p[:, 0:H], er[0:1, 0:H], ALU.add)
                link.run(dve.scalar_tensor_tensor(high2[:, :], high[:, :], SLOPE, high[:, :], ALU.mult, ALU.max))
                link.run(dve.scalar_tensor_tensor(old[:, 1, :], old[:, 0, :], SLOPE, old[:, 0, :], ALU.mult, ALU.max))
                link.run(dve.tensor_tensor(old[:, 2, :], old[:, 1, :], high2[0:1, 0:H], ALU.subtract))
                dve.tensor_scalar(old[:, 2, :], old[:, 2, :], 0.0, None, ALU.min)
                dve.tensor_tensor(diff[:, :], low2[:, :], high2[:, :], ALU.subtract).then_inc(diff_up, 1)
                yield
                dve.wait_ge(shrink_up, i + 1)
                dve.tensor_copy(shrink[:, H:2 * H], goes_on[0:1, p, 0:1].broadcast_to([1, H]))
                dve.tensor_scalar(shrink[:, 0:H], shrink[:, 0:H], goes_on[0:1, p, 0:1], None, ALU.mult).then_inc(shrunk_up, 1)
                yield
                link.run(dve.tensor_copy(first_n[:, :], hotT[:, 0, 0:1]))
                dve.wait_ge(keep_in, i + 1)
                dve.tensor_scalar(other[:, :], keep_p[:, H:2 * H], first_n[:, 0:1], -1.0, ALU.mult, ALU.mult)
                link.run(dve.tensor_scalar(same[:, :], keep_p[:, 0:H], first_n[:, 0:1], None, ALU.mult))
                dve.scalar_tensor_tensor(keep[:, p, :], other[:, :], 1.0, same[:, :], ALU.add, ALU.add).then_inc(keep_up, 1)
                assert link.n == LINKS, link.n
                yield

            def add(i, p, u):
                t = dve.snap(regs[u], min_val=0, max_val=S.NT - 1)
                if u == 0:
                    dve.wait_ge(keep_up, i + 1)
                dve.wait_ge(summed, i * U + u + 1)
                dve.wait_ge(added, i * U + (u + CREDIT))
                if u == 0:
                    for h in range(H):
                        s = acc[:, bass.ds(t * ROW + h * HW, HW)]
                        ins = dve.scalar_tensor_tensor(s, s, keep[:, p, h:h + 1], psP[:, u % BANKS, h * HW:h * HW + HW],
                                                       ALU.mult, ALU.add)
                else:
                    s = acc[:, bass.ds(t * ROW, ROW)]
                    ins = dve.tensor_tensor(s, s, psP[:, u % BANKS, 0:ROW], ALU.add)
                ins.then_inc(added, 1)

            dve.memset(apart[:, :, P:P + 1], 0.0)
            dve.memset(back[:, :], -BIG)
            dve.memset(carry[:, :], -BIG).then_inc(ready, 1)
            dve.wait_ge(ready, 1)
            dve.memset(acc[:, :], 0.0).then_inc(added, CREDIT)
            dve.wait_ge(tiles_up, 16)
            for _ in one_hot(0, 0):
                pass
            for _ in prepare(0, 0, 0):
                pass
            after, hot_after = {0, 4, 5, 6, 8, 10, 12, 14}, {1, 2, 3, 13}
            with dve.Fori(0, NI // 2) as j:
                for p in range(2):
                    i = j * 2 + p
                    steps = prepare(i + 1, 1 - p, j + p)
                    hots = one_hot(1 - p, j + p)
                    dve.load(regs, tile_r[0:1, bass.ds(i * U, U)])
                    for u in range(U):
                        add(i, p, u)
                        if u in hot_after:
                            next(hots, None)
                        if u in after:
                            next(steps, None)
                    for _ in steps:
                        pass
            dve.wait_ge(added, NI * U + CREDIT)


def renew_nodes(nc, S, K, M, x, acc):
    nodes = Nodes(S)
    with ExitStack() as ctx:
        sb, ps, sem = allocators(nc, ctx, "renew", M.context)
        xin = sb("xin", [P, 2, G4, F])
        hin = sb("hin", [P, 2, G4, F])
        q = sb("q", [P, 2, G4, F])
        low = sb("low", [P, 2, G4, F])
        r = sb("r", [P, 2, G4, F])
        h = sb("h", [P, 2, G4, F])
        xh = sb("xh", [P, 2, G4, F])
        stats = sb("stats", [P, 2, G4, nc.vector.BN_STATS_DIM])
        mv = sb("mv", [P, 2, G4, 2])
        den = sb("den", [P, 2, G4, H])
        dev = sb("dev", [P, 2, G4])
        scale = sb("scale", [P, 2, G4])
        shift = sb("shift", [P, 2, G4])
        x_used, h_used, moments, devs, scales, h_up, low_up, exp_up, xh_up, out_free, mean_linked, elu_linked, cleared = (
            sem(n) for n in ("x_used", "h_used", "moments", "devs", "scales", "h_up", "low_up", "exp_up", "xh_up",
                             "out_free", "mean_linked", "elu_linked", "cleared"))
        passed = sem("passed")
        x_loaded, h_loaded = ([sem(f"{n}_loaded{p}") for p in range(2)] for n in ("x", "h"))
        stored = [sem.lasting("stored0"), sem.lasting("stored1")]
        block = phase_block(nc, ctx, sem)

        @block.sync
        def _(sp):
            def load_h(tile, g, p, n, rows):
                sp.wait_ge(h_used, g + 1)
                sp.dma_start(hin[:, p, 0:n, :], tiles_of(M.h2, tile, n)).then_inc(h_loaded[p], 16)

            def load_x(tile, g, p, n, rows):
                sp.wait_ge(x_used, g + 1)
                if rows != P:
                    sp.wait_ge(cleared, 1)
                load_tiles(sp, xin, p, x, tile, n, rows, x_loaded[p])
            nodes.skewed(sp, [load_h, load_x])

        @block.gpsimd
        def _(pool):
            def group(tile, g, p, n, rows):
                hold(pool, h_up, tile + n, passed)
                pool.dma_start(tiles_of(M.h3, tile, n), h[:, p, 0:n, :]).then_inc(stored[p], 16)
                hold(pool, xh_up, g + 3, passed)
                pool.dma_start(tiles_of(M.xh, tile, n), xh[:, p, 0:n, :]).then_inc(stored[p], 16)
                pool.wait_ge(stored[p], half(g, p) * 32 + 32)
                pool.sem_inc(out_free, 1)
            nodes.run(pool, group)

        @block.scalar
        def _(act):
            def exp(tile, g, p, n, rows):
                act.wait_ge(low_up, g + 1)
                act.activation(low[:, p, 0:n, :], low[:, p, 0:n, :], ACT.Exp).then_inc(exp_up, 1)

            def normal(tile, g, p, n, rows):
                act.wait_ge(moments, g + 1)
                act.activation(dev[:, p, 0:n], mv[:, p, 0:n, 1], ACT.Sqrt, bias=K.eps[:, 0:1]).then_inc(devs, 1)
                act.wait_ge(scales, g + 1)
                act.wait_ge(out_free, g + 1)
                for k in range(n):
                    act.activation(h[:, p, k, :], r[:, p, k, :], ACT.Relu, bias=shift[:, p, k:k + 1],
                                   scale=scale[:, p, k:k + 1]).then_inc(h_up, 1)
            nodes.skewed(act, [exp, normal])

        @block.vector
        def _(dve):
            dve.sem_inc(x_used, 2)
            dve.sem_inc(h_used, 2)
            dve.sem_inc(out_free, 2)
            dve.sem_inc(xh_up, 2)

            def mean(tile, g, p, n, rows):
                link = LoopLinked(dve, mean_linked, g, 4)
                sums = by_tile_and_head(acc, tile, n)
                link.run(dve.tensor_scalar(den[:, p, 0:n, :], sums[:, :, :, D], 1e-30, None, ALU.max))
                link.run(dve.reciprocal(den[:, p, 0:n, :], den[:, p, 0:n, :]))
                link.run(dve.tensor_tensor(q[:, p, 0:n, :].rearrange("p k (h d) -> p k h d", d=D), sums[:, :, :, 0:D],
                                           den[:, p, 0:n, :].unsqueeze(3).broadcast_to([P, n, H, D]), ALU.mult))
                dve.wait_ge(h_loaded[p], half(g, p) * 16 + 16)
                link.run(dve.tensor_tensor(q[:, p, 0:n, :], q[:, p, 0:n, :], hin[:, p, 0:n, :], ALU.add))
                dve.sem_inc(h_used, 1)
                dve.tensor_scalar(low[:, p, 0:n, :], q[:, p, 0:n, :], 0.0, None, ALU.min).then_inc(low_up, 1)

            def elu(tile, g, p, n, rows):
                link = LoopLinked(dve, elu_linked, g, 4)
                if rows != P:
                    dve.wait_ge(x_used, g + 1)
                    dve.memset(xin[:, p, n - 1, :], 0.0).then_inc(cleared, 1)
                dve.wait_ge(exp_up, g + 1)
                dve.wait_ge(xh_up, g + 1)
                link.run(dve.scalar_tensor_tensor(r[:, p, 0:n, :], low[:, p, 0:n, :], -1.0, q[:, p, 0:n, :], ALU.add, ALU.max))
                dve.wait_ge(x_loaded[p], half(g, p) * 32 + 32)
                link.run(dve.tensor_tensor(r[:, p, 0:n, :], r[:, p, 0:n, :], xin[:, p, 0:n, :], ALU.add))
                dve.sem_inc(x_used, 1)
                for k in range(n):
                    ins = dve.bn_stats(stats[:, p, k, :], r[:, p, k, :])
                link.run(ins)
                dve.sem_inc(passed, 1)
                for k in range(n):
                    ins = dve.bn_aggr(mv[:, p, k, :], stats[:, p, k, :])
                ins.then_inc(moments, 1)
                dve.wait_ge(devs, g + 1)
                link.run(dve.reciprocal(scale[:, p, 0:n], dev[:, p, 0:n]))
                dve.scalar_tensor_tensor(shift[:, p, 0:n], mv[:, p, 0:n, 0], -1.0, scale[:, p, 0:n], ALU.mult, ALU.mult)\
                    .then_inc(scales, 1)

            def add(tile, g, p, n, rows):
                dve.wait_ge(out_free, g + 1)
                dve.wait_ge(h_up, tile + n)
                dve.tensor_tensor(xh[:, p, 0:n, :], r[:, p, 0:n, :], h[:, p, 0:n, :], ALU.add).then_inc(xh_up, 1)
            nodes.skewed(dve, [mean, elu, add])


def split_bias(dve, link, K, out, b3, part, rest):
    link.run(dve.tensor_copy(part[:, :], b3[:, :]))
    for k in range(3):
        link.run(dve.tensor_scalar(rest[:, 1, :], part[:, :], K.col3[:, k:k + 1], None, ALU.mult))
        if k == 0:
            link.run(dve.tensor_copy(out[:, :], rest[:, 1, :]))
        else:
            link.run(dve.tensor_tensor(out[:, :], out[:, :], rest[:, 1, :], ALU.add))
        if k < 2:
            link.run(dve.tensor_tensor(b3[:, :], b3[:, :], part[:, :], ALU.subtract))
            link.run(dve.tensor_copy(part[:, :], b3[:, :]))


def split_exactly(dve, link, high, low, rest, x, done=None):
    link.run(dve.tensor_scalar(rest.bitcast(I32), x.bitcast(I32), -4096, None, ALU.bitwise_and))
    dve.tensor_copy(high, rest)
    ins = dve.tensor_tensor(low, x, rest, ALU.subtract)
    if done is None:
        link.run(ins)
    else:
        ins.then_inc(done, 1)


def pass_messages(nc, S, K, M, attr, W1_d, b1_d, W2_d, b2_d, acc):
    NI = S.NI
    Q = 4
    with ExitStack() as ctx:
        sb, ps, sem = allocators(nc, ctx, "messages", M.context)
        G = sb("G", [P, 2, U, F])
        hot = sb("hot", [P, 2, U, P])
        index = sb("index", [P, 2, U], I32)
        local_c = sb("local_c", [P, 2, U])
        rbf = sb("rbf", [P, 2, U, NR])
        halves = sb("halves", [P, 2, Q, 2, NR], F32R)
        leading = sb("leading", [P, Q, NR])
        rbfT = sb("rbfT", [P, Q * P], F32R)
        hidden = sb("hidden", [P, 2, 2, Q * P])
        gate = sb("gate", [P, 2, 2, F])
        tile_r = sb("tile_r", [1, S.V], I32)
        block_r = sb("block_r", [1, S.V], I32)
        W1 = sb("W1", [P, F])
        W1_part = sb("W1_part", [P, 2, F], F32R)
        W1_high = sb("W1_high", [P, F])
        W2 = sb("W2", [P, 2, F])
        b1 = sb("b1", [P, 2])
        b2 = sb("b2", [3, F])
        b2_3 = sb("b2_3", [3, F], BF16)
        part = sb("part", [3, F], BF16)
        rest = sb("rest", [3, 2, F])
        psX = ps("psX", [P, 512])
        psH = ps("psH", [P, 2, 512])
        psG = ps("psG", [P, 2, 512])
        psP = ps("psP", [P, 2, 2, F])
        index_up, tables_up = ([sem(f"{n}{p}") for p in range(2)] for n in ("index_up", "tables_up"))
        gathered = [sem.lasting(f"gathered{p}") for p in range(2)]
        (lists_up, weights_up, ready, hot_up, halves_up, turned, rbfT_up, hidden_in, hidden_up, gate_in, gate_up, weighed, summed,
         added, linked) = (sem(n) for n in (
             "lists_up", "weights_up", "ready", "hot_up", "halves_up", "attributes_turned", "rbfT_up", "hidden_in", "hidden_up", "gate_in",
             "gate_up", "weighed", "summed", "added", "dve_linked"))
        gate_free, passed_pool, halved = sem("gate_free"), sem("passed_pool"), sem("halved")
        CREDIT = 4
        block = phase_block(nc, ctx, sem)

        @block.sync
        def _(sp):
            regs = [sp.alloc_register(f"sp_block{u}") for u in range(U)]
            sp.dma_start(tile_r[:, :], M.tile.rearrange("(o n) -> o n", o=1)).then_inc(lists_up, 16)
            sp.dma_start(block_r[:, :], M.block.rearrange("(o n) -> o n", o=1)).then_inc(lists_up, 16)
            for n in range(2):
                sp.dma_start(W1[n * NR:n * NR + NR, :], W1_d).then_inc(weights_up, 16)
            sp.dma_start(W2[:, :, :], W2_d.rearrange("(k p) f -> p k f", p=P)).then_inc(weights_up, 16)
            sp.dma_start(b1[:, :].unsqueeze(2), b1_d.rearrange("(k p o) -> p k o", p=P, o=1), allow_slow_non_contiguous=True)\
                .then_inc(weights_up, 16)
            sp.dma_start(b2[:, :], b2_d.rearrange("(o f) -> o f", o=1).broadcast_to([3, F])).then_inc(weights_up, 16)
            sp.wait_ge(lists_up, 32)
            sp.wait_ge(M.attr_up, S.attr_copies * 16)

            def tables(i, p):
                sp.dma_start(index[:, p, :], M.src_col[:, bass.ds(i * U, U)]).then_inc(index_up[p], 16)
                sp.dma_start(local_c[:, p, :], M.local_col[:, bass.ds(i * U, U)]).then_inc(tables_up[p], 16)
                sp.load(regs, block_r[0:1, bass.ds(i * U, U)])
                for u in range(U):
                    b = sp.snap(regs[u], min_val=0, max_val=S.EB - 1)
                    sp.dma_start(rbf[:, p, u, :], attr[bass.ds(b * P, P), :]).then_inc(tables_up[p], 16)

            tables(0, 0)
            tables(1, 1)
            with sp.Fori(0, NI // 2) as j:
                for p in range(2):
                    i = j * 2 + p
                    sp.wait_ge(gathered[p], j * (16 * U) + 16 * U)
                    sp.wait_ge(hot_up, i * (U // Q) + U // Q)
                    sp.wait_ge(halves_up, i * (U // Q) + U // Q)
                    tables(i + 2, p)
            for p in range(2):
                sp.wait_ge(tables_up[p], (NI // 2 + 1) * 16 * (U + 1))
                sp.wait_ge(index_up[p], (NI // 2 + 1) * 16)

        @block.gpsimd
        def _(pool):
            def gather(j, p, before=None):
                hold(pool, index_up[p], j * 16 + 16, passed_pool)
                for u in range(U):
                    if before is not None:
                        hold(pool, summed, before * U + u + 1, passed_pool)
                    pool.indirect_dma_start(G[:, p, u, :], None, M.h3, bass.IndirectOffsetOnAxis(index[:, p, u:u + 1], 0))\
                        .then_inc(gathered[p], 16)
            gather(0, 0)
            gather(0, 1)
            with pool.Fori(0, NI // 2) as j:
                for p in range(2):
                    gather(j + 1, p, j * 2 + p)
            for p in range(2):
                pool.wait_ge(gathered[p], (NI // 2 + 1) * 16 * U)

        @block.tensor
        def _(pe):
            def turn(q, s):
                if not (isinstance(q, int) and q == 0):
                    pe.wait_ge(rbfT_up, q)
                pe.wait_ge(halves_up, q + 1)
                for k in range(Q):
                    both = halves[:, s % 2, k, :, :].rearrange("p a r -> p (a r)")
                    mm = pe.matmul(psX[:, k * P:k * P + P], both, K.ident_r[:, :], start=True, stop=True)
                mm.then_inc(turned, 1)

            def first(q):
                pe.wait_ge(rbfT_up, q + 1)
                if not (isinstance(q, int) and q == 0):
                    pe.wait_ge(hidden_up, 2 * q)
                for m in range(2):
                    for n in range(2):
                        mm = pe.matmul(psH[:, m, :], W1_part[:, n, m * P:m * P + P], rbfT[:, :],
                                       start=(n == 0), stop=(n == 1))
                    mm.then_inc(hidden_in, 1)

            def second(q, c, s):
                if c == 0:
                    pe.wait_ge(hidden_up, 2 * q + 2)
                pe.wait_ge(gate_up, 2 * q + c + 1)
                for k in range(2):
                    out = psG[:, c, k * F:k * F + F]
                    e = (c * 2 + k) * P
                    pe.matmul(out, K.ones3[:, :], b2_3[:, :], start=True, stop=False)
                    for m in range(2):
                        mm = pe.matmul(out, hidden[:, s % 2, m, e:e + P], W2[:, m, :], start=False, stop=(m == 1))
                mm.then_inc(gate_in, 1)

            def sums(q, p, s, c):
                pe.wait_ge(weighed, 2 * q + c + 1)
                pe.wait_ge(added, Q * q + (2 * c + 2))
                for k in range(2):
                    v = 2 * c + k
                    pe.matmul(psP[:, c, k, :], hot[:, p, s * Q + v, :], G[:, p, s * Q + v, :], start=True, stop=True).then_inc(summed, 1)

            pe.wait_ge(weights_up, 80)
            pe.wait_ge(ready, 1)
            turn(0, 0)
            first(0)
            turn(1, 1)
            second(0, 0, 0)
            first(1)
            second(0, 1, 0)
            with pe.Fori(0, NI // 2) as j:
                for p in range(2):
                    for s in range(U // Q):
                        q = j * (2 * U // Q) + (p * (U // Q) + s)
                        turn(q + 2, s)
                        second(q + 1, 0, s + 1)
                        pe.wait_ge(hot_up, q + 1)
                        sums(q, p, s, 0)
                        first(q + 2)
                        second(q + 1, 1, s + 1)
                        sums(q, p, s, 1)

        @block.scalar
        def _(act):
            def silus(q, s):
                for m in range(2):
                    act.wait_ge(hidden_in, 2 * q + m + 1)
                    act.activation(hidden[:, s, m, :], psH[:, m, :], ACT.Silu, bias=b1[:, m:m + 1]).then_inc(hidden_up, 1)

            def gates(q, c):
                act.wait_ge(gate_in, 2 * q + c + 1)
                act.wait_ge(gate_free, 2 * q + c + 1)
                act.activation(gate[:, c, :, :], psG[:, c, :], ACT.Tanh, scale=0.5).then_inc(gate_up, 1)

            def quad(q, s):
                gates(q, 0)
                silus(q + 1, 1 - s)
                gates(q, 1)

            act.sem_inc(gate_up, 2)
            act.wait_ge(weights_up, 80)
            silus(0, 0)
            with act.Fori(0, NI * (U // Q) // 2) as pair:
                for s in range(2):
                    quad(pair * 2 + s, s)
            quad(NI * (U // Q), 0)

        @block.vector
        def _(dve):
            link = Linked(dve, linked)
            dve.wait_ge(weights_up, 80)
            split_bias(dve, link, K, b2_3, b2, part, rest)
            dve.memset(acc[:, :], 0.0).then_inc(added, CREDIT)
            dve.sem_inc(gate_free, 2)
            split_exactly(dve, link, W1_part[:, 0, :], W1_part[:, 1, :], W1_high[:, :], W1[:, :])
            dve.sem_inc(ready, 1)
            dve.wait_ge(lists_up, 32)
            regs = [dve.alloc_register(f"dve_block{u}") for u in range(U)]

            def halve(q, p, s, j):
                if s == 0:
                    dve.wait_ge(tables_up[p], j * (16 * (U + 1)) + 16 * (U + 1))
                if not (isinstance(q, int) and q < 2):
                    dve.wait_ge(turned, q - 1)
                if not (isinstance(q, int) and q == 0):
                    dve.wait_ge(halves_up, q)
                own = rbf[:, p, s * Q:s * Q + Q, :]
                high, low = (halves[:, s % 2, :, n, :] for n in range(2))
                split_exactly(dve, LoopLinked(dve, halved, q, 1), high, low, leading[:, :, :], own, halves_up)

            def turn(q):
                dve.wait_ge(turned, q + 1)
                if not (isinstance(q, int) and q == 0):
                    dve.wait_ge(hidden_in, 2 * q)
                dve.tensor_copy(rbfT[:, :], psX[:, :]).then_inc(rbfT_up, 1)

            def weigh(q, c, p, s, j):
                if s == 0 and c == 0:
                    dve.wait_ge(gathered[p], j * (16 * U) + 16 * U)
                u = s * Q + 2 * c
                dve.wait_ge(gate_up, 2 * q + c + 3)
                dve.scalar_tensor_tensor(G[:, p, u:u + 2, :], gate[:, c, :, :], 1.0, G[:, p, u:u + 2, :], ALU.add, ALU.mult)\
                    .then_inc(weighed, 1)

            def freed(q, c):
                dve.wait_ge(weighed, 2 * q + c + 1)
                dve.sem_inc(gate_free, 1)

            def one_hot(p, s):
                dve.tensor_tensor(hot[:, p, s * Q:s * Q + Q, :], K.col[:, :].unsqueeze(1).broadcast_to([P, Q, P]),
                                  local_c[:, p, s * Q:s * Q + Q].unsqueeze(2).broadcast_to([P, Q, P]), ALU.is_equal).then_inc(hot_up, 1)

            def add(q, c, s, regs):
                for v in range(2 * c, 2 * c + 2):
                    t = dve.snap(regs[s * Q + v], min_val=0, max_val=S.NT - 1)
                    dve.wait_ge(summed, Q * q + (2 * c + 2))
                    dve.wait_ge(added, Q * q + (v + CREDIT))
                    a = acc[:, bass.ds(t * F, F)]
                    dve.tensor_tensor(a, a, psP[:, c, v % 2, :], ALU.add).then_inc(added, 1)

            halve(0, 0, 0, 0)
            halve(1, 0, 1, 0)
            turn(0)
            halve(2, 0, 2, 0)
            turn(1)
            for s in range(U // Q):
                one_hot(0, s)
            for c in range(2):
                weigh(0, c, 0, 0, 0)
                freed(0, c)
            with dve.Fori(0, NI // 2) as j:
                for p in range(2):
                    i = j * 2 + p
                    dve.load(regs, tile_r[0:1, bass.ds(i * U, U)])
                    for s in range(U // Q):
                        q = j * (2 * U // Q) + (p * (U // Q) + s)

                        def at(ahead):
                            k = p * (U // Q) + s + ahead
                            return k // (U // Q) % 2, k % (U // Q), j + 1 if k >= 2 * (U // Q) else j

                        turn(q + 2)
                        weigh(q + 1, 0, *at(1))
                        if s == 0:
                            dve.wait_ge(tables_up[1 - p], (j + p) * (16 * (U + 1)) + 16 * (U + 1))
                        one_hot(1 - p, s)
                        freed(q + 1, 0)
                        add(q, 0, s, regs)
                        halve(q + 3, *at(3))
                        weigh(q + 1, 1, *at(1))
                        freed(q + 1, 1)
                        add(q, 1, s, regs)
            dve.wait_ge(added, NI * U + CREDIT)


def finish_nodes(nc, S, K, M, U1_d, c1_d, U2_d, c2_d, acc, out):
    nodes = Nodes(S)
    with ExitStack() as ctx:
        sb, ps, sem = allocators(nc, ctx, "finish", M.context)
        hin = sb("hin", [P, 2, G4, F])
        xh = sb("xh", [P, 2, G4, F])
        agg = sb("agg", [P, 2, F])
        both = sb("both", [P, 2, 4, P])
        act1 = sb("act1", [P, 2, 2, P])
        res = sb("res", [P, 2, G4, F])
        U1 = sb("U1", [P, 4, F])
        U2 = sb("U2", [P, 2, F])
        c1 = sb("c1", [P, 2])
        c2 = sb("c2", [3, F])
        c2_3 = sb("c2_3", [3, F], BF16)
        part = sb("part", [3, F], BF16)
        rest = sb("rest", [3, 2, F])
        psT = ps("psT", [P, 2, 512])
        psH = ps("psH", [P, 2, 512])
        psO = ps("psO", [P, 2, 512])
        (weights_up, ready, agg_up, turned, both_up, hidden_in, hidden_up, products, res_up, out_free, in_free, linked) = (
            sem(n) for n in ("weights_up", "ready", "agg_up", "turned", "both_up", "hidden_in", "hidden_up", "products", "res_up",
                             "out_free", "in_free", "dve_linked"))
        loaded = [sem("loaded0"), sem("loaded1")]
        stored = [sem.lasting("stored0"), sem.lasting("stored1")]
        block = phase_block(nc, ctx, sem)

        @block.sync
        def _(sp):
            sp.dma_start(U1[:, :, :], U1_d.rearrange("(k p) f -> p k f", p=P)).then_inc(weights_up, 16)
            sp.dma_start(U2[:, :, :], U2_d.rearrange("(k p) f -> p k f", p=P)).then_inc(weights_up, 16)
            sp.dma_start(c1[:, :].unsqueeze(2), c1_d.rearrange("(k p o) -> p k o", p=P, o=1), allow_slow_non_contiguous=True)\
                .then_inc(weights_up, 16)
            sp.dma_start(c2[:, :], c2_d.rearrange("(o f) -> o f", o=1).broadcast_to([3, F])).then_inc(weights_up, 16)

            def group(tile, g, p, n, rows):
                sp.wait_ge(in_free, g + 1)
                sp.dma_start(hin[:, p, 0:n, :], tiles_of(M.h3, tile, n)).then_inc(loaded[p], 16)
                sp.dma_start(xh[:, p, 0:n, :], tiles_of(M.xh, tile, n)).then_inc(loaded[p], 16)
            nodes.run(sp, group)

        @block.gpsimd
        def _(pool):
            def group(tile, g, p, n, rows):
                pool.wait_ge(res_up, tile + n + 2)
                pool.sem_inc(in_free, 1)
                pool.dma_start(tiles_of(out, tile, n - 1), res[:, p, 0:n - 1, :]).then_inc(stored[p], 16)
                pool.dma_start(out[bass.ds((tile + n - 1) * P, rows), :], res[0:rows, p, n - 1, :]).then_inc(stored[p], 16)
                pool.wait_ge(stored[p], half(g, p) * 32 + 32)
                pool.sem_inc(out_free, 1)
            nodes.run(pool, group)

        @block.tensor
        def _(pe):
            pe.wait_ge(ready, 1)

            def turn(T, g, p, k):
                if k == 0:
                    pe.wait_ge(loaded[p], half(g, p) * 32 + 32)
                pe.wait_ge(agg_up, T + 1)
                if not (isinstance(T, int) and T < 2):
                    pe.wait_ge(both_up, T - 1)
                for c in range(4):
                    rows = hin[:, p, k, c * P:c * P + P] if c < 2 else agg[:, k % 2, c % 2 * P:c % 2 * P + P]
                    mm = pe.transpose(psT[:, k % 2, c * P:c * P + P], rows, K.ident[:, :])
                mm.then_inc(turned, 1)

            def first(T, k):
                pe.wait_ge(both_up, T + 1)
                pe.wait_ge(hidden_up, T + 1)
                for m in range(2):
                    for c in range(4):
                        mm = pe.matmul(psH[:, k % 2, m * P:m * P + P], U1[:, c, m * P:m * P + P], both[:, k % 2, c, :],
                                       start=(c == 0), stop=(c == 3))
                mm.then_inc(hidden_in, 1)

            def second(T, k):
                pe.wait_ge(hidden_up, T + 3)
                pe.wait_ge(res_up, T + 1)
                pe.matmul(psO[:, k % 2, 0:F], K.ones3[:, :], c2_3[:, :], start=True, stop=False)
                for m in range(2):
                    mm = pe.matmul(psO[:, k % 2, 0:F], act1[:, k % 2, m, :], U2[:, m, :], start=False, stop=(m == 1))
                mm.then_inc(products, 1)

            turn(0, 0, 0, 0)
            turn(1, 0, 0, 1)
            first(0, 0)

            def group(tile, g, p, n, rows):
                for k in range(n):
                    if k + 2 < n:
                        turn(tile + (k + 2), g, p, k + 2)
                    elif n == G4:
                        turn(tile + (k + 2), g + 1, 1 - p, k + 2 - n)
                    if k + 1 < n or n == G4:
                        first(tile + (k + 1), k + 1)
                    second(tile + k, k)
            nodes.run(pe, group)

        @block.scalar
        def _(act):
            act.sem_inc(hidden_up, 2)
            act.wait_ge(weights_up, 64)

            def halve(T, k):
                if not (isinstance(T, int) and T < 2):
                    act.wait_ge(turned, T - 1)
                act.activation(agg[:, k % 2, :], acc[:, bass.ds(T * F, F)], ACT.Copy, scale=0.5).then_inc(agg_up, 1)

            halve(0, 0)
            halve(1, 1)

            def group(tile, g, p, n, rows):
                for k in range(n):
                    T = tile + k
                    if k + 2 < n or n == G4:
                        halve(tile + (k + 2), k)
                    act.wait_ge(hidden_in, T + 1)
                    for m in range(2):
                        ins = act.activation(act1[:, k % 2, m, :], psH[:, k % 2, m * P:m * P + P], ACT.Silu, bias=c1[:, m:m + 1])
                    ins.then_inc(hidden_up, 1)
            nodes.run(act, group)

        @block.vector
        def _(dve):
            link = Linked(dve, linked)
            dve.wait_ge(weights_up, 64)
            split_bias(dve, link, K, c2_3, c2, part, rest)
            dve.sem_inc(ready, 1)
            dve.sem_inc(res_up, 2)
            dve.sem_inc(in_free, 2)
            dve.sem_inc(out_free, 2)

            def copy(T, k):
                dve.wait_ge(turned, T + 1)
                if not (isinstance(T, int) and T < 2):
                    dve.wait_ge(hidden_in, T - 1)
                dve.tensor_copy(both[:, k % 2, :, :], psT[:, k % 2, :].rearrange("p (c e) -> p c e", c=4)).then_inc(both_up, 1)

            copy(0, 0)
            copy(1, 1)

            def group(tile, g, p, n, rows):
                dve.wait_ge(out_free, g + 1)
                dve.wait_ge(loaded[p], half(g, p) * 32 + 32)
                for k in range(n):
                    if k + 2 < n or n == G4:
                        copy(tile + (k + 2), k)
                    dve.wait_ge(products, tile + k + 1)
                    dve.tensor_tensor(res[:, p, k, :], psO[:, k % 2, 0:F], xh[:, p, k, :], ALU.add).then_inc(res_up, 1)
            nodes.run(dve, group)


class Memory:

    def __init__(self, nc, S):
        def dram(name, shape, dt=F32):
            return nc.dram_tensor(name, shape, dt).ap()

        V = S.V
        self.dst_all = dram("dst_e", (S.EB * P + 1,), I32)
        self.dst_e = self.dst_all[0:S.EB * P]
        self.src_e = dram("src_e", (S.EB * P,), I32)
        self.dst_v = dram("dst_v", (1 + V * P,))
        self.tile = dram("tile", (V,), I32)
        self.block = dram("block", (V,), I32)
        self.local_row = dram("local_row", (V * P,), BF16)
        self.local_col = dram("local_col", (P, V))
        self.src_col = dram("src_col", (P, V), I32)
        self.apart = dram("apart", (V * H, P))
        self.whole = dram("whole", (V,))
        self.alike = dram("alike", (V,))
        self.goes_on = dram("goes_on", (V,))
        self.table = dram("table", (S.NT * P, ROW))
        self.h2 = dram("h2", (S.NT * P, F))
        self.h3 = dram("h3", (S.NT * P, F))
        self.xh = dram("xh", (S.NT * P, F))
        self.attr = dram("attr", (S.EB * P, NR))
        self.record = [dram(f"record{d}", (S.EB * P, 4), I32) for d in range(2)]


class Patterns:
    pass


def build(nc, x, src, dst, attr, W1, al1, ar1, W2, al2, ar2, V1, b1, V2, b2, U1, c1, U2, c2, out):
    S = Sizes(x.shape[0], src.shape[0])
    M = Memory(nc, S)
    with ExitStack() as ctx:
        M.context = ctx
        sb, _, sem = allocators(nc, ctx, "all")
        K = Patterns()
        K.col = sb("col", [P, P])
        K.row = sb("rown", [P, 1])
        K.ident = sb("ident", [P, P])
        K.hu = sb("hu", [R, 2])
        K.head_of = sb("head_of", [R, H])
        K.visit_of = sb("visit_of", [R, U])
        K.rows_of = sb("rows_of", [H, R])
        K.ones = sb("ones", [1, P])
        K.ones3 = sb("ones3", [3, P], BF16)
        K.col3 = sb("col3", [3, 3])
        K.eps = sb("eps", [P, 1])
        K.every = sb("every", [P, P])
        K.ident_r = sb("ident_r", [P, P], F32R)
        K.unsorted = sb("unsorted", [1, 1], I32)
        M.zeros = sb("zeros", [S.EB * P - S.E, NR])
        M.attr_up = sem("attributes_up")
        constants(nc, K)
        pad_edges(nc, S, K, M, src, dst)
        sort_edges(nc, S, K, M)
        visit_tables(nc, S, K, M)
        er3 = sb("er3", [P, S.NT, 3, H], BF16)
        acc = sb("acc", [P, S.NT * ROW])
        Waug = sb("Waug", [P, 2, ROW + H])
        attention_weights(nc, K, M, W1, al1, ar1, Waug, 1)
        project_nodes(nc, S, K, M, True, x, Waug, er3, acc)
        attend(nc, S, K, M, er3, acc, 1, attr)
        sort_attributes(nc, S, K, M, attr)
        attention_weights(nc, K, M, W2, al2, ar2, Waug, 2)
        project_nodes(nc, S, K, M, False, x, Waug, er3, acc)
        attend(nc, S, K, M, er3, acc, 2)
        renew_nodes(nc, S, K, M, x, acc)
        pass_messages(nc, S, K, M, M.attr, V1, b1, V2, b2, acc)
        finish_nodes(nc, S, K, M, U1, c1, U2, c2, acc, out)


_INS = ["x", "src", "dst", "edge_attr_64", "L0_gnn_W1", "L0_gnn_al1", "L0_gnn_ar1", "L0_gnn_W2", "L0_gnn_al2", "L0_gnn_ar2",
        "L1_gnn_W1", "L1_gnn_b1", "L1_gnn_W2", "L1_gnn_b2", "L1_gnn_U1", "L1_gnn_c1", "L1_gnn_U2", "L1_gnn_c2"]


def kernel(**inputs):
    import numpy as _np
    import concourse.bacc as _bacc
    from concourse import mybir as _mybir
    from concourse.bass_utils import run_bass_kernel_spmd as _run

    nc = _bacc.Bacc("TRN2", target_bir_lowering=False, num_devices=1)
    arrays, args = {}, []
    for name in _INS:
        a = _np.ascontiguousarray(inputs[name])
        arrays[f"in_{name}_dram"] = a
        args.append(nc.dram_tensor(f"in_{name}_dram", a.shape, _mybir.dt.from_np(a.dtype), kind="ExternalInput").ap())
    out = nc.dram_tensor("out_0_dram", tuple(inputs["x"].shape), _mybir.dt.float32, kind="ExternalOutput").ap()
    build(nc, *args, out)
    r = _run(nc, [arrays], core_ids=[0])
    return r.results[0]["out_0_dram"]
```
